# Optimizing a Trainium2 kernel written in Bass

```python
import numpy as np
import jax
import jax.numpy as jnp

def _softmax(x, axis=-1):
    return jax.nn.softmax(x, axis=axis)

def _gelu(x):
    return jax.nn.gelu(x, approximate=True)

def _silu(x):
    return jax.nn.silu(x)

def _sigmoid(x):
    return jax.nn.sigmoid(x)

def _layernorm(x, axis=-1, eps=1e-05):
    m = jnp.mean(x, axis=axis, keepdims=True)
    v = jnp.var(x, axis=axis, keepdims=True)
    return (x - m) / jnp.sqrt(v + eps)

def _scatter_add(tgt, idx, src, axis=0):
    return tgt.at[idx].add(src)

def _segment_sum(src, seg, n):
    return jax.ops.segment_sum(src, seg, n)
kernel_name = 'mk_recurrent_d4_jaxref_r8_c09f49'

def setup_inputs(seed: int=0):
    np.random.seed(seed)
    _w = jnp.asarray

    def _L0_attn_setup():
        import jax, jax.numpy as jnp
        import numpy as np
        DT_RANK = 64
        N_STATES = 16

        def selective_scan(u, delta, A, B, C, D):
            dA = jnp.einsum('bld,dn->bldn', delta, A)
            dB_u = jnp.einsum('bld,bld,bln->bldn', delta, u, B)
            dA_shift = jnp.concatenate([dA[:, 1:], jnp.zeros_like(dA[:, :1])], axis=1)
            dA_cumsum = jnp.exp(jnp.flip(jnp.cumsum(jnp.flip(dA_shift, axis=1), axis=1), axis=1))
            xs = jnp.cumsum(dB_u * dA_cumsum, axis=1) / (dA_cumsum + 1e-12)
            y = jnp.einsum('bldn,bln->bld', xs, C)
            return y + u * D
        key = jax.random.key(seed)
        ks = jax.random.split(key, 6)
        b, l, d = (2, 128, 128)
        dt_rank, n = (DT_RANK, N_STATES)
        x = jax.random.normal(ks[0], (b, l, d), dtype=jnp.float32)
        W_x = jax.random.normal(ks[1], (d, dt_rank + 2 * n), dtype=jnp.float32) * (1.0 / np.sqrt(d))
        W_dt = jax.random.normal(ks[2], (dt_rank, d), dtype=jnp.float32) * (1.0 / np.sqrt(dt_rank))
        b_dt = jnp.zeros((d,), dtype=jnp.float32)
        A_log = jnp.log(jnp.tile(jnp.arange(1, n + 1, dtype=jnp.float32)[None, :], (d, 1)))
        D = jnp.ones((d,), dtype=jnp.float32)
        W_out = jax.random.normal(ks[3], (d, d), dtype=jnp.float32) * (1.0 / np.sqrt(d))
        b_out = jnp.zeros((d,), dtype=jnp.float32)
        return {'x': x, 'W_x': W_x, 'W_dt': W_dt, 'b_dt': b_dt, 'A_log': A_log, 'D': D, 'W_out': W_out, 'b_out': b_out}
    _L0_attn_in = _L0_attn_setup()

    def _L0_ffn_setup():
        import jax, jax.numpy as jnp
        import numpy as np
        D_MODEL = 128
        D_HIDDEN = 512
        NUM_EXPERT = 8
        TOP_K = 2
        B, N = (1, 1024)

        def _expert_mlp(x, W1, b1, W2, b2, W3, b3):
            h = jax.nn.gelu(jnp.einsum('bnd,dh->bnh', x, W1) + b1, approximate=False)
            h = jax.nn.gelu(jnp.einsum('bnh,hk->bnk', h, W2) + b2, approximate=False)
            return jnp.einsum('bnh,hd->bnd', h, W3) + b3
        key = jax.random.key(seed)
        ks = jax.random.split(key, 8)
        s1 = 1.0 / np.sqrt(D_MODEL)
        s2 = 1.0 / np.sqrt(D_HIDDEN)
        return {'x': jax.random.normal(ks[0], (B, N, D_MODEL), jnp.float32), 'expert_tokens': jax.random.normal(ks[1], (NUM_EXPERT, D_MODEL), jnp.float32), 'W1': jax.random.normal(ks[2], (NUM_EXPERT, D_MODEL, D_HIDDEN), jnp.float32) * s1, 'b1': jnp.zeros((NUM_EXPERT, D_HIDDEN), jnp.float32), 'W2': jax.random.normal(ks[3], (NUM_EXPERT, D_HIDDEN, D_HIDDEN), jnp.float32) * s2, 'b2': jnp.zeros((NUM_EXPERT, D_HIDDEN), jnp.float32), 'W3': jax.random.normal(ks[4], (NUM_EXPERT, D_HIDDEN, D_MODEL), jnp.float32) * s2, 'b3': jnp.zeros((NUM_EXPERT, D_MODEL), jnp.float32)}
    _L0_ffn_in = _L0_ffn_setup()

    def _L1_attn_setup():
        import jax, jax.numpy as jnp
        import numpy as np
        B, S, D, H = (4, 256, 128, 16)
        DH = D // H
        key = jax.random.key(seed)
        ks = jax.random.split(key, 5)
        std = 1.0 / np.sqrt(D)
        return {'x': jax.random.normal(ks[0], (B, S, D), dtype=jnp.float32), 'mask': jnp.ones((S, S), dtype=bool), 'Wq': jax.random.normal(ks[1], (D, D), dtype=jnp.float32) * std, 'Wk': jax.random.normal(ks[2], (D, D), dtype=jnp.float32) * std, 'Wv': jax.random.normal(ks[3], (D, D), dtype=jnp.float32) * std, 'Wout': jax.random.normal(ks[4], (D, D), dtype=jnp.float32) * std}
    _L1_attn_in = _L1_attn_setup()

    def _L1_ffn_setup():
        import jax, jax.numpy as jnp
        import numpy as np
        E, K, D, H = (8, 2, 128, 256)
        B, S = (1, 128)

        def _grouped_swiglu(x_sorted, counts, w1, w2, w3):
            if hasattr(jax.lax, 'ragged_dot'):
                gs = counts.astype(jnp.int32)
                h = jax.nn.silu(jax.lax.ragged_dot(x_sorted, w1, gs)) * jax.lax.ragged_dot(x_sorted, w3, gs)
                return jax.lax.ragged_dot(h, w2, gs)
            pos = jnp.arange(x_sorted.shape[0])
            eid = jnp.searchsorted(jnp.cumsum(counts), pos, side='right')
            out = jnp.zeros((x_sorted.shape[0], w2.shape[-1]), x_sorted.dtype)
            for e in range(w1.shape[0]):
                xm = jnp.where((eid == e)[:, None], x_sorted, 0.0)
                he = jax.nn.silu(xm @ w1[e]) * (xm @ w3[e])
                out = out + he @ w2[e]
            return out
        key = jax.random.key(seed)
        k0, k1, k2, k3, k4 = jax.random.split(key, 5)
        sD = 1.0 / np.sqrt(D)
        sH = 1.0 / np.sqrt(H)
        return {'hidden_states': jax.random.normal(k0, (B, S, D), jnp.float32), 'gate_w': jax.random.normal(k1, (E, D), jnp.float32) * sD, 'w1': jax.random.normal(k2, (E, D, H), jnp.float32) * sD, 'w2': jax.random.normal(k3, (E, H, D), jnp.float32) * sH, 'w3': jax.random.normal(k4, (E, D, H), jnp.float32) * sD}
    _L1_ffn_in = _L1_ffn_setup()

    def _L2_attn_setup():
        import jax, jax.numpy as jnp
        import numpy as np
        HIDDEN = 128
        B, S = (8, 256)
        key = jax.random.key(seed)
        k1, k2, k3, k4 = jax.random.split(key, 4)
        gain = 1.2
        bound = gain * np.sqrt(6.0 / (HIDDEN + HIDDEN))
        return {'hidden_states': jax.random.normal(k1, (B, S, HIDDEN), dtype=jnp.float32), 'Wq': jax.random.uniform(k2, (HIDDEN, HIDDEN), jnp.float32, -bound, bound), 'bq': jnp.zeros((HIDDEN,), jnp.float32), 'Wv': jax.random.uniform(k3, (HIDDEN, HIDDEN), jnp.float32, -bound, bound), 'bv': jnp.zeros((HIDDEN,), jnp.float32), 'anomaly_matrix': jax.random.uniform(k4, (HIDDEN, HIDDEN), jnp.float32, -2.0, 2.0)}
    _L2_attn_in = _L2_attn_setup()

    def _L2_ffn_setup():
        import jax, jax.numpy as jnp
        import numpy as np
        DIM = 128
        EXPERT_DIM = 64
        N_EXPERTS = 16
        TOPK = 2
        SHARED_HIDDEN = EXPERT_DIM * TOPK
        B, T = (4, 128)

        def _moe_forward(x, router_w, router_bias, up_proj, gate_proj, down_proj, sh_gate, sh_up, sh_down):
            Bb, Tt, D = x.shape
            flat = x.reshape(Bb * Tt, D)
            N = flat.shape[0]
            logits = flat @ router_w.T
            topk_scores, topk_idx = jax.lax.top_k(logits + router_bias, TOPK)
            topk_scores = jax.nn.softmax(topk_scores, axis=-1)
            combine = jnp.zeros((N, N_EXPERTS), flat.dtype)
            combine = combine.at[jnp.arange(N)[:, None], topk_idx].add(topk_scores)
            up_all = jnp.einsum('nd,kde->nke', flat, up_proj)
            gate_all = jnp.einsum('nd,kde->nke', flat, gate_proj)
            hidden = jax.nn.silu(gate_all) * up_all
            down_all = jnp.einsum('nke,ked->nkd', hidden, down_proj)
            out = jnp.einsum('nk,nkd->nd', combine, down_all)
            sh_hidden = jax.nn.silu(flat @ sh_gate.T) * (flat @ sh_up.T)
            out = out + sh_hidden @ sh_down.T
            return out.reshape(Bb, Tt, D)
        key = jax.random.key(seed)
        ks = jax.random.split(key, 9)
        std = 0.02
        return {'x': jax.random.normal(ks[0], (B, T, DIM), jnp.float32), 'router_w': jax.random.normal(ks[1], (N_EXPERTS, DIM), jnp.float32) * std, 'router_bias': jnp.zeros((N_EXPERTS,), jnp.float32), 'up_proj': jax.random.normal(ks[2], (N_EXPERTS, DIM, EXPERT_DIM), jnp.float32) * std, 'gate_proj': jax.random.normal(ks[3], (N_EXPERTS, DIM, EXPERT_DIM), jnp.float32) * std, 'down_proj': jax.random.normal(ks[4], (N_EXPERTS, EXPERT_DIM, DIM), jnp.float32) * std, 'sh_gate': jax.random.normal(ks[5], (SHARED_HIDDEN, DIM), jnp.float32) * std, 'sh_up': jax.random.normal(ks[6], (SHARED_HIDDEN, DIM), jnp.float32) * std, 'sh_down': jax.random.normal(ks[7], (DIM, SHARED_HIDDEN), jnp.float32) * std}
    _L2_ffn_in = _L2_ffn_setup()

    def _L3_attn_setup():
        import jax, jax.numpy as jnp
        import numpy as np
        B, T, C = (4, 128, 128)
        HEAD_SIZE = 64
        H = C // HEAD_SIZE
        N_LAYER, LAYER_ID = (24, 12)
        D_MIX_LORA, D_DECAY_LORA = (32, 64)
        HEAD_SIZE_DIVISOR = 8
        LN_EPS = 1e-05 * HEAD_SIZE_DIVISOR ** 2

        def _wkv6(r, k, v, w, u):

            def step(S, inp):
                r_t, k_t, v_t, w_t = inp
                y = jnp.einsum('bhj,bhji->bhi', r_t, S) + jnp.sum(r_t * u * k_t, axis=-1, keepdims=True) * v_t
                decay = jnp.exp(-jnp.exp(w_t))
                S = decay[..., None] * S + k_t[..., None] * v_t[..., None, :]
                return (S, y)
            to_t = lambda a: jnp.transpose(a, (1, 0, 2, 3))
            S0 = jnp.zeros(r.shape[:1] + (r.shape[2], r.shape[3], r.shape[3]), r.dtype)
            _, ys = jax.lax.scan(step, S0, (to_t(r), to_t(k), to_t(v), to_t(w)))
            return jnp.transpose(ys, (1, 0, 2, 3))
        key = jax.random.key(seed)
        ks = jax.random.split(key, 16)
        x = jax.random.normal(ks[0], (B, T, C), jnp.float32)
        r01 = LAYER_ID / (N_LAYER - 1)
        r10 = 1.0 - LAYER_ID / N_LAYER
        ddd = np.arange(C, dtype=np.float64) / C
        time_maa_x = jnp.asarray((1.0 - ddd ** r10).astype(np.float32))
        time_maa_w = jnp.asarray((1.0 - ddd ** r10).astype(np.float32))
        time_maa_k = jnp.asarray((1.0 - ddd ** r10).astype(np.float32))
        time_maa_v = jnp.asarray((1.0 - (ddd ** r10 + 0.3 * r01)).astype(np.float32))
        time_maa_r = jnp.asarray((1.0 - ddd ** (0.5 * r10)).astype(np.float32))
        time_maa_g = jnp.asarray((1.0 - ddd ** (0.5 * r10)).astype(np.float32))
        n = np.arange(C, dtype=np.float64)
        time_decay = jnp.asarray((-6.0 + 5.0 * (n / (C - 1)) ** (0.7 + 1.3 * r01)).astype(np.float32))
        zigzag = ((n + 1) % 3 - 1) * 0.1
        time_faaaa = jnp.asarray((r01 * (1.0 - n / (C - 1)) + zigzag).astype(np.float32)).reshape(H, HEAD_SIZE)
        u = lambda k, shp: jax.random.uniform(k, shp, jnp.float32, -0.01, 0.01)
        time_maa_w1 = u(ks[1], (C, D_MIX_LORA * 5))
        time_maa_w2 = u(ks[2], (5, D_MIX_LORA, C))
        time_decay_w1 = u(ks[3], (C, D_DECAY_LORA))
        time_decay_w2 = u(ks[4], (D_DECAY_LORA, C))
        s = 1.0 / np.sqrt(C)
        Wr = jax.random.normal(ks[5], (C, C), jnp.float32) * s
        Wk = jax.random.normal(ks[6], (C, C), jnp.float32) * s
        Wv = jax.random.normal(ks[7], (C, C), jnp.float32) * s
        Wg = jax.random.normal(ks[8], (C, C), jnp.float32) * s
        Wo = jax.random.normal(ks[9], (C, C), jnp.float32) * s
        ln_w = jnp.ones((C,), jnp.float32)
        ln_b = jnp.zeros((C,), jnp.float32)
        return dict(x=x, time_maa_x=time_maa_x, time_maa_w=time_maa_w, time_maa_k=time_maa_k, time_maa_v=time_maa_v, time_maa_r=time_maa_r, time_maa_g=time_maa_g, time_maa_w1=time_maa_w1, time_maa_w2=time_maa_w2, time_decay=time_decay, time_decay_w1=time_decay_w1, time_decay_w2=time_decay_w2, time_faaaa=time_faaaa, Wr=Wr, Wk=Wk, Wv=Wv, Wg=Wg, Wo=Wo, ln_w=ln_w, ln_b=ln_b)
    _L3_attn_in = _L3_attn_setup()

    def _L3_ffn_setup():
        import jax, jax.numpy as jnp
        import numpy as np
        B, S, H, NH, E, F = (4, 128, 128, 16, 8, 512)
        D = H // NH
        EPS = 1e-05

        def _layernorm(x, g, b):
            mu = jnp.mean(x, axis=-1, keepdims=True)
            var = jnp.var(x, axis=-1, keepdims=True)
            return (x - mu) * jax.lax.rsqrt(var + EPS) * g + b
        key = jax.random.key(seed)
        ks = jax.random.split(key, 16)
        s = 0.02
        return {'x': jax.random.normal(ks[0], (B, S, H), jnp.float32), 'ln1_g': jnp.ones((H,), jnp.float32), 'ln1_b': jnp.zeros((H,), jnp.float32), 'ln2_g': jnp.ones((H,), jnp.float32), 'ln2_b': jnp.zeros((H,), jnp.float32), 'wq': jax.random.normal(ks[1], (H, H), jnp.float32) * s, 'bq': jnp.zeros((H,), jnp.float32), 'wk': jax.random.normal(ks[2], (H, H), jnp.float32) * s, 'bk': jnp.zeros((H,), jnp.float32), 'wv': jax.random.normal(ks[3], (H, H), jnp.float32) * s, 'bv': jnp.zeros((H,), jnp.float32), 'wo': jax.random.normal(ks[4], (H, H), jnp.float32) * s, 'bo': jnp.zeros((H,), jnp.float32), 'gate_w': jax.random.normal(ks[5], (H, E), jnp.float32) * s, 'gate_b': jnp.zeros((E,), jnp.float32), 'w1': jax.random.normal(ks[6], (E, H, F), jnp.float32) * s, 'b1': jnp.zeros((E, F), jnp.float32), 'w2': jax.random.normal(ks[7], (E, F, H), jnp.float32) * s, 'b2': jnp.zeros((E, H), jnp.float32)}
    _L3_ffn_in = _L3_ffn_setup()
    _d = {'L0_attn_x': _L0_attn_in['x'], 'L0_attn_W_x': _L0_attn_in['W_x'], 'L0_attn_W_dt': _L0_attn_in['W_dt'], 'L0_attn_b_dt': _L0_attn_in['b_dt'], 'L0_attn_A_log': _L0_attn_in['A_log'], 'L0_attn_D': _L0_attn_in['D'], 'L0_attn_W_out': _L0_attn_in['W_out'], 'L0_attn_b_out': _L0_attn_in['b_out'], 'L0_ffn_expert_tokens': _L0_ffn_in['expert_tokens'], 'L0_ffn_W1': _L0_ffn_in['W1'], 'L0_ffn_b1': _L0_ffn_in['b1'], 'L0_ffn_W2': _L0_ffn_in['W2'], 'L0_ffn_b2': _L0_ffn_in['b2'], 'L0_ffn_W3': _L0_ffn_in['W3'], 'L0_ffn_b3': _L0_ffn_in['b3'], 'L1_attn_mask': _L1_attn_in['mask'], 'L1_attn_Wq': _L1_attn_in['Wq'], 'L1_attn_Wk': _L1_attn_in['Wk'], 'L1_attn_Wv': _L1_attn_in['Wv'], 'L1_attn_Wout': _L1_attn_in['Wout'], 'L1_ffn_gate_w': _L1_ffn_in['gate_w'], 'L1_ffn_w1': _L1_ffn_in['w1'], 'L1_ffn_w2': _L1_ffn_in['w2'], 'L1_ffn_w3': _L1_ffn_in['w3'], 'L2_attn_Wq': _L2_attn_in['Wq'], 'L2_attn_bq': _L2_attn_in['bq'], 'L2_attn_Wv': _L2_attn_in['Wv'], 'L2_attn_bv': _L2_attn_in['bv'], 'L2_attn_anomaly_matrix': _L2_attn_in['anomaly_matrix'], 'L2_ffn_router_w': _L2_ffn_in['router_w'], 'L2_ffn_router_bias': _L2_ffn_in['router_bias'], 'L2_ffn_up_proj': _L2_ffn_in['up_proj'], 'L2_ffn_gate_proj': _L2_ffn_in['gate_proj'], 'L2_ffn_down_proj': _L2_ffn_in['down_proj'], 'L2_ffn_sh_gate': _L2_ffn_in['sh_gate'], 'L2_ffn_sh_up': _L2_ffn_in['sh_up'], 'L2_ffn_sh_down': _L2_ffn_in['sh_down'], 'L3_attn_time_maa_x': _L3_attn_in['time_maa_x'], 'L3_attn_time_maa_w': _L3_attn_in['time_maa_w'], 'L3_attn_time_maa_k': _L3_attn_in['time_maa_k'], 'L3_attn_time_maa_v': _L3_attn_in['time_maa_v'], 'L3_attn_time_maa_r': _L3_attn_in['time_maa_r'], 'L3_attn_time_maa_g': _L3_attn_in['time_maa_g'], 'L3_attn_time_maa_w1': _L3_attn_in['time_maa_w1'], 'L3_attn_time_maa_w2': _L3_attn_in['time_maa_w2'], 'L3_attn_time_decay': _L3_attn_in['time_decay'], 'L3_attn_time_decay_w1': _L3_attn_in['time_decay_w1'], 'L3_attn_time_decay_w2': _L3_attn_in['time_decay_w2'], 'L3_attn_time_faaaa': _L3_attn_in['time_faaaa'], 'L3_attn_Wr': _L3_attn_in['Wr'], 'L3_attn_Wk': _L3_attn_in['Wk'], 'L3_attn_Wv': _L3_attn_in['Wv'], 'L3_attn_Wg': _L3_attn_in['Wg'], 'L3_attn_Wo': _L3_attn_in['Wo'], 'L3_attn_ln_w': _L3_attn_in['ln_w'], 'L3_attn_ln_b': _L3_attn_in['ln_b'], 'L3_ffn_ln1_g': _L3_ffn_in['ln1_g'], 'L3_ffn_ln1_b': _L3_ffn_in['ln1_b'], 'L3_ffn_ln2_g': _L3_ffn_in['ln2_g'], 'L3_ffn_ln2_b': _L3_ffn_in['ln2_b'], 'L3_ffn_wq': _L3_ffn_in['wq'], 'L3_ffn_bq': _L3_ffn_in['bq'], 'L3_ffn_wk': _L3_ffn_in['wk'], 'L3_ffn_bk': _L3_ffn_in['bk'], 'L3_ffn_wv': _L3_ffn_in['wv'], 'L3_ffn_bv': _L3_ffn_in['bv'], 'L3_ffn_wo': _L3_ffn_in['wo'], 'L3_ffn_bo': _L3_ffn_in['bo'], 'L3_ffn_gate_w': _L3_ffn_in['gate_w'], 'L3_ffn_gate_b': _L3_ffn_in['gate_b'], 'L3_ffn_w1': _L3_ffn_in['w1'], 'L3_ffn_b1': _L3_ffn_in['b1'], 'L3_ffn_w2': _L3_ffn_in['w2'], 'L3_ffn_b2': _L3_ffn_in['b2']}
    _x0 = _d['L0_attn_x']
    _d['L0_attn_x'] = jax.random.normal(jax.random.fold_in(jax.random.key(seed), 1), (2, 1024, 128), dtype=_x0.dtype)
    del _x0
    return _d

def reference(L0_attn_x, L0_attn_W_x, L0_attn_W_dt, L0_attn_b_dt, L0_attn_A_log, L0_attn_D, L0_attn_W_out, L0_attn_b_out, L0_ffn_expert_tokens, L0_ffn_W1, L0_ffn_b1, L0_ffn_W2, L0_ffn_b2, L0_ffn_W3, L0_ffn_b3, L1_attn_mask, L1_attn_Wq, L1_attn_Wk, L1_attn_Wv, L1_attn_Wout, L1_ffn_gate_w, L1_ffn_w1, L1_ffn_w2, L1_ffn_w3, L2_attn_Wq, L2_attn_bq, L2_attn_Wv, L2_attn_bv, L2_attn_anomaly_matrix, L2_ffn_router_w, L2_ffn_router_bias, L2_ffn_up_proj, L2_ffn_gate_proj, L2_ffn_down_proj, L2_ffn_sh_gate, L2_ffn_sh_up, L2_ffn_sh_down, L3_attn_time_maa_x, L3_attn_time_maa_w, L3_attn_time_maa_k, L3_attn_time_maa_v, L3_attn_time_maa_r, L3_attn_time_maa_g, L3_attn_time_maa_w1, L3_attn_time_maa_w2, L3_attn_time_decay, L3_attn_time_decay_w1, L3_attn_time_decay_w2, L3_attn_time_faaaa, L3_attn_Wr, L3_attn_Wk, L3_attn_Wv, L3_attn_Wg, L3_attn_Wo, L3_attn_ln_w, L3_attn_ln_b, L3_ffn_ln1_g, L3_ffn_ln1_b, L3_ffn_ln2_g, L3_ffn_ln2_b, L3_ffn_wq, L3_ffn_bq, L3_ffn_wk, L3_ffn_bk, L3_ffn_wv, L3_ffn_bv, L3_ffn_wo, L3_ffn_bo, L3_ffn_gate_w, L3_ffn_gate_b, L3_ffn_w1, L3_ffn_b1, L3_ffn_w2, L3_ffn_b2):

    def _L0_attn_ref(x, W_x, W_dt, b_dt, A_log, D, W_out, b_out):
        import jax, jax.numpy as jnp
        import numpy as np
        DT_RANK = 64
        N_STATES = 16

        def selective_scan(u, delta, A, B, C, D):
            dA = jnp.einsum('bld,dn->bldn', delta, A)
            dB_u = jnp.einsum('bld,bld,bln->bldn', delta, u, B)
            dA_shift = jnp.concatenate([dA[:, 1:], jnp.zeros_like(dA[:, :1])], axis=1)
            dA_cumsum = jnp.exp(jnp.flip(jnp.cumsum(jnp.flip(dA_shift, axis=1), axis=1), axis=1))
            xs = jnp.cumsum(dB_u * dA_cumsum, axis=1) / (dA_cumsum + 1e-12)
            y = jnp.einsum('bldn,bln->bld', xs, C)
            return y + u * D
        n = A_log.shape[1]
        A = -jnp.exp(A_log)
        x_dbl = jnp.einsum('bld,de->ble', x, W_x)
        delta = x_dbl[..., :DT_RANK]
        B = x_dbl[..., DT_RANK:DT_RANK + n]
        C = x_dbl[..., DT_RANK + n:]
        delta = jax.nn.softplus(jnp.einsum('blr,rd->bld', delta, W_dt) + b_dt)
        y = selective_scan(x, delta, A, B, C, D)
        return jnp.einsum('bld,de->ble', y, W_out) + b_out

    def _L0_ffn_ref(x, expert_tokens, W1, b1, W2, b2, W3, b3):
        import jax, jax.numpy as jnp
        import numpy as np
        D_MODEL = 128
        D_HIDDEN = 512
        NUM_EXPERT = 8
        TOP_K = 2
        B, N = (1, 1024)

        def _expert_mlp(x, W1, b1, W2, b2, W3, b3):
            h = jax.nn.gelu(jnp.einsum('bnd,dh->bnh', x, W1) + b1, approximate=False)
            h = jax.nn.gelu(jnp.einsum('bnh,hk->bnk', h, W2) + b2, approximate=False)
            return jnp.einsum('bnh,hd->bnd', h, W3) + b3
        scores = jnp.einsum('bnd,ed->bne', x, expert_tokens)
        _, topk_idx = jax.lax.top_k(scores, TOP_K)
        outputs = jnp.zeros_like(x)
        num_expert = W1.shape[0]
        for i in range(num_expert):
            w = jnp.mean((topk_idx == i).astype(x.dtype), axis=-1, keepdims=True)
            y = _expert_mlp(x, W1[i], b1[i], W2[i], b2[i], W3[i], b3[i])
            outputs = outputs + y * w
        return outputs

    def _L1_attn_ref(x, mask, Wq, Wk, Wv, Wout):
        import jax, jax.numpy as jnp
        import numpy as np
        B, S, D, H = (4, 256, 128, 16)
        DH = D // H
        n, s, d = x.shape
        scale = 1.0 / np.sqrt(DH).astype(np.float32)
        q = (x @ Wq).reshape(n, s, H, DH)
        k = (x @ Wk).reshape(n, s, H, DH)
        v = (x @ Wv).reshape(n, s, H, DH)
        attn = jnp.einsum('nqhd,nkhd->nqkh', q, k) * scale
        attn = jax.nn.softmax(attn, axis=-2)
        z = jnp.einsum('nqkh,nkhd->nqhd', attn, v).reshape(n, s, d)
        z = jnp.einsum('nqd,de->nqe', z, Wout)
        return x + z

    def _L1_ffn_ref(hidden_states, gate_w, w1, w2, w3):
        import jax, jax.numpy as jnp
        import numpy as np
        E, K, D, H = (8, 2, 128, 256)
        B, S = (1, 128)

        def _grouped_swiglu(x_sorted, counts, w1, w2, w3):
            if hasattr(jax.lax, 'ragged_dot'):
                gs = counts.astype(jnp.int32)
                h = jax.nn.silu(jax.lax.ragged_dot(x_sorted, w1, gs)) * jax.lax.ragged_dot(x_sorted, w3, gs)
                return jax.lax.ragged_dot(h, w2, gs)
            pos = jnp.arange(x_sorted.shape[0])
            eid = jnp.searchsorted(jnp.cumsum(counts), pos, side='right')
            out = jnp.zeros((x_sorted.shape[0], w2.shape[-1]), x_sorted.dtype)
            for e in range(w1.shape[0]):
                xm = jnp.where((eid == e)[:, None], x_sorted, 0.0)
                he = jax.nn.silu(xm @ w1[e]) * (xm @ w3[e])
                out = out + he @ w2[e]
            return out
        x = hidden_states.reshape(-1, D)
        N = x.shape[0]
        scores = jax.nn.softmax(x @ gate_w.T, axis=-1)
        top_scores, sel = jax.lax.top_k(scores, K)
        sel_flat = sel.T.reshape(-1)
        scores_flat = top_scores.T.reshape(-1)
        order = jnp.argsort(sel_flat, stable=True)
        tok_sorted = order % N
        scores_sorted = scores_flat[order]
        counts = jnp.bincount(sel_flat, length=E)
        x_sorted = x[tok_sorted]
        y = _grouped_swiglu(x_sorted, counts, w1, w2, w3)
        weighted = y * scores_sorted[:, None]
        out = jnp.zeros((N, D), x.dtype).at[tok_sorted].add(weighted)
        return out.reshape(hidden_states.shape)

    def _L2_attn_ref(hidden_states, Wq, bq, Wv, bv, anomaly_matrix):
        import jax, jax.numpy as jnp
        import numpy as np
        HIDDEN = 128
        B, S = (8, 256)
        input_norm = jnp.linalg.norm(hidden_states, axis=-1, keepdims=True)
        scaled = hidden_states / (input_norm + 1e-09)
        q = jnp.einsum('bsh,oh->bso', scaled, Wq) + bq
        v = jnp.einsum('bsh,oh->bso', scaled, Wv) + bv
        tq = jnp.einsum('bsh,hk->bsk', q, anomaly_matrix)
        scores = jnp.einsum('bsh,bth->bst', q, tq) / jnp.sqrt(jnp.float32(HIDDEN))
        probs = jax.nn.softmax(scores, axis=-1)
        ctx = jnp.einsum('bst,bth->bsh', probs, v)
        return ctx * input_norm

    def _L2_ffn_ref(x, router_w, router_bias, up_proj, gate_proj, down_proj, sh_gate, sh_up, sh_down):
        import jax, jax.numpy as jnp
        import numpy as np
        DIM = 128
        EXPERT_DIM = 64
        N_EXPERTS = 16
        TOPK = 2
        SHARED_HIDDEN = EXPERT_DIM * TOPK
        B, T = (4, 128)

        def _moe_forward(x, router_w, router_bias, up_proj, gate_proj, down_proj, sh_gate, sh_up, sh_down):
            Bb, Tt, D = x.shape
            flat = x.reshape(Bb * Tt, D)
            N = flat.shape[0]
            logits = flat @ router_w.T
            topk_scores, topk_idx = jax.lax.top_k(logits + router_bias, TOPK)
            topk_scores = jax.nn.softmax(topk_scores, axis=-1)
            combine = jnp.zeros((N, N_EXPERTS), flat.dtype)
            combine = combine.at[jnp.arange(N)[:, None], topk_idx].add(topk_scores)
            up_all = jnp.einsum('nd,kde->nke', flat, up_proj)
            gate_all = jnp.einsum('nd,kde->nke', flat, gate_proj)
            hidden = jax.nn.silu(gate_all) * up_all
            down_all = jnp.einsum('nke,ked->nkd', hidden, down_proj)
            out = jnp.einsum('nk,nkd->nd', combine, down_all)
            sh_hidden = jax.nn.silu(flat @ sh_gate.T) * (flat @ sh_up.T)
            out = out + sh_hidden @ sh_down.T
            return out.reshape(Bb, Tt, D)
        return _moe_forward(x, router_w, router_bias, up_proj, gate_proj, down_proj, sh_gate, sh_up, sh_down)

    def _L3_attn_ref(x, time_maa_x, time_maa_w, time_maa_k, time_maa_v, time_maa_r, time_maa_g, time_maa_w1, time_maa_w2, time_decay, time_decay_w1, time_decay_w2, time_faaaa, Wr, Wk, Wv, Wg, Wo, ln_w, ln_b):
        import jax, jax.numpy as jnp
        import numpy as np
        B, T, C = (4, 128, 128)
        HEAD_SIZE = 64
        H = C // HEAD_SIZE
        N_LAYER, LAYER_ID = (24, 12)
        D_MIX_LORA, D_DECAY_LORA = (32, 64)
        HEAD_SIZE_DIVISOR = 8
        LN_EPS = 1e-05 * HEAD_SIZE_DIVISOR ** 2

        def _wkv6(r, k, v, w, u):

            def step(S, inp):
                r_t, k_t, v_t, w_t = inp
                y = jnp.einsum('bhj,bhji->bhi', r_t, S) + jnp.sum(r_t * u * k_t, axis=-1, keepdims=True) * v_t
                decay = jnp.exp(-jnp.exp(w_t))
                S = decay[..., None] * S + k_t[..., None] * v_t[..., None, :]
                return (S, y)
            to_t = lambda a: jnp.transpose(a, (1, 0, 2, 3))
            S0 = jnp.zeros(r.shape[:1] + (r.shape[2], r.shape[3], r.shape[3]), r.dtype)
            _, ys = jax.lax.scan(step, S0, (to_t(r), to_t(k), to_t(v), to_t(w)))
            return jnp.transpose(ys, (1, 0, 2, 3))
        b, t, c = x.shape
        h, n = (H, HEAD_SIZE)
        xx = jnp.concatenate([jnp.zeros_like(x[:, :1]), x[:, :-1]], axis=1) - x
        xxx = x + xx * time_maa_x
        mix = jnp.tanh(xxx @ time_maa_w1).reshape(b, t, 5, D_MIX_LORA)
        m = jnp.einsum('btsd,sdc->sbtc', mix, time_maa_w2)
        xw = x + xx * (time_maa_w + m[0])
        xk = x + xx * (time_maa_k + m[1])
        xv = x + xx * (time_maa_v + m[2])
        xr = x + xx * (time_maa_r + m[3])
        xg = x + xx * (time_maa_g + m[4])
        r = xr @ Wr
        k = xk @ Wk
        v = xv @ Wv
        g = jax.nn.silu(xg @ Wg)
        w = time_decay + jnp.tanh(xw @ time_decay_w1) @ time_decay_w2
        y = _wkv6(r.reshape(b, t, h, n), k.reshape(b, t, h, n), v.reshape(b, t, h, n), w.reshape(b, t, h, n), time_faaaa)
        mu = y.mean(-1, keepdims=True)
        var = y.var(-1, keepdims=True)
        yn = ((y - mu) / jnp.sqrt(var + LN_EPS)).reshape(b, t, c) * ln_w + ln_b
        return yn * g @ Wo

    def _L3_ffn_ref(x, ln1_g, ln1_b, ln2_g, ln2_b, wq, bq, wk, bk, wv, bv, wo, bo, gate_w, gate_b, w1, b1, w2, b2):
        import jax, jax.numpy as jnp
        import numpy as np
        B, S, H, NH, E, F = (4, 128, 128, 16, 8, 512)
        D = H // NH
        EPS = 1e-05

        def _layernorm(x, g, b):
            mu = jnp.mean(x, axis=-1, keepdims=True)
            var = jnp.var(x, axis=-1, keepdims=True)
            return (x - mu) * jax.lax.rsqrt(var + EPS) * g + b
        b, s, h = x.shape
        hn = _layernorm(x, ln1_g, ln1_b)
        q = (hn @ wq + bq).reshape(b, s, NH, D).transpose(0, 2, 1, 3)
        k = (hn @ wk + bk).reshape(b, s, NH, D).transpose(0, 2, 1, 3)
        v = (hn @ wv + bv).reshape(b, s, NH, D).transpose(0, 2, 1, 3)
        scores = jnp.einsum('bhqd,bhkd->bhqk', q, k) / jnp.sqrt(jnp.float32(D))
        attn = jax.nn.softmax(scores, axis=-1)
        o = jnp.einsum('bhqk,bhkd->bhqd', attn, v)
        o = o.transpose(0, 2, 1, 3).reshape(b, s, h)
        x = x + (o @ wo + bo)
        hn2 = _layernorm(x, ln2_g, ln2_b).reshape(-1, h)
        logits = hn2 @ gate_w + gate_b
        idx = jnp.argmax(logits, axis=-1)
        mid = jax.nn.relu(jnp.einsum('th,ehf->etf', hn2, w1) + b1[:, None, :])
        y = jnp.einsum('etf,efh->eth', mid, w2) + b2[:, None, :]
        moe = y[idx, jnp.arange(hn2.shape[0])]
        return x + moe.reshape(b, s, h)
    x = L0_attn_x
    xn = _layernorm(x, axis=-1)
    s = _L0_attn_ref(xn, L0_attn_W_x, L0_attn_W_dt, L0_attn_b_dt, L0_attn_A_log, L0_attn_D, L0_attn_W_out, L0_attn_b_out)
    g = _silu(_L0_ffn_ref(xn, L0_ffn_expert_tokens, L0_ffn_W1, L0_ffn_b1, L0_ffn_W2, L0_ffn_b2, L0_ffn_W3, L0_ffn_b3))
    x = x + s * g
    xn = _layernorm(x, axis=-1)
    s = _L1_attn_ref(xn, L1_attn_mask, L1_attn_Wq, L1_attn_Wk, L1_attn_Wv, L1_attn_Wout)
    g = _silu(_L1_ffn_ref(xn, L1_ffn_gate_w, L1_ffn_w1, L1_ffn_w2, L1_ffn_w3))
    x = x + s * g
    xn = _layernorm(x, axis=-1)
    s = _L2_attn_ref(xn, L2_attn_Wq, L2_attn_bq, L2_attn_Wv, L2_attn_bv, L2_attn_anomaly_matrix)
    g = _silu(_L2_ffn_ref(xn, L2_ffn_router_w, L2_ffn_router_bias, L2_ffn_up_proj, L2_ffn_gate_proj, L2_ffn_down_proj, L2_ffn_sh_gate, L2_ffn_sh_up, L2_ffn_sh_down))
    x = x + s * g
    xn = _layernorm(x, axis=-1)
    s = _L3_attn_ref(xn, L3_attn_time_maa_x, L3_attn_time_maa_w, L3_attn_time_maa_k, L3_attn_time_maa_v, L3_attn_time_maa_r, L3_attn_time_maa_g, L3_attn_time_maa_w1, L3_attn_time_maa_w2, L3_attn_time_decay, L3_attn_time_decay_w1, L3_attn_time_decay_w2, L3_attn_time_faaaa, L3_attn_Wr, L3_attn_Wk, L3_attn_Wv, L3_attn_Wg, L3_attn_Wo, L3_attn_ln_w, L3_attn_ln_b)
    g = _silu(_L3_ffn_ref(xn, L3_ffn_ln1_g, L3_ffn_ln1_b, L3_ffn_ln2_g, L3_ffn_ln2_b, L3_ffn_wq, L3_ffn_bq, L3_ffn_wk, L3_ffn_bk, L3_ffn_wv, L3_ffn_bv, L3_ffn_wo, L3_ffn_bo, L3_ffn_gate_w, L3_ffn_gate_b, L3_ffn_w1, L3_ffn_b1, L3_ffn_w2, L3_ffn_b2))
    x = x + s * g
    return x

_drawn_inputs = setup_inputs


def setup_inputs(seed=0):
    import zlib

    import numpy as np

    out = dict(_drawn_inputs(seed))
    spreads = {'L0_attn_b_dt': (0.0, 0.8),
     'L0_attn_D': (1.0, 0.2),
     'L0_attn_b_out': (0.0, 0.38),
     'L0_ffn_b1': (0.0, 0.339),
     'L0_ffn_b2': (0.0, 0.1),
     'L0_ffn_b3': (0.0, 0.1),
     'L2_attn_bq': (0.0, 0.8),
     'L2_attn_bv': (0.0, 0.8),
     'L2_ffn_router_bias': (0.0, 0.8),
     'L3_attn_ln_w': (1.0, 0.6),
     'L3_attn_ln_b': (0.0, 0.8),
     'L3_ffn_ln1_g': (1.0, 0.6),
     'L3_ffn_ln1_b': (0.0, 0.8),
     'L3_ffn_ln2_g': (1.0, 0.6),
     'L3_ffn_ln2_b': (0.0, 2.0),
     'L3_ffn_bq': (0.0, 2.0),
     'L3_ffn_bk': (0.0, 2.0),
     'L3_ffn_bv': (0.0, 2.0),
     'L3_ffn_bo': (0.0, 0.8),
     'L3_ffn_gate_b': (0.0, 2.0),
     'L3_ffn_b1': (0.0, 2.0),
     'L3_ffn_b2': (0.0, 2.0)}
    factors = {'L1_attn_Wq': 3.658,
     'L1_attn_Wk': 3.45,
     'L1_attn_Wv': 3.662,
     'L1_attn_Wout': 3.537,
     'L2_attn_Wq': 8.0,
     'L2_attn_Wv': 8.0,
     'L2_attn_anomaly_matrix': 8.0,
     'L2_ffn_router_w': 8.0,
     'L2_ffn_up_proj': 8.0,
     'L2_ffn_gate_proj': 8.0,
     'L2_ffn_down_proj': 8.0,
     'L2_ffn_sh_gate': 8.0,
     'L2_ffn_sh_up': 8.0,
     'L2_ffn_sh_down': 8.0,
     'L3_attn_time_maa_x': 25.221,
     'L3_attn_time_maa_w': 64.0,
     'L3_attn_time_maa_w1': 8.0,
     'L3_attn_time_maa_w2': 8.0,
     'L3_attn_time_decay_w1': 64.0,
     'L3_attn_time_decay_w2': 64.0,
     'L3_attn_time_faaaa': 45.8,
     'L3_ffn_wq': 8.0,
     'L3_ffn_wk': 8.0,
     'L3_ffn_wv': 8.0,
     'L3_ffn_wo': 5.95,
     'L3_ffn_w1': 25.112,
     'L3_attn_time_maa_k': 5.029,
     'L3_attn_time_maa_v': 5.914,
     'L3_attn_time_maa_r': 4.163,
     'L3_attn_time_maa_g': 4.698,
     'L3_ffn_gate_w': 8.0,
     'L3_ffn_w2': 8.0}
    for name, (base, spread) in spreads.items():
        noise = np.random.default_rng([zlib.crc32(name.encode()), seed]).standard_normal(out[name].shape)
        drawn = base * np.exp(spread * noise) if base else spread * noise
        out[name] = jnp.asarray(drawn.astype(out[name].dtype))
    for name, factor in factors.items():
        out[name] = (out[name] * factor).astype(out[name].dtype)
    return out
```

```python
from contextlib import ExitStack

import numpy as np
import concourse.bass as bass
from concourse import mybir

ALU = mybir.AluOpType
ACT = mybir.ActivationFunctionType
F32 = mybir.dt.float32
BF16 = mybir.dt.bfloat16
U32 = mybir.dt.uint32
AX = mybir.AxisListType

P = 128
BATCH, SEQ = 2, 1024
TOK = BATCH * SEQ
NT = TOK // P
CH = 512
NC = TOK // CH
SLOTS = 18
NSTATE = 16
HEADS, DH = 16, 8
WKV_HEAD = 64
WC = 16
NWC = TOK // WC


class Layout:

    def __init__(self, parts):
        self.at, self.width = {}, 0
        for name, p, n in parts:
            self.at[name] = (self.width, p, n)
            self.width += n


SMALL = Layout([
    ("W_x", 128, 96), ("W_dt", 64, 128), ("W_out", 128, 128), ("A_log", 128, 16), ("b_dt", 128, 1), ("D", 128, 1),
    ("b_out", 128, 1), ("tokens", 128, 8), ("e_b1", 128, 32), ("e_b2", 128, 32), ("e_b3", 8, 128),
    ("q1", 128, 128), ("k1", 128, 128), ("v1", 128, 128), ("o1", 128, 128), ("gate1", 128, 8),
    ("q2", 128, 128), ("v2", 128, 128), ("anomaly", 128, 128), ("bq2", 128, 1), ("bv2", 128, 128),
    ("router", 128, 16), ("router_bias", 128, 16),
    ("maa_x", 128, 1), ("maa", 128, 5), ("maa_w1", 128, 160), ("maa_w2", 32, 640), ("decay_w1", 128, 64),
    ("decay_w2", 64, 128), ("decay", 128, 1), ("faaaa", 128, 1), ("Wr", 128, 128), ("Wk", 128, 128),
    ("Wv", 128, 128), ("Wg", 128, 128), ("Wo", 128, 128), ("ln_w", 128, 1), ("ln_b", 128, 1),
    ("ln1_g", 128, 1), ("ln1_b", 128, 1), ("ln2_g", 128, 1), ("ln2_b", 128, 1), ("q3", 128, 128), ("k3", 128, 128),
    ("v3", 128, 128), ("o3", 128, 128), ("bq3", 128, 1), ("bk3", 128, 1), ("bv3", 128, 1), ("bo3", 128, 1),
    ("gate3", 128, 8), ("gate_b3", 128, 8), ("f_b1", 128, 32), ("f_b2", 8, 128),
])
CONSTS = Layout([
    ("ident", 128, 128), ("ones", 128, 128), ("mean", 128, 128), ("head_ones", 128, 128), ("head_mean", 128, 128),
    ("iota", 128, 16), ("even", 128, 1), ("odd", 128, 1), ("eps_1e5", 128, 1), ("eps_scan", 128, 1),
    ("eps_wkv", 128, 1), ("start", 128, 16), ("zero", 128, 1),
])


class Kit:

    def __init__(self, nc, slots, small, consts, experts, sel, psum, scratch):
        self.nc, self.slots, self.small, self.consts = nc, slots, small, consts
        self.experts, self.sel, self.psum, self.scratch = experts, sel, psum, scratch

    def slot(self, i):
        return self.slots[:, i, :]

    def chunk(self, i, c):
        return self.slots[:, i, c * CH:(c + 1) * CH]

    def w(self, name):
        a, p, n = SMALL.at[name]
        return self.small[0:p, a:a + n]

    def c(self, name):
        a, p, n = CONSTS.at[name]
        return self.consts[0:p, a:a + n]

    def bank(self, b):
        return self.psum[:, b, :]


class Stage:

    def __init__(self, kit, name):
        self.kit, self.name, self.stack, self.sems = kit, name, ExitStack(), []

    def __enter__(self):
        self.stack.__enter__()
        return self

    def sem(self, name):
        self.sems.append(self.kit.nc.alloc_semaphore(f"{self.name}_{name}"))
        return self.sems[-1]

    def block(self):
        return self.stack.enter_context(self.kit.nc.Block())

    def __exit__(self, *e):
        self.stack.__exit__(*e)
        if e[0] is None:
            for sem in self.sems:
                self.kit.nc.gpsimd.sem_clear(sem)
                self.kit.nc.release_semaphore(sem)


def spread(ap, n):
    return ap.unsqueeze(2).broadcast_to([ap.shape[0], ap.shape[1], n])



def load_inputs(kit, x_dram, small_dram, consts_dram, sel_dram, x):
    with Stage(kit, "load") as st:
        loaded, sel_loaded = st.sem("loaded"), st.sem("sel_loaded")
        block = st.block()
        sel_f32 = flat_slots(kit, X + 1, 3)[0:96, 0:40 * P]

        @block.sync
        def _(sp):
            sp.dma_start(kit.slot(x), x_dram).then_inc(loaded, 16)
            sp.dma_start(kit.small[:, :], small_dram).then_inc(loaded, 16)

        @block.scalar
        def _(act):
            act.dma_start(kit.consts[:, :], consts_dram).then_inc(loaded, 16)
            act.dma_start(sel_f32, sel_dram).then_inc(sel_loaded, 16)
            act.wait_ge(loaded, 48)

        @block.vector
        def _(dve):
            dve.wait_ge(sel_loaded, 16)
            nc = kit.nc
            nc.vector.tensor_copy(kit.sel[:, :, :].rearrange("p a b -> p (a b)"), sel_f32)


def store_output(kit, out_dram, x, stored):
    with Stage(kit, "store") as st:
        block = st.block()

        @block.sync
        def _(sp):
            sp.dma_start(out_dram, kit.slot(x)).then_inc(stored, 16)
            sp.wait_ge(stored, 16)



def layer_norm(kit, name, src, dst, square, stat, gamma=None, beta=None):
    nc = kit.nc
    with Stage(kit, name) as st:
        mean_ready, centered, squared, var_ready = map(st.sem, ("mean", "centered", "squared", "var"))
        std_ready, rstd_ready, diag_ready, bcast_ready = map(st.sem, ("std", "rstd", "diag", "bcast"))
        scaled = st.sem("scaled")
        std = kit.slot(stat)[:, 0:NT]
        rstd = kit.slot(stat)[:, NT:2 * NT]
        diag = kit.slot(square).rearrange("p (j q) -> p j q", q=P)
        block = st.block()

        @block.tensor
        def _(pe):
            for c in range(NC):
                nc.tensor.matmul(kit.bank(c), kit.c("mean"), kit.chunk(src, c), start=True, stop=True).then_inc(mean_ready, 1)
            for j in range(NT):
                pe.wait_ge(squared, j // 4 + 1)
                last = nc.tensor.matmul(kit.psum[:, 4, j:j + 1], kit.slot(square)[:, j * P:(j + 1) * P],
                                        kit.c("mean")[:, 0:1], start=True, stop=True)
            last.then_inc(var_ready, 1)
            pe.wait_ge(diag_ready, 1)
            for c in range(NC):
                nc.tensor.matmul(kit.bank(c), kit.c("ones"), kit.chunk(square, c), start=True, stop=True).then_inc(bcast_ready, 1)

        @block.vector
        def _(dve):
            for c in range(NC):
                dve.wait_ge(mean_ready, c + 1)
                nc.vector.tensor_tensor(kit.chunk(dst, c), kit.chunk(src, c), kit.bank(c), ALU.subtract).then_inc(centered, 1)
            dve.wait_ge(std_ready, 1)
            nc.vector.reciprocal(rstd, std).then_inc(rstd_ready, 1)
            dve.wait_ge(rstd_ready, 1)
            nc.vector.tensor_tensor(diag, kit.c("ident").unsqueeze(1).broadcast_to([P, NT, P]), spread(rstd, P),
                                    ALU.mult).then_inc(diag_ready, 1)
            for c in range(NC):
                dve.wait_ge(bcast_ready, c + 1)
                if gamma is None:
                    nc.vector.tensor_tensor(kit.chunk(dst, c), kit.chunk(dst, c), kit.bank(c), ALU.mult).then_inc(scaled, 1)
                else:
                    nc.vector.scalar_tensor_tensor(kit.chunk(dst, c), kit.bank(c), kit.w(gamma), kit.chunk(dst, c),
                                                   ALU.mult, ALU.mult).then_inc(scaled, 1)
                    dve.wait_ge(scaled, 2 * c + 1)
                    nc.vector.tensor_scalar(kit.chunk(dst, c), kit.chunk(dst, c), kit.w(beta), None,
                                            ALU.add).then_inc(scaled, 1)

        @block.scalar
        def _(act):
            for c in range(NC):
                act.wait_ge(centered, c + 1)
                nc.scalar.activation(kit.chunk(square, c), kit.chunk(dst, c), ACT.Square).then_inc(squared, 1)
            act.wait_ge(var_ready, 1)
            nc.scalar.activation(std, kit.psum[:, 4, 0:NT], ACT.Sqrt, bias=kit.c("eps_1e5")).then_inc(std_ready, 1)



def project(kit, name, jobs):
    nc = kit.nc
    with Stage(kit, name) as st:
        product, by_act, by_dve = map(st.sem, ("product", "by_act", "by_dve"))
        block = st.block()
        steps = [(job, c) for job in jobs for c in range(NC)]

        @block.tensor
        def _(pe):
            for i, ((dst, w, src, bias), c) in enumerate(steps):
                if i >= 8:
                    pe.wait_ge(by_act if i % 2 == 0 else by_dve, (i - 8) // 2 + 1)
                nc.tensor.matmul(kit.bank(i % 8), kit.w(w), kit.chunk(src, c), start=True, stop=True).then_inc(product, 1)

        @block.scalar
        def _(act):
            for i, ((dst, w, src, bias), c) in enumerate(steps):
                if i % 2 == 0:
                    act.wait_ge(product, i + 1)
                    nc.scalar.activation(kit.chunk(dst, c), kit.bank(i % 8), ACT.Identity,
                                         bias=kit.w(bias) if bias else 0.0).then_inc(by_act, 1)

        @block.vector
        def _(dve):
            for i, ((dst, w, src, bias), c) in enumerate(steps):
                if i % 2 == 1:
                    dve.wait_ge(product, i + 1)
                    if bias:
                        nc.vector.tensor_scalar(kit.chunk(dst, c), kit.bank(i % 8), kit.w(bias), None, ALU.add).then_inc(by_dve, 1)
                    else:
                        nc.vector.tensor_copy(kit.chunk(dst, c), kit.bank(i % 8)).then_inc(by_dve, 1)



def selective_scan(kit, xn, out, free):
    nc = kit.nc
    low, delta, du, suffix, y, decay, inv, work, rows, tmp = free
    with Stage(kit, "scan_in") as st:
        proj, low_ready, bc_ready, z_ready, z_copied = map(st.sem, ("proj", "low", "bc", "z", "z_copied"))
        neg_abs, exped, logged, own, a_exp = map(st.sem, ("neg_abs", "exped", "logged", "own", "a_exp"))
        block = st.block()
        bc = kit.slot(rows)[0:32, :]

        @block.tensor
        def _(pe):
            for c in range(NC):
                nc.tensor.matmul(kit.bank(c)[0:64], kit.w("W_x")[:, 0:64], kit.chunk(xn, c), start=True, stop=True).then_inc(proj, 1)
            for c in range(NC):
                nc.tensor.matmul(kit.bank(4 + c)[0:32], kit.w("W_x")[:, 64:96], kit.chunk(xn, c), start=True, stop=True).then_inc(proj, 1)
            for c in range(NC):
                pe.wait_ge(low_ready, c + 1)
                nc.tensor.matmul(kit.bank(c), kit.w("W_dt"), kit.chunk(low, c)[0:64], start=True, stop=True).then_inc(z_ready, 1)

        @block.scalar
        def _(act):
            nc.scalar.preload_act_table_set("natural_log_exp_and_others")
            nc.scalar.activation(kit.scratch[:, 0:NSTATE], kit.w("A_log"), ACT.Exp).then_inc(a_exp, 1)
            for c in range(NC):
                act.wait_ge(proj, c + 1)
                nc.scalar.activation(kit.chunk(low, c)[0:64], kit.bank(c)[0:64], ACT.Copy).then_inc(low_ready, 1)
            for c in range(NC):
                act.wait_ge(z_ready, c + 1)
                nc.scalar.activation(kit.chunk(delta, c), kit.bank(c), ACT.Identity, bias=kit.w("b_dt")).then_inc(z_copied, 1)
            for c in range(NC):
                act.wait_ge(neg_abs, c + 1)
                nc.scalar.activation(kit.chunk(suffix, c), kit.chunk(suffix, c), ACT.Exp).then_inc(exped, 1)
                act.wait_ge(exped, c + 1)
                nc.scalar.activation(kit.chunk(suffix, c), kit.chunk(suffix, c), ACT.Ln, bias=kit.c("ones")[:, 0:1]).then_inc(logged, 1)

        @block.vector
        def _(dve):
            for c in range(NC):
                dve.wait_ge(proj, NC + c + 1)
                nc.vector.tensor_copy(kit.chunk(rows, c)[0:32], kit.bank(4 + c)[0:32]).then_inc(bc_ready, 1)
            dve.wait_ge(a_exp, 1)
            nc.vector.tensor_scalar(kit.scratch[:, 16:32], kit.scratch[:, 0:NSTATE], -1.0, None, ALU.mult)
            for c in range(NC):
                dve.wait_ge(z_copied, c + 1)
                nc.vector.scalar_tensor_tensor(kit.chunk(suffix, c), kit.chunk(delta, c), -1.0, kit.chunk(delta, c),
                                               ALU.mult, ALU.min).then_inc(neg_abs, 1)
            for c in range(NC):
                dve.wait_ge(logged, c + 1)
                nc.vector.scalar_tensor_tensor(kit.chunk(delta, c), kit.chunk(delta, c), 0.0, kit.chunk(suffix, c),
                                               ALU.max, ALU.add).then_inc(own, 1)
            dve.wait_ge(own, NC)
            for b in range(BATCH):
                a, z = b * SEQ, (b + 1) * SEQ
                nc.vector.tensor_tensor_scan(kit.slot(suffix)[:, a:z - 1][:, ::-1],
                                             kit.c("ones")[:, 0:1].broadcast_to([P, SEQ - 1]),
                                             kit.slot(delta)[:, a + 1:z][:, ::-1], 0.0, ALU.mult, ALU.add)
                nc.vector.memset(kit.slot(suffix)[:, z - 1:z], 0.0)
            nc.vector.tensor_tensor(kit.slot(du), kit.slot(delta), kit.slot(xn), ALU.mult)
            nc.vector.tensor_scalar(kit.slot(y), kit.slot(xn), kit.w("D"), None, ALU.mult)

    split_rows(kit, "scan_split", rows, 2 * NSTATE, low, tmp)
    a_neg = kit.scratch[:, 16:32]
    stacked = kit.slot(low).bitcast(BF16)[0:96, 0:TOK]
    with Stage(kit, "scan") as st:
        b_bcast, c_bcast, s_ready, log_ready, inv_ready, bu = map(st.sem, ("b", "c", "s", "log", "inv", "bu"))
        bus, scanned, c_used, weighted, y_ready, b_used = map(st.sem, ("bus", "scanned", "c_used", "weighted", "y", "b_used"))
        block = st.block()

        @block.tensor
        def _(pe):
            for n in range(NSTATE):
                for which, row, done, used in ((0, n, b_bcast, b_used), (1, NSTATE + n, c_bcast, c_used)):
                    if n >= 1:
                        pe.wait_ge(used, n)
                    for c in range(NC):
                        last = nc.tensor.matmul(kit.bank(4 * which + c), kit.sel[0:96, row, :],
                                                stacked[:, c * CH:(c + 1) * CH], start=True, stop=True)
                    last.then_inc(done, 1)

        @block.scalar
        def _(act):
            nc.scalar.preload_act_table_set("natural_log_exp_and_others")
            for n in range(NSTATE):
                if n >= 1:
                    act.wait_ge(bus, n)
                nc.scalar.activation(kit.slot(decay), kit.slot(suffix), ACT.Exp, scale=a_neg[:, n:n + 1]).then_inc(s_ready, 1)
                act.wait_ge(s_ready, n + 1)
                if n >= 1:
                    act.wait_ge(weighted, n)
                nc.scalar.activation(kit.slot(inv), kit.slot(decay), ACT.Ln, bias=kit.c("eps_scan")).then_inc(log_ready, 1)
                act.wait_ge(log_ready, n + 1)
                nc.scalar.activation(kit.slot(inv), kit.slot(inv), ACT.Exp, scale=-1.0).then_inc(inv_ready, 1)

        @block.vector
        def _(dve):
            bank_b = kit.psum[:, 0:4, :].rearrange("p a b -> p (a b)")
            bank_c = kit.psum[:, 4:8, :].rearrange("p a b -> p (a b)")
            for n in range(NSTATE):
                dve.wait_ge(b_bcast, n + 1)
                if n >= 1:
                    dve.wait_ge(weighted, n)
                nc.vector.tensor_tensor(kit.slot(work), kit.slot(du), bank_b, ALU.mult).then_inc(b_used, 1)
                dve.wait_ge(b_used, n + 1)
                dve.wait_ge(s_ready, n + 1)
                nc.vector.tensor_tensor(kit.slot(work), kit.slot(work), kit.slot(decay), ALU.mult).then_inc(bus, 1)
                dve.wait_ge(bus, n + 1)
                for b in range(BATCH):
                    a, z = b * SEQ, (b + 1) * SEQ
                    nc.vector.tensor_tensor_scan(kit.slot(rows)[:, a:z], kit.c("ones")[:, 0:1].broadcast_to([P, SEQ]),
                                                 kit.slot(work)[:, a:z], 0.0, ALU.mult, ALU.add).then_inc(scanned, 1)
                dve.wait_ge(scanned, BATCH * (n + 1))
                dve.wait_ge(c_bcast, n + 1)
                nc.vector.tensor_tensor(kit.slot(work), kit.slot(rows), bank_c, ALU.mult).then_inc(c_used, 1)

        @block.gpsimd
        def _(pool):
            for n in range(NSTATE):
                pool.wait_ge(c_used, n + 1)
                pool.wait_ge(inv_ready, n + 1)
                if n >= 1:
                    pool.wait_ge(y_ready, n)
                nc.gpsimd.tensor_tensor(kit.slot(tmp), kit.slot(work), kit.slot(inv), ALU.mult).then_inc(weighted, 1)
                pool.wait_ge(weighted, n + 1)
                nc.gpsimd.tensor_tensor(kit.slot(y), kit.slot(y), kit.slot(tmp), ALU.add).then_inc(y_ready, 1)

    project(kit, "scan_out", [(out, "W_out", y, "b_out")])


def split_rows(kit, name, src, n, dst, tmp):
    nc = kit.nc
    rows = kit.slot(src)[0:n, :]
    rest = kit.slot(tmp)[0:n, :]
    parts = kit.slot(dst).bitcast(BF16)
    middle = parts[0:n, TOK:2 * TOK]
    with Stage(kit, name) as st:
        own = st.sem("own")
        block = st.block()

        @block.vector
        def _(dve):
            if n < 32:
                nc.vector.memset(kit.slot(dst)[0:96, 0:TOK // 2], 0.0).then_inc(own, 1)
                dve.wait_ge(own, 1)
            o = 1 if n < 32 else 0
            nc.vector.tensor_copy(parts[0:n, 0:TOK], rows).then_inc(own, 1)
            dve.wait_ge(own, o + 1)
            nc.vector.tensor_tensor(rest, rows, parts[0:n, 0:TOK], ALU.subtract).then_inc(own, 1)
            dve.wait_ge(own, o + 2)
            nc.vector.tensor_copy(middle, rest).then_inc(own, 1)
            dve.wait_ge(own, o + 3)
            nc.vector.tensor_copy(parts[32:32 + n, 0:TOK], middle)
            nc.vector.tensor_tensor(parts[64:64 + n, 0:TOK], rest, middle, ALU.subtract)



def router(kit, name, src, gate, bias, experts, rule, rows, stacked, work, tmp):
    nc = kit.nc
    flat = kit.slot(work)

    def field(at, n):
        return flat[:, at:at + NT * n].rearrange("p (j n) -> p j n", n=n)

    score, total, best = field(0, experts), field(256, 1), field(272, 8)
    index = flat[:, 400:400 + NT * 8].bitcast(U32).rearrange("p (j n) -> p j n", n=8)
    index_f, first, second = field(528, 8), field(656, experts), field(912, experts)
    e2, w1, w2, weight = field(1168, 1), field(1184, 1), field(1200, 1), field(1216, experts)
    iota = kit.c("iota")[:, 0:experts].unsqueeze(1).broadcast_to([P, NT, experts])

    def wide(ap):
        return ap.broadcast_to([P, NT, experts])

    with Stage(kit, name) as st:
        logits, exp_in, exp_out, own = map(st.sem, ("logits", "exp_in", "exp_out", "own"))
        weights_ready, turned = map(st.sem, ("weights", "turned"))
        block = st.block()

        @block.tensor
        def _(pe):
            for j in range(NT):
                last = nc.tensor.matmul(kit.bank(0)[:, j * experts:(j + 1) * experts], kit.slot(src)[:, j * P:(j + 1) * P],
                                        kit.w(gate), start=True, stop=True)
            last.then_inc(logits, 1)
            pe.wait_ge(weights_ready, 1)
            for j in range(NT):
                last = nc.tensor.transpose(kit.bank(4 + j // 4)[0:experts, (j % 4) * P:(j % 4 + 1) * P], weight[:, j, :],
                                           kit.c("ident"))
            last.then_inc(turned, 1)

        @block.scalar
        def _(act):
            if rule in ("scores", "top"):
                act.wait_ge(exp_in, 1)
                what = score if rule == "scores" else e2
                nc.scalar.activation(what, what, ACT.Exp).then_inc(exp_out, 1)

        @block.vector
        def _(dve):
            done = [0]

            def then(instruction):
                done[0] += 1
                instruction.then_inc(own, 1)
                dve.wait_ge(own, done[0])

            dve.wait_ge(logits, 1)
            raw = kit.bank(0)[:, 0:NT * experts].rearrange("p (j n) -> p j n", n=experts)
            if bias:
                then(nc.vector.tensor_tensor(score, raw, kit.w(bias).unsqueeze(1).broadcast_to([P, NT, experts]), ALU.add))
            else:
                then(nc.vector.tensor_copy(score, raw))
            if rule == "scores":
                then(nc.vector.tensor_reduce(total, score, AX.X, ALU.max))
                nc.vector.tensor_tensor(score, score, wide(total), ALU.subtract).then_inc(exp_in, 1)
                dve.wait_ge(exp_out, 1)
                then(nc.vector.tensor_reduce(total, score, AX.X, ALU.add))
                then(nc.vector.reciprocal(total, total))
                then(nc.vector.tensor_tensor(score, score, wide(total), ALU.mult))
            for j in range(NT):
                last = nc.vector.max(best[:, j, :], score[:, j, :])
            then(last)
            for j in range(NT):
                last = nc.vector.max_index(index[:, j, :], best[:, j, :], score[:, j, :])
            then(last)
            then(nc.vector.tensor_copy(index_f, index))
            nc.vector.tensor_tensor(first, iota, wide(index_f[:, :, 0:1]), ALU.is_equal)
            then(nc.vector.tensor_tensor(second, iota, wide(index_f[:, :, 1:2]), ALU.is_equal))
            if rule == "half":
                then(nc.vector.tensor_tensor(first, first, second, ALU.add))
                nc.vector.tensor_scalar(weight, first, 0.5, None, ALU.mult).then_inc(weights_ready, 1)
            elif rule == "scores":
                then(nc.vector.tensor_tensor(first, first, second, ALU.add))
                nc.vector.tensor_tensor(weight, first, score, ALU.mult).then_inc(weights_ready, 1)
            elif rule == "top":
                nc.vector.tensor_tensor(e2, best[:, :, 1:2], best[:, :, 0:1], ALU.subtract).then_inc(exp_in, 1)
                dve.wait_ge(exp_out, 1)
                then(nc.vector.tensor_scalar(w1, e2, 1.0, None, ALU.add))
                then(nc.vector.reciprocal(w1, w1))
                then(nc.vector.tensor_tensor(w2, w1, e2, ALU.mult))
                nc.vector.tensor_tensor(first, first, wide(w1), ALU.mult)
                then(nc.vector.tensor_tensor(second, second, wide(w2), ALU.mult))
                nc.vector.tensor_tensor(weight, first, second, ALU.add).then_inc(weights_ready, 1)
            else:
                nc.vector.tensor_copy(weight, first).then_inc(weights_ready, 1)
            dve.wait_ge(turned, 1)
            nc.vector.tensor_copy(kit.slot(rows)[0:experts, :], kit.psum[0:experts, 4:8, :].rearrange("p a b -> p (a b)"))

    split_rows(kit, name + "_split", rows, experts, stacked, tmp)


def spread_rows(kit, name, stacked, matrices, slots):
    nc = kit.nc
    parts = kit.slot(stacked).bitcast(BF16)[0:96, 0:TOK]
    with Stage(kit, name) as st:
        spread_ready, by_act, by_dve = map(st.sem, ("spread", "by_act", "by_dve"))
        block = st.block()

        @block.tensor
        def _(pe):
            for i, m in enumerate(matrices):
                if i >= 2:
                    pe.wait_ge(by_act if i % 2 == 0 else by_dve, i // 2)
                for c in range(NC):
                    last = nc.tensor.matmul(kit.bank(4 * (i % 2) + c), kit.sel[0:96, m, :], parts[:, c * CH:(c + 1) * CH],
                                            start=True, stop=True)
                last.then_inc(spread_ready, 1)

        @block.scalar
        def _(act):
            for i in range(0, len(matrices), 2):
                act.wait_ge(spread_ready, i + 1)
                nc.scalar.activation(kit.slot(slots[i]), kit.psum[:, 0:4, :].rearrange("p a b -> p (a b)"),
                                     ACT.Copy).then_inc(by_act, 1)

        @block.vector
        def _(dve):
            for i in range(1, len(matrices), 2):
                dve.wait_ge(spread_ready, i + 1)
                nc.vector.tensor_copy(kit.slot(slots[i]), kit.psum[:, 4:8, :].rearrange("p a b -> p (a b)")).then_inc(by_dve, 1)



def merge(kit, name, x, s, tmp, g=None):
    nc = kit.nc
    with Stage(kit, name) as st:
        gated, own = map(st.sem, ("gated", "own"))
        block = st.block()

        @block.scalar
        def _(act):
            for c in range(NC):
                nc.scalar.activation(kit.chunk(tmp, c), kit.bank(4 + c) if g is None else kit.chunk(g, c), ACT.Silu).then_inc(gated, 1)

        @block.vector
        def _(dve):
            for c in range(NC):
                dve.wait_ge(gated, c + 1)
                nc.vector.tensor_tensor(kit.chunk(tmp, c), kit.chunk(tmp, c), kit.chunk(s, c), ALU.mult).then_inc(own, 1)
                dve.wait_ge(own, c + 1)
                nc.vector.tensor_tensor(kit.chunk(x, c), kit.chunk(x, c), kit.chunk(tmp, c), ALU.add)



HID = 512
HB = HID // P
E0_COLS = HID + HB * HID + HB * P


def experts_gelu(kit, dram, xn, weights, rows, h1, h2):
    nc = kit.nc
    n_exp = 8
    steps = [(e, c) for e in range(n_exp) for c in range(NC)]
    w1 = [kit.experts[:, b * E0_COLS:b * E0_COLS + HID] for b in range(2)]
    w2 = [kit.experts[:, b * E0_COLS + HID:b * E0_COLS + HID + HB * HID].rearrange("p (k n) -> p k n", n=HID) for b in range(2)]
    w3 = [kit.experts[:, (b + 1) * E0_COLS - HB * P:(b + 1) * E0_COLS].rearrange("p (k n) -> p k n", n=P) for b in range(2)]
    with Stage(kit, "e0") as st:
        landed = [st.sem("landed0"), st.sem("landed1")]
        hidden, gelu_done, weighted, expert_done = map(st.sem, ("hidden", "gelu", "weighted", "expert_done"))
        block = st.block()

        @block.sync
        def _(sp):
            for e in range(n_exp):
                if e >= 2:
                    sp.wait_ge(expert_done, e - 1)
                sp.dma_start(kit.experts[:, (e % 2) * E0_COLS:(e % 2 + 1) * E0_COLS], dram[e]).then_inc(landed[e % 2], 16)

        @block.tensor
        def _(pe):
            group = [0]

            def hidden_group(operands):
                g = group[0]
                if g >= 4:
                    pe.wait_ge(gelu_done, g - 3)
                for n, (lhs, rhs) in enumerate(operands):
                    last = nc.tensor.matmul(kit.bank(g % 4), lhs, rhs, start=n == 0, stop=n == len(operands) - 1)
                last.then_inc(hidden, 1)
                group[0] = g + 1

            def first(i):
                e, c = steps[i]
                if c == 0:
                    pe.wait_ge(landed[e % 2], 16 * (e // 2 + 1))
                for m in range(HB):
                    hidden_group([(w1[e % 2][:, m * P:(m + 1) * P], kit.chunk(xn, c))])

            def second(i):
                e, c = steps[i]
                pe.wait_ge(gelu_done, 8 * i if i else 4)
                for m in range(HB):
                    hidden_group([(w2[e % 2][:, k, m * P:(m + 1) * P], kit.chunk(h1[i % 2], k)) for k in range(HB)])

            def third(i):
                e, c = steps[i]
                pe.wait_ge(weighted, i + 1)
                if e == 0:
                    nc.tensor.matmul(kit.bank(4 + c), kit.w("e_b3"), kit.chunk(rows, c)[0:n_exp], start=True, stop=False)
                for k in range(HB):
                    last = nc.tensor.matmul(kit.bank(4 + c), w3[e % 2][:, k, :], kit.chunk(h2[i % 2], k), start=False,
                                            stop=e == n_exp - 1 and k == HB - 1)
                if c == NC - 1:
                    last.then_inc(expert_done, 1)

            for i in range(len(steps) + 2):
                if i < len(steps):
                    first(i)
                if 1 <= i <= len(steps):
                    second(i - 1)
                if i >= 2:
                    third(i - 2)

        @block.scalar
        def _(act):
            group = [0]

            def gelu(out, bias):
                g = group[0]
                act.wait_ge(hidden, g + 1)
                nc.scalar.activation(out, kit.bank(g % 4), ACT.Gelu, bias=bias).then_inc(gelu_done, 1)
                group[0] = g + 1

            for i in range(len(steps) + 1):
                if i < len(steps):
                    e, c = steps[i]
                    for m in range(HB):
                        gelu(kit.chunk(h1[i % 2], m), kit.w("e_b1")[:, HB * e + m:HB * e + m + 1])
                if i >= 1:
                    e, c = steps[i - 1]
                    for m in range(HB):
                        gelu(kit.chunk(h2[(i - 1) % 2], m), kit.w("e_b2")[:, HB * e + m:HB * e + m + 1])

        @block.vector
        def _(dve):
            for i, (e, c) in enumerate(steps):
                dve.wait_ge(gelu_done, min(8 * (i + 1) + 4, 8 * len(steps)))
                h = kit.slot(h2[i % 2]).rearrange("p (m t) -> p m t", t=CH)
                nc.vector.tensor_tensor(h, h, kit.chunk(weights[e], c).unsqueeze(1).broadcast_to([P, HB, CH]),
                                        ALU.mult).then_inc(weighted, 1)



PIECES_Q = (0, 0, 1, 1, 0, 2)
PIECES_K = (0, 1, 0, 1, 2, 0)
PAIR_ROWS = 8 * len(PIECES_Q)
FULL_ROWS = PAIR_ROWS + 3
PAIRS = HEADS // 2
KT = SEQ // P
LAG = 2


def flat_slots(kit, i, n):
    return kit.slots[:, i:i + n, :].rearrange("p a b -> p (a b)")


def attention(kit, name, xn, weights, out, q_stack, k_stack, values, work):
    nc = kit.nc
    wq, wk, wv, bq, bk = weights
    q, k = work, work + 1
    project(kit, name + "_qk", [(q, wq, xn, bq), (k, wk, xn, bk)])

    qs = flat_slots(kit, q_stack, 4).bitcast(BF16).rearrange("p (b h t) -> p b h t", b=BATCH, h=PAIRS)
    ks = flat_slots(kit, k_stack, 4).bitcast(BF16).rearrange("p (b h t) -> p b h t", b=BATCH, h=PAIRS)
    v = flat_slots(kit, values, 2).rearrange("p (j h n) -> p j h n", h=HEADS, n=2 * DH)
    split = kit.experts[:, :].bitcast(BF16).rearrange("p (w s t) -> p w s t", w=2, s=3)

    with Stage(kit, name + "_prep") as st:
        tile_ready, ones_set, v_ready = map(st.sem, ("tile", "ones_set", "v"))
        high, mid, rest = map(st.sem, ("high", "mid", "rest"))
        block = st.block()

        @block.tensor
        def _(pe):
            for j in range(NT):
                nc.tensor.matmul(kit.bank(j // 4)[:, (j % 4) * P:(j % 4 + 1) * P], kit.slot(xn)[:, j * P:(j + 1) * P],
                                 kit.w(wv), start=True, stop=True).then_inc(tile_ready, 1)

        @block.scalar
        def _(act):
            for w, src in enumerate((q, k)):
                nc.scalar.activation(split[:, w, 0], kit.slot(src), ACT.Copy).then_inc(high, 1)
            for w, src in enumerate((q, k)):
                act.wait_ge(rest, w + 1)
                nc.scalar.activation(split[:, w, 1], kit.slot(src), ACT.Copy).then_inc(mid, 1)
            act.wait_ge(ones_set, 3)
            for g in range(4):
                act.wait_ge(tile_ready, 4 * g + 4)
                nc.scalar.activation(v[:, 4 * g:4 * g + 4, :, 0:DH], kit.bank(g).rearrange("p (j h n) -> p j h n", j=4, n=DH),
                                     ACT.Copy).then_inc(v_ready, 1)

        @block.vector
        def _(dve):
            for w, src in enumerate((q, k)):
                dve.wait_ge(high, w + 1)
                nc.vector.tensor_tensor(kit.slot(src), kit.slot(src), split[:, w, 0], ALU.subtract).then_inc(rest, 1)
            for w, src in enumerate((q, k)):
                dve.wait_ge(mid, w + 1)
                nc.vector.tensor_tensor(split[:, w, 2], kit.slot(src), split[:, w, 1], ALU.subtract)

        @block.gpsimd
        def _(pool):
            nc.gpsimd.memset(v, 1.0).then_inc(ones_set, 1)
            pool.wait_ge(ones_set, 1)
            nc.gpsimd.memset(ks[32:64], 1.0).then_inc(ones_set, 1)
            nc.gpsimd.memset(ks[96:128], 1.0).then_inc(ones_set, 1)

    scale = 1.0 / float(np.sqrt(np.float32(DH)))
    heads = [(b, h) for b in range(BATCH) for h in range(HEADS)]
    n_heads = len(heads)
    n_tiles = KT * n_heads
    QUAD = 4
    QUAD_TILES = QUAD * KT
    n_quads = n_heads // QUAD
    AHEAD = QUAD_TILES + KT
    RING = 2 * QUAD
    probs = flat_slots(kit, work, 4).rearrange("p (r t) -> p r t", t=SEQ)
    evac = kit.experts[:, 0:TOK].rearrange("p (r t) -> p r t", t=SEQ)
    den = kit.experts[:, TOK:2 * TOK]
    half_max = kit.scratch[:, 0:4 * KT].rearrange("p (r n c) -> p r n c", n=KT, c=2)
    neg_max = kit.scratch[:, 32:32 + 2 * KT].rearrange("p (r n) -> p r n", n=KT)
    tail = kit.scratch[:, P:]
    turned = tail[0:KT, 0:2 * P].rearrange("p (r n) -> p r n", n=P)
    turned_rest = tail[0:KT, 256:256 + 2 * P].rearrange("p (r n) -> p r n", n=P)
    max_parts = tail[:, 512:896].bitcast(BF16)[0:KT].rearrange("p (r s n) -> p r s n", r=2, n=P)
    with Stage(kit, name) as st:
        stacked = [st.sem(f"stacked{h}") for h in range(HEADS)]
        scores_a, maxed, combined, max_turned, max_copied = map(st.sem, ("scores_a", "maxed", "combined", "max_turned", "max_copied"))
        max_split, max_placed = st.sem("max_split"), [st.sem(f"placed{j}") for j in range(QUAD)]
        scores_b, exped, summed, evacuated, own = map(st.sem, ("scores_b", "exped", "summed", "evacuated", "own"))
        stored = [st.sem("stored0"), st.sem("stored1")]
        block = st.block()
        banks_b = [kit.psum[:, 2 + 2 * r:4 + 2 * r, :].rearrange("p a b -> p (a b)") for r in range(2)]

        def rows(h, n):
            return slice(64 * (h % 2), 64 * (h % 2) + n)

        def tile_b(u):
            return u // QUAD_TILES * QUAD + u % QUAD, u % QUAD_TILES // QUAD

        def weigh(pe, g):
            pe.wait_ge(exped, QUAD * (g + 1))
            i, t = tile_b(QUAD * g)
            if t == 0 and i > 0:
                pe.wait_ge(evacuated, i // QUAD)
            for c in range(2):
                for j in range(QUAD):
                    b, h = heads[i + j]
                    last = nc.tensor.matmul(kit.bank(6 + c)[32 * j:32 * j + 32], v[:, KT * b + t, h // 2 * 2:h // 2 * 2 + 2, :],
                                            probs[:, (QUAD * g + j) % RING, c * CH:(c + 1) * CH], start=t == 0, stop=t == KT - 1)
            last.then_inc(summed, 1)

        def take(act, quad):
            act.wait_ge(summed, KT * (quad + 1))
            if quad >= 2:
                act.wait_ge(stored[quad % 2], 16 * 2 * QUAD * (quad // 2))
            if quad == 0:
                for h in range(HEADS):
                    act.wait_ge(stacked[h], 16 * 2 * len(PIECES_Q))
            nc.scalar.activation(evac[:, quad % 2, :], kit.psum[:, 6:8, :].rearrange("p a b -> p (a b)"), ACT.Copy).then_inc(evacuated, 1)

        @block.tensor
        def _(pe):
            for n in range(n_tiles + AHEAD):
                i = n // KT
                if n % KT == 1 and 1 <= i <= n_heads:
                    pe.wait_ge(combined, i)
                    pe.wait_ge(maxed, min(2 * n - 1, 2 * n_tiles))
                    nc.tensor.transpose(kit.bank(0)[0:KT, 0:P], neg_max[:, (i - 1) % 2, :], kit.c("ident")).then_inc(max_turned, 1)
                if n >= AHEAD:
                    u = n - AHEAD
                    i_b, t = tile_b(u)
                    b, h = heads[i_b]
                    if t == 0:
                        pe.wait_ge(max_placed[i_b % QUAD], 16 * 3 * (i_b // QUAD + 1))
                    if u >= 2:
                        pe.wait_ge(exped, u - 1)
                    for c in range(2):
                        last = nc.tensor.matmul(banks_b[u % 2][:, c * CH:(c + 1) * CH], ks[rows(h, FULL_ROWS), b, h // 2, t * P:(t + 1) * P],
                                                qs[rows(h, FULL_ROWS), b, h // 2, c * CH:(c + 1) * CH], start=True, stop=True)
                    last.then_inc(scores_b, 1)
                    if u % QUAD == 1 and u >= QUAD:
                        weigh(pe, u // QUAD - 1)
                if n < n_tiles:
                    b, h = heads[i]
                    t = n % KT
                    if b == 0 and t == 0:
                        pe.wait_ge(stacked[h], 16 * 2 * len(PIECES_Q))
                    for c in range(2):
                        if n >= 1:
                            pe.wait_ge(maxed, 2 * n + c - 1)
                        if t == 1 and c == 0 and i >= 1:
                            pe.wait_ge(max_copied, i)
                        nc.tensor.matmul(kit.bank(c), qs[rows(h, PAIR_ROWS), b, h // 2, t * P:(t + 1) * P],
                                         ks[rows(h, PAIR_ROWS), b, h // 2, c * CH:(c + 1) * CH], start=True, stop=True).then_inc(scores_a, 1)
            weigh(pe, n_tiles // QUAD - 1)

        def place_maxima(dve, i):
            dve.wait_ge(max_turned, i + 1)
            if i >= 2:
                dve.wait_ge(max_placed[(i - 2) % QUAD], 16 * 3 * ((i - 2) // QUAD + 1))
            nc.vector.tensor_copy(turned[:, i % 2], kit.bank(0)[0:KT, 0:P]).then_inc(max_copied, 1)
            dve.wait_ge(max_copied, i + 1)
            nc.vector.tensor_copy(max_parts[:, i % 2, 0], turned[:, i % 2]).then_inc(own, 1)
            dve.wait_ge(own, 3 * i + 1)
            nc.vector.tensor_tensor(turned_rest[:, i % 2], turned[:, i % 2], max_parts[:, i % 2, 0], ALU.subtract).then_inc(own, 1)
            dve.wait_ge(own, 3 * i + 2)
            nc.vector.tensor_copy(max_parts[:, i % 2, 1], turned_rest[:, i % 2]).then_inc(own, 1)
            dve.wait_ge(own, 3 * i + 3)
            nc.vector.tensor_tensor(max_parts[:, i % 2, 2], turned_rest[:, i % 2], max_parts[:, i % 2, 1],
                                    ALU.subtract).then_inc(max_split, 1)

        @block.vector
        def _(dve):
            for i in range(n_heads):
                for t in range(KT):
                    if t == 1 and i >= 1:
                        place_maxima(dve, i - 1)
                    for c in range(2):
                        dve.wait_ge(scores_a, 2 * (KT * i + t) + c + 1)
                        nc.vector.tensor_reduce(half_max[:, i % 2, t, c:c + 1], kit.bank(c), AX.X, ALU.max, negate=True).then_inc(maxed, 1)
                dve.wait_ge(maxed, 2 * KT * (i + 1))
                if i >= 2:
                    dve.wait_ge(max_turned, i - 1)
                nc.vector.tensor_tensor(neg_max[:, i % 2].unsqueeze(2), half_max[:, i % 2, :, 0:1], half_max[:, i % 2, :, 1:2], ALU.min).then_inc(combined, 1)
            place_maxima(dve, n_heads - 1)

        @block.sync
        def _(sp):
            def stack(h):
                for w, (dst, pieces) in enumerate(((qs, PIECES_Q), (ks, PIECES_K))):
                    for piece, part in enumerate(pieces):
                        row = 64 * (h % 2) + DH * piece
                        sp.dma_start(dst[row:row + DH, :, h // 2, :],
                                     split[DH * h:DH * h + DH, w, part].rearrange("p (b t) -> p b t", b=BATCH)).then_inc(stacked[h], 16)

            def store(quad):
                sp.wait_ge(evacuated, quad + 1)
                for j in range(QUAD):
                    b, h = heads[QUAD * quad + j]
                    row = 32 * j + 16 * (h % 2)
                    for dst, r in ((kit.slot(out), row), (den, row + DH)):
                        sp.dma_start(dst[DH * h:DH * h + DH, b * SEQ:(b + 1) * SEQ], evac[r:r + DH, quad % 2]).then_inc(stored[quad % 2], 16)

            for h in range(QUAD):
                stack(h)
            for i in range(n_heads):
                for h in range(QUAD + 2 * i, min(QUAD + 2 * i + 2, HEADS)):
                    stack(h)
                b, h = heads[i]
                sp.wait_ge(max_split, i + 1)
                for s in range(3):
                    row = 64 * (h % 2) + PAIR_ROWS + s
                    sp.dma_start(qs[row:row + 1, b, h // 2, :].rearrange("p (n t) -> p n t", n=KT),
                                 max_parts[:, i % 2, s]).then_inc(max_placed[i % QUAD], 16)
                if i >= 10 and i % QUAD == 2:
                    store((i - 10) // QUAD)
            for quad in range((n_heads - 11) // QUAD + 1, n_quads):
                store(quad)
            for r in range(2):
                sp.wait_ge(stored[r], 16 * 2 * QUAD * (n_quads // 2))

        @block.scalar
        def _(act):
            for u in range(n_tiles):
                act.wait_ge(scores_b, u + 1)
                if u >= RING:
                    act.wait_ge(summed, (u - RING) // QUAD + 1)
                nc.scalar.activation(probs[:, u % RING, :], banks_b[u % 2], ACT.Exp, scale=scale).then_inc(exped, 1)
                if u % QUAD_TILES == 3 and u >= QUAD_TILES:
                    take(act, u // QUAD_TILES - 1)
            take(act, n_quads - 1)

    with Stage(kit, name + "_norm") as st:
        own = st.sem("own")
        block = st.block()

        @block.vector
        def _(dve):
            for c in range(NC):
                inv = den[:, c * CH:(c + 1) * CH]
                nc.vector.reciprocal(inv, inv).then_inc(own, 1)
                dve.wait_ge(own, c + 1)
                nc.vector.tensor_tensor(kit.chunk(out, c), kit.chunk(out, c), inv, ALU.mult)


def add(kit, name, dst, a, b, bias=None):
    nc = kit.nc
    with Stage(kit, name) as st:
        block = st.block()

        @block.vector
        def _(dve):
            nc.vector.scalar_tensor_tensor(kit.slot(dst), kit.slot(a), kit.w(bias) if bias else 0.0, kit.slot(b), ALU.add, ALU.add)



E1_HID = 256
E1_COLS = 3 * E1_HID


def experts_swiglu(kit, name, dram, xn, weights, blocks, cols, up, gate, down, gates, acts):
    nc = kit.nc
    steps = [(m, c) for m in range(blocks) for c in range(NC)]
    with Stage(kit, name) as st:
        landed, product, silu_done, gated, weighted = map(st.sem, ("landed", "product", "silu", "gated", "weighted"))
        block = st.block()

        def weight(a):
            return kit.experts[:, a:a + P]

        @block.sync
        def _(sp):
            sp.dma_start(kit.experts[:, 0:cols], dram).then_inc(landed, 16)

        @block.tensor
        def _(pe):
            pe.wait_ge(landed, 16)
            for i in range(len(steps) + 2):
                if i < len(steps):
                    m, c = steps[i]
                    if i >= 2:
                        pe.wait_ge(gated, i - 1)
                    nc.tensor.matmul(kit.bank(2 * (i % 2)), weight(gate(m)), kit.chunk(xn, c), start=True, stop=True)
                    nc.tensor.matmul(kit.bank(2 * (i % 2) + 1), weight(up(m)), kit.chunk(xn, c), start=True,
                                     stop=True).then_inc(product, 1)
                if i >= 2:
                    m, c = steps[i - 2]
                    if weights(m) is None:
                        pe.wait_ge(gated, i - 1)
                    else:
                        pe.wait_ge(weighted, i - 1)
                    nc.tensor.matmul(kit.bank(4 + c), weight(down(m)), kit.chunk(acts, (i - 2) % 4), start=m == 0,
                                     stop=m == blocks - 1)

        @block.scalar
        def _(act):
            for i, (m, c) in enumerate(steps):
                act.wait_ge(product, i + 1)
                if i >= 4:
                    act.wait_ge(gated, i - 2)
                nc.scalar.activation(kit.chunk(gates, i % 4), kit.bank(2 * (i % 2)), ACT.Silu).then_inc(silu_done, 1)

        @block.vector
        def _(dve):
            for i, (m, c) in enumerate(steps):
                dve.wait_ge(silu_done, i + 1)
                w = weights(m)
                nc.vector.tensor_tensor(kit.chunk(gates, i % 4) if w is not None else kit.chunk(acts, i % 4), kit.chunk(gates, i % 4),
                                        kit.bank(2 * (i % 2) + 1), ALU.mult).then_inc(gated, 1)
                if w is not None:
                    dve.wait_ge(gated, i + 1)
                    nc.vector.tensor_tensor(kit.chunk(acts, i % 4), kit.chunk(gates, i % 4), kit.chunk(w, c), ALU.mult).then_inc(weighted, 1)



def norm_attention(kit, name, xn, out, square, scaled, q, tq, values, probs, turned, result):
    nc = kit.nc
    norm, inv, row_scale = (kit.scratch[:, a:a + NT] for a in (0, 16, 32))
    neg_max, row_sum, inv_sum = (kit.scratch[:, a:a + NT] for a in (48, 64, 80))
    diag = kit.slot(square).rearrange("p (j q) -> p j q", q=P)
    with Stage(kit, name + "_rows") as st:
        squared, sum_ready, norm_ready, diag_ready, bcast_ready, own = map(st.sem, ("squared", "sum", "norm", "diag", "bcast", "own"))
        block = st.block()

        @block.tensor
        def _(pe):
            for j in range(NT):
                pe.wait_ge(squared, j // 4 + 1)
                last = nc.tensor.matmul(kit.psum[:, 4, j:j + 1], kit.slot(square)[:, j * P:(j + 1) * P],
                                        kit.c("ones")[:, 0:1], start=True, stop=True)
            last.then_inc(sum_ready, 1)
            pe.wait_ge(diag_ready, 1)
            for c in range(NC):
                nc.tensor.matmul(kit.bank(c), kit.c("ones"), kit.chunk(square, c), start=True, stop=True).then_inc(bcast_ready, 1)

        @block.scalar
        def _(act):
            for c in range(NC):
                nc.scalar.activation(kit.chunk(square, c), kit.chunk(xn, c), ACT.Square).then_inc(squared, 1)
            act.wait_ge(sum_ready, 1)
            nc.scalar.activation(norm, kit.psum[:, 4, 0:NT], ACT.Sqrt).then_inc(norm_ready, 1)

        @block.vector
        def _(dve):
            dve.wait_ge(norm_ready, 1)
            nc.vector.tensor_scalar(inv, norm, 1e-9, None, ALU.add).then_inc(own, 1)
            dve.wait_ge(own, 1)
            nc.vector.reciprocal(inv, inv).then_inc(own, 1)
            dve.wait_ge(own, 2)
            nc.vector.tensor_tensor(diag, kit.c("ident").unsqueeze(1).broadcast_to([P, NT, P]), spread(inv, P),
                                    ALU.mult).then_inc(diag_ready, 1)
            for c in range(NC):
                dve.wait_ge(bcast_ready, c + 1)
                nc.vector.tensor_tensor(kit.chunk(scaled, c), kit.chunk(xn, c), kit.bank(c), ALU.mult)

    project(kit, name + "_q", [(q, "q2", scaled, "bq2")])
    project(kit, name + "_tq", [(tq, "anomaly", q, None)])
    scale = 1.0 / float(np.sqrt(np.float32(P)))
    v = kit.slot(values).rearrange("p (j n) -> p j n", n=P)
    p_ring = kit.slot(probs).rearrange("p (r t) -> p r t", t=SEQ)
    pt_ring = kit.slot(turned).rearrange("p (r t) -> p r t", t=SEQ)
    res = kit.slot(result).rearrange("p (j n) -> p j n", n=P)
    with Stage(kit, name + "_v") as st:
        v_ready = st.sem("v")
        block = st.block()

        @block.tensor
        def _(pe):
            for j in range(NT):
                nc.tensor.matmul(kit.bank(j // 4)[:, (j % 4) * P:(j % 4 + 1) * P], kit.slot(scaled)[:, j * P:(j + 1) * P],
                                 kit.w("v2"), start=True, stop=True).then_inc(v_ready, 1)

        @block.vector
        def _(dve):
            for g in range(4):
                dve.wait_ge(v_ready, 4 * g + 4)
                nc.vector.tensor_tensor(v[:, 4 * g:4 * g + 4, :], kit.bank(g).rearrange("p (j n) -> p j n", n=P),
                                        kit.w("bv2").unsqueeze(1).broadcast_to([P, 4, P]), ALU.add)

    with Stage(kit, name) as st:
        scores, maxed, bias_ready, exped, p_turned = map(st.sem, ("scores", "maxed", "bias", "exped", "p_turned"))
        pt_copied, ctx_ready, ctx_scaled, ctx_turned, copied, own = map(st.sem, ("pt", "ctx", "ctx_scaled", "ctx_turned", "copied", "own"))
        block = st.block()

        @block.tensor
        def _(pe):
            for i in range(NT + 3):
                if i < NT:
                    if i >= 2:
                        pe.wait_ge(exped, i - 1)
                    a = i // KT * SEQ
                    for c in range(2):
                        last = nc.tensor.matmul(kit.bank(2 * (i % 2) + c), kit.slot(q)[:, i * P:(i + 1) * P],
                                                kit.slot(tq)[:, a + c * CH:a + (c + 1) * CH], start=True, stop=True)
                    last.then_inc(scores, 1)
                if 1 <= i <= NT:
                    t = i - 1
                    pe.wait_ge(exped, t + 1)
                    if t >= 1:
                        pe.wait_ge(pt_copied, t)
                    for n in range(KT):
                        last = nc.tensor.transpose(kit.bank(4 + n // 4)[:, (n % 4) * P:(n % 4 + 1) * P],
                                                   p_ring[:, t % 2, n * P:(n + 1) * P], kit.c("ident"))
                    last.then_inc(p_turned, 1)
                if 2 <= i <= NT + 1:
                    t = i - 2
                    pe.wait_ge(pt_copied, t + 1)
                    if t >= 1:
                        pe.wait_ge(ctx_scaled, t)
                    for n in range(KT):
                        last = nc.tensor.matmul(kit.bank(6)[:, 0:P], pt_ring[:, t % 2, n * P:(n + 1) * P],
                                                v[:, t // KT * KT + n, :], start=n == 0, stop=n == KT - 1)
                    last.then_inc(ctx_ready, 1)
                if i >= 3:
                    t = i - 3
                    pe.wait_ge(ctx_scaled, t + 1)
                    if t >= 1:
                        pe.wait_ge(copied, t)
                    nc.tensor.transpose(kit.bank(7)[:, 0:P], res[:, t, :], kit.c("ident")).then_inc(ctx_turned, 1)

        @block.scalar
        def _(act):
            for i in range(NT + 3):
                if i < NT:
                    act.wait_ge(bias_ready, i + 1)
                    if i >= 2:
                        act.wait_ge(p_turned, i - 1)
                    nc.scalar.activation(p_ring[:, i % 2, :], kit.psum[:, 2 * (i % 2):2 * (i % 2) + 2, :].rearrange("p a b -> p (a b)"),
                                         ACT.Exp, bias=neg_max[:, i:i + 1], scale=scale, accum_out=row_sum[:, i:i + 1]).then_inc(exped, 1)
                if i >= 3:
                    t = i - 3
                    act.wait_ge(ctx_turned, t + 1)
                    nc.scalar.activation(kit.slot(out)[:, t * P:(t + 1) * P], kit.bank(7)[:, 0:P], ACT.Copy).then_inc(copied, 1)

        @block.vector
        def _(dve):
            for i in range(NT + 2):
                if i < NT:
                    dve.wait_ge(scores, i + 1)
                    nc.vector.tensor_reduce(neg_max[:, i:i + 1], kit.psum[:, 2 * (i % 2):2 * (i % 2) + 2, :].rearrange("p a b -> p (a b)"),
                                            AX.X, ALU.max, negate=True).then_inc(maxed, 1)
                    dve.wait_ge(maxed, i + 1)
                    nc.vector.tensor_scalar(neg_max[:, i:i + 1], neg_max[:, i:i + 1], scale, None, ALU.mult).then_inc(bias_ready, 1)
                if 1 <= i <= NT:
                    t = i - 1
                    dve.wait_ge(p_turned, t + 1)
                    if t >= 2:
                        dve.wait_ge(ctx_ready, t - 1)
                    nc.vector.tensor_copy(pt_ring[:, t % 2, :], kit.psum[:, 4:6, :].rearrange("p a b -> p (a b)")).then_inc(pt_copied, 1)
                if i >= 2:
                    t = i - 2
                    dve.wait_ge(ctx_ready, t + 1)
                    dve.wait_ge(exped, t + 1)
                    nc.vector.reciprocal(inv_sum[:, t:t + 1], row_sum[:, t:t + 1]).then_inc(own, 1)
                    dve.wait_ge(own, t + 1)
                    nc.vector.tensor_scalar(res[:, t, :], kit.bank(6)[:, 0:P], inv_sum[:, t:t + 1], norm[:, t:t + 1],
                                            ALU.mult, ALU.mult).then_inc(ctx_scaled, 1)



def wkv_inputs(kit, name, xn, xx, r, kk, v_in, g, w, v, mix, t0, t1):
    nc = kit.nc
    mixes = flat_slots(kit, mix, 5)
    with Stage(kit, name + "_mix") as st:
        own, mix_ready, tanh_ready = map(st.sem, ("own", "mix", "tanh"))
        m_ready, m_used = st.sem("m"), st.sem("m_used")
        block = st.block()
        targets = (w, kk, v_in, r, g)

        @block.vector
        def _(dve):
            for b in range(BATCH):
                a, z = b * SEQ, (b + 1) * SEQ
                nc.vector.tensor_tensor(kit.slot(xx)[:, a + 1:z], kit.slot(xn)[:, a:z - 1], kit.slot(xn)[:, a + 1:z], ALU.subtract)
                nc.vector.tensor_scalar(kit.slot(xx)[:, a:a + 1], kit.slot(xn)[:, a:a + 1], -1.0, None, ALU.mult).then_inc(own, 1)
            dve.wait_ge(own, 2)
            nc.vector.scalar_tensor_tensor(kit.slot(t0), kit.slot(xx), kit.w("maa_x"), kit.slot(xn), ALU.mult, ALU.add).then_inc(own, 1)
            for n in range(5 * NC):
                s, c = n // NC, n % NC
                dve.wait_ge(m_ready, n + 1)
                nc.vector.scalar_tensor_tensor(kit.chunk(targets[s], c), kit.bank(4 + n % 4), kit.w("maa")[:, s:s + 1], kit.chunk(xx, c),
                                               ALU.add, ALU.mult).then_inc(m_used, 1)
                dve.wait_ge(m_used, n + 1)
                nc.vector.tensor_tensor(kit.chunk(targets[s], c), kit.chunk(targets[s], c), kit.chunk(xn, c), ALU.add)

        @block.tensor
        def _(pe):
            pe.wait_ge(own, 3)
            for n in range(5 * NC + 4):
                if n < 5 * NC:
                    s, c = n // NC, n % NC
                    if n >= 4:
                        pe.wait_ge(tanh_ready, n - 3)
                    nc.tensor.matmul(kit.bank(n % 4)[0:32], kit.w("maa_w1")[:, 32 * s:32 * s + 32], kit.chunk(t0, c),
                                     start=True, stop=True).then_inc(mix_ready, 1)
                if n >= 4:
                    k = n - 4
                    s, c = k // NC, k % NC
                    pe.wait_ge(tanh_ready, k + 1)
                    if k >= 4:
                        pe.wait_ge(m_used, k - 3)
                    nc.tensor.matmul(kit.bank(4 + k % 4), kit.w("maa_w2")[:, P * s:P * s + P],
                                     mixes[0:32, k * CH:(k + 1) * CH], start=True, stop=True).then_inc(m_ready, 1)

        @block.scalar
        def _(act):
            for n in range(5 * NC):
                act.wait_ge(mix_ready, n + 1)
                nc.scalar.activation(mixes[0:32, n * CH:(n + 1) * CH], kit.bank(n % 4)[0:32], ACT.Tanh).then_inc(tanh_ready, 1)

    with Stage(kit, name + "_decay") as st:
        low, tanh_done, full, exp_done = map(st.sem, ("low", "tanh", "full", "exp"))
        block = st.block()

        @block.tensor
        def _(pe):
            for c in range(NC):
                nc.tensor.matmul(kit.bank(c)[0:64], kit.w("decay_w1"), kit.chunk(w, c), start=True, stop=True).then_inc(low, 1)
            for c in range(NC):
                pe.wait_ge(tanh_done, c + 1)
                nc.tensor.matmul(kit.bank(4 + c), kit.w("decay_w2"), kit.chunk(t1, c)[0:64], start=True, stop=True).then_inc(full, 1)

        @block.scalar
        def _(act):
            for c in range(NC):
                act.wait_ge(low, c + 1)
                nc.scalar.activation(kit.chunk(t1, c)[0:64], kit.bank(c)[0:64], ACT.Tanh).then_inc(tanh_done, 1)
            for c in range(NC):
                act.wait_ge(full, c + 1)
                nc.scalar.activation(kit.chunk(w, c), kit.bank(4 + c), ACT.Exp, bias=kit.w("decay")).then_inc(exp_done, 1)
                act.wait_ge(exp_done, 2 * c + 1)
                nc.scalar.activation(kit.chunk(w, c), kit.chunk(w, c), ACT.Exp, scale=-1.0).then_inc(exp_done, 1)

    project(kit, name + "_rkvg", [(r, "Wr", r, None), (kk, "Wk", kk, None), (v, "Wv", v_in, None), (g, "Wg", g, None)])


def wkv(kit, name, r, kk, v_in, v, w, y, rd, t0, t1, head_decay, tail_decay, key_even, key_odd, v_tok, states):
    nc = kit.nc

    def by_chunk(slot):
        return kit.slot(slot).rearrange("p (n t) -> p n t", t=WC)

    R, K, V, W_, Y, RD, T0, T1 = map(by_chunk, (r, kk, v, w, y, rd, t0, t1))
    PER = NWC // NC

    with Stage(kit, name + "_near") as st:
        pair, spread_ready, used, own = map(st.sem, ("pair", "spread", "used", "own"))
        e_free = st.sem("e_free")
        block = st.block()

        @block.vector
        def _(dve):
            done = [0]

            def then(instruction):
                done[0] += 1
                instruction.then_inc(own, 1)
                dve.wait_ge(own, done[0])

            def produce(d):
                T = (T0, T1)[d % 2]
                if d == 0:
                    nc.vector.scalar_tensor_tensor(T[:, :, :], R[:, :, :], kit.w("faaaa"), K[:, :, :], ALU.mult, ALU.mult).then_inc(pair, 1)
                    return
                if d == 1:
                    then(nc.vector.tensor_copy(RD[:, :, 1:], R[:, :, 1:]))
                else:
                    then(nc.vector.tensor_tensor(RD[:, :, d:], RD[:, :, d:], W_[:, :, 1:WC - d + 1], ALU.mult))
                nc.vector.tensor_tensor(T[:, :, d:], RD[:, :, d:], K[:, :, 0:WC - d], ALU.mult).then_inc(pair, 1)

            produce(0)
            for d in range(WC):
                dve.wait_ge(spread_ready, d + 1)
                if d + 1 < WC:
                    produce(d + 1)
                n = WC - d
                bank = kit.psum[:, 4 * (d % 2):4 * (d % 2) + 4, 0:PER * n].rearrange("p b (m t) -> p b m t", t=n)
                T = (T0, T1)[d % 2]
                Tv, Vv = (kit_slot.rearrange("p (b m) t -> p b m t", b=NC) for kit_slot in (T[:, :, d:], V[:, :, 0:n]))
                for b in range(NC):
                    last = nc.vector.tensor_tensor(Tv[:, b], bank[:, b], Vv[:, b], ALU.mult)
                last.then_inc(used, 1)
                dve.wait_ge(used, d + 1)
                if d == 0:
                    nc.vector.tensor_copy(kit.slot(y), kit.slot(t0))
                else:
                    nc.vector.tensor_tensor(Y[:, :, d:], Y[:, :, d:], T[:, :, d:], ALU.add)

        @block.tensor
        def _(pe):
            for d in range(WC):
                n = WC - d
                T = (T0, T1)[d % 2]
                pe.wait_ge(pair, d + 1)
                if d >= 2:
                    pe.wait_ge(used, d - 1)
                for c in range(NC):
                    last = nc.tensor.matmul(kit.bank(4 * (d % 2) + c)[:, 0:PER * n], kit.c("head_ones"),
                                            T[:, c * PER:(c + 1) * PER, d:], start=True, stop=True)
                last.then_inc(spread_ready, 1)

    HD, TD = by_chunk(head_decay), by_chunk(tail_decay)
    ke = kit.slot(key_even).rearrange("p (j n) -> p j n", n=P)
    ko = kit.slot(key_odd).rearrange("p (j n) -> p j n", n=P)
    vt = kit.slot(v_tok).rearrange("p (j n) -> p j n", n=P)
    whole = kit.scratch[:, 0:NWC]
    with Stage(kit, name + "_far") as st:
        own, turned, turned_used, v_ready, keys_ready = map(st.sem, ("own", "turned", "turned_used", "v", "keys"))
        block = st.block()

        @block.vector
        def _(dve):
            done = [0]

            def then(instruction):
                done[0] += 1
                instruction.then_inc(own, 1)
                dve.wait_ge(own, done[0])

            then(nc.vector.tensor_copy(T0[:, :, 1:], W_[:, :, 0:WC - 1]))
            then(nc.vector.memset(T0[:, :, 0:1], 0.0))
            starts = kit.c("start").unsqueeze(1).broadcast_to([P, NWC, WC])
            then(nc.vector.tensor_copy(T1[:, :, :], starts))
            then(nc.vector.tensor_tensor_scan(kit.slot(head_decay), kit.slot(t0), kit.slot(t1), 0.0, ALU.mult, ALU.add))
            nc.vector.tensor_tensor(whole.unsqueeze(2), HD[:, :, WC - 1:WC], W_[:, :, WC - 1:WC], ALU.mult)
            then(nc.vector.tensor_tensor(kit.slot(rd), kit.slot(r), kit.slot(head_decay), ALU.mult))
            then(nc.vector.tensor_copy(T0[:, :, 0:WC - 1], W_[:, :, 1:WC]))
            then(nc.vector.memset(T0[:, :, WC - 1:WC], 0.0))
            then(nc.vector.tensor_copy(T1[:, :, ::-1], starts))
            then(nc.vector.tensor_tensor_scan(kit.slot(tail_decay)[:, ::-1], kit.slot(t0)[:, ::-1], kit.slot(t1)[:, ::-1],
                                              0.0, ALU.mult, ALU.add))
            nc.vector.tensor_tensor(kit.slot(kk), kit.slot(kk), kit.slot(tail_decay), ALU.mult).then_inc(keys_ready, 1)
            for g in range(4):
                dve.wait_ge(turned, 4 * g + 4)
                bank = kit.bank(g).rearrange("p (j n) -> p j n", n=P)
                nc.vector.tensor_scalar(ke[:, 4 * g:4 * g + 4, :], bank, kit.c("even"), None, ALU.mult)
                nc.vector.tensor_scalar(ko[:, 4 * g:4 * g + 4, :], bank, kit.c("odd"), None, ALU.mult)

        @block.tensor
        def _(pe):
            for j in range(NT):
                nc.tensor.matmul(kit.bank(4 + j // 4)[:, (j % 4) * P:(j % 4 + 1) * P], kit.slot(v_in)[:, j * P:(j + 1) * P],
                                 kit.w("Wv"), start=True, stop=True).then_inc(v_ready, 1)
            pe.wait_ge(keys_ready, 1)
            for j in range(NT):
                nc.tensor.transpose(kit.bank(j // 4)[:, (j % 4) * P:(j % 4 + 1) * P], kit.slot(kk)[:, j * P:(j + 1) * P],
                                    kit.c("ident")).then_inc(turned, 1)

        @block.scalar
        def _(act):
            for g in range(4):
                act.wait_ge(v_ready, 4 * g + 4)
                nc.scalar.activation(vt[:, 4 * g:4 * g + 4, :], kit.bank(4 + g).rearrange("p (j n) -> p j n", n=P), ACT.Copy)

    state = flat_slots(kit, states, 4).rearrange("p (n i) -> p n i", i=WKV_HEAD)
    GROUP = 8
    with Stage(kit, name + "_state") as st:
        kv_ready, state_ready, first_state, state_own = map(st.sem, ("kv", "state", "first", "state_own"))
        block = st.block()

        def kv(j, n):
            return kit.bank(4 * (j % 2) + n // 2)[:, 64 * (n % 2):64 * (n % 2) + 64]

        @block.tensor
        def _(pe):
            for j in range(NT):
                if j >= 2:
                    pe.wait_ge(state_ready, j - 1)
                for n in range(GROUP):
                    rows = slice(32 * (n // 2), 32 * (n // 2) + 32)
                    keys = (ke, ko)[n % 2]
                    for h in range(2):
                        head = slice(64 * h, 64 * h + 64)
                        last = nc.tensor.matmul(kv(j, n)[head], keys[rows, j, head], vt[rows, j, head], start=True, stop=True)
                last.then_inc(kv_ready, 1)

        @block.vector
        def _(dve):
            own = 0
            for b in range(BATCH):
                nc.vector.memset(state[:, b * (NWC // 2), :], 0.0).then_inc(first_state, 1)
            dve.wait_ge(first_state, BATCH)
            for j in range(NT):
                dve.wait_ge(kv_ready, j + 1)
                final = GROUP - 2 if (j + 1) % KT == 0 else GROUP - 1
                for n in range(final + 1):
                    c = j * GROUP + n
                    update = nc.vector.scalar_tensor_tensor(state[:, c + 1, :], state[:, c, :], whole[:, c:c + 1],
                                                            kv(j, n), ALU.mult, ALU.add)
                    if n < final:
                        update.then_inc(state_own, 1)
                        own += 1
                        dve.wait_ge(state_own, own)
                    else:
                        update.then_inc(state_ready, 1)
                        dve.wait_ge(state_ready, j + 1)

    with Stage(kit, name + "_read") as st:
        y_ready = st.sem("y")
        block = st.block()

        @block.tensor
        def _(pe):
            for c in range(NC):
                for n in range(PER):
                    for h in range(2):
                        rows = slice(64 * h, 64 * h + 64)
                        last = nc.tensor.matmul(kit.bank(c)[rows, n * WC:n * WC + WC], state[rows, c * PER + n, :],
                                                kit.chunk(rd, c)[rows, n * WC:n * WC + WC], start=True, stop=True)
                last.then_inc(y_ready, 1)

        @block.vector
        def _(dve):
            for c in range(NC):
                dve.wait_ge(y_ready, c + 1)
                nc.vector.tensor_tensor(kit.chunk(y, c), kit.chunk(y, c), kit.bank(c), ALU.add)


def group_norm(kit, name, y, square, stat, g):
    nc = kit.nc
    with Stage(kit, name) as st:
        mean_ready, centered, squared, var_ready, std_ready, own = map(st.sem, ("mean", "centered", "squared", "var", "std", "own"))
        silu_done = st.sem("silu")
        block = st.block()

        @block.tensor
        def _(pe):
            for c in range(NC):
                nc.tensor.matmul(kit.bank(c), kit.c("head_mean"), kit.chunk(y, c), start=True, stop=True).then_inc(mean_ready, 1)
            for c in range(NC):
                pe.wait_ge(squared, c + 1)
                nc.tensor.matmul(kit.bank(4 + c), kit.c("head_mean"), kit.chunk(square, c), start=True, stop=True).then_inc(var_ready, 1)

        @block.scalar
        def _(act):
            for c in range(NC):
                act.wait_ge(centered, c + 1)
                nc.scalar.activation(kit.chunk(square, c), kit.chunk(y, c), ACT.Square).then_inc(squared, 1)
            for c in range(NC):
                act.wait_ge(var_ready, c + 1)
                nc.scalar.activation(kit.chunk(stat, c), kit.bank(4 + c), ACT.Sqrt, bias=kit.c("eps_wkv")).then_inc(std_ready, 1)
            for c in range(NC):
                nc.scalar.activation(kit.chunk(g, c), kit.chunk(g, c), ACT.Silu).then_inc(silu_done, 1)

        @block.vector
        def _(dve):
            done = [0]

            def then(instruction):
                done[0] += 1
                instruction.then_inc(own, 1)
                dve.wait_ge(own, done[0])

            for c in range(NC):
                dve.wait_ge(mean_ready, c + 1)
                nc.vector.tensor_tensor(kit.chunk(y, c), kit.chunk(y, c), kit.bank(c), ALU.subtract).then_inc(centered, 1)
            for c in range(NC):
                dve.wait_ge(std_ready, c + 1)
                then(nc.vector.reciprocal(kit.chunk(stat, c), kit.chunk(stat, c)))
                then(nc.vector.scalar_tensor_tensor(kit.chunk(y, c), kit.chunk(y, c), kit.w("ln_w"), kit.chunk(stat, c), ALU.mult, ALU.mult))
                dve.wait_ge(silu_done, c + 1)
                nc.vector.scalar_tensor_tensor(kit.chunk(y, c), kit.chunk(y, c), kit.w("ln_b"), kit.chunk(g, c), ALU.add, ALU.mult)



E3_COLS = HID + HB * P
E3_RING = 6


def experts_relu(kit, name, dram, xn, weights, rows, hidden_slots):
    nc = kit.nc
    n_exp = 8
    steps = [(e, c) for e in range(n_exp) for c in range(NC)]

    def w1(e, m):
        a = e % E3_RING * E3_COLS + m * P
        return kit.experts[:, a:a + P]

    def w2(e, k):
        return w1(e, HB + k)

    with Stage(kit, name) as st:
        landed = [st.sem(f"landed{r}") for r in range(E3_RING)]
        hidden, relu_done, weighted, expert_done = map(st.sem, ("hidden", "relu", "weighted", "expert_done"))
        block = st.block()

        @block.sync
        def _(sp):
            for e in range(n_exp):
                r = e % E3_RING
                if e >= E3_RING:
                    sp.wait_ge(expert_done, e - E3_RING + 1)
                sp.dma_start(kit.experts[:, r * E3_COLS:(r + 1) * E3_COLS], dram[e]).then_inc(landed[r], 16)

        @block.tensor
        def _(pe):
            for i in range(len(steps) + 1):
                if i < len(steps):
                    e, c = steps[i]
                    if c == 0:
                        pe.wait_ge(landed[e % E3_RING], 16 * (e // E3_RING + 1))
                    for m in range(HB):
                        if i >= 1:
                            pe.wait_ge(relu_done, HB * (i - 1) + m + 1)
                        nc.tensor.matmul(kit.bank(m), w1(e, m), kit.chunk(xn, c), start=True, stop=True).then_inc(hidden, 1)
                if i >= 1:
                    e, c = steps[i - 1]
                    pe.wait_ge(weighted, i)
                    if e == 0:
                        nc.tensor.matmul(kit.bank(4 + c), kit.w("f_b2"), kit.chunk(rows, c)[0:n_exp], start=True, stop=False)
                    for k in range(HB):
                        last = nc.tensor.matmul(kit.bank(4 + c), w2(e, k), kit.chunk(hidden_slots[(i - 1) % 2], k), start=False,
                                                stop=e == n_exp - 1 and k == HB - 1)
                    if c == NC - 1:
                        last.then_inc(expert_done, 1)

        @block.scalar
        def _(act):
            for i, (e, c) in enumerate(steps):
                for m in range(HB):
                    act.wait_ge(hidden, HB * i + m + 1)
                    nc.scalar.activation(kit.chunk(hidden_slots[i % 2], m), kit.bank(m), ACT.Relu,
                                         bias=kit.w("f_b1")[:, HB * e + m:HB * e + m + 1]).then_inc(relu_done, 1)

        @block.vector
        def _(dve):
            for i, (e, c) in enumerate(steps):
                dve.wait_ge(relu_done, HB * (i + 1))
                h = kit.slot(hidden_slots[i % 2]).rearrange("p (m t) -> p m t", t=CH)
                nc.vector.tensor_tensor(h, h, kit.chunk(weights[e], c).unsqueeze(1).broadcast_to([P, HB, CH]),
                                        ALU.mult).then_inc(weighted, 1)


def add_banks(kit, name, dst, a):
    nc = kit.nc
    with Stage(kit, name) as st:
        block = st.block()

        @block.vector
        def _(dve):
            nc.vector.tensor_tensor(kit.slot(dst), kit.slot(a), kit.psum[:, 4:8, :].rearrange("p a b -> p (a b)"), ALU.add)



X, XN, RES = 0, 1, 2
WEIGHTS = list(range(5, 13))


def layer0(kit, dram):
    layer_norm(kit, "n0", X, XN, 3, 4)
    selective_scan(kit, XN, RES, list(range(3, 13)))
    router(kit, "r0", XN, "tokens", None, 8, "half", rows=3, stacked=4, work=5, tmp=6)
    spread_rows(kit, "sp0", 4, range(8), WEIGHTS)
    experts_gelu(kit, dram, XN, WEIGHTS, 3, h1=[13, 14], h2=[15, 16])
    merge(kit, "m0", X, RES, 13)


def layer1(kit, dram):
    layer_norm(kit, "n1", X, XN, 3, 4)
    attention(kit, "a1", XN, ("q1", "k1", "v1", None, None), RES, q_stack=3, k_stack=7, values=11, work=13)
    project(kit, "o1", [(3, "o1", RES, None)])
    add(kit, "s1", RES, 3, XN)
    router(kit, "r1", XN, "gate1", None, 8, "scores", rows=3, stacked=4, work=5, tmp=6)
    spread_rows(kit, "sp1", 4, range(8), WEIGHTS)
    experts_swiglu(kit, "e1", dram, XN, lambda m: WEIGHTS[m // 2], 16, 8 * E1_COLS,
                   up=lambda m: m // 2 * E1_COLS + E1_HID + m % 2 * P, gate=lambda m: m // 2 * E1_COLS + m % 2 * P,
                   down=lambda m: m // 2 * E1_COLS + 2 * E1_HID + m % 2 * P, gates=13, acts=14)
    merge(kit, "m1", X, RES, 13)


def layer2(kit, dram):
    layer_norm(kit, "n2", X, XN, 3, 4)
    norm_attention(kit, "a2", XN, RES, 3, 4, 5, 6, 7, 8, 9, 10)
    router(kit, "r2", XN, "router", "router_bias", 16, "top", rows=3, stacked=4, work=5, tmp=6)
    spread_rows(kit, "sp2", 4, range(32, 40), WEIGHTS)
    experts_swiglu(kit, "e2", dram, XN, lambda m: WEIGHTS[m] if m < 8 else None, 9, 27 * P,
                   up=lambda m: (m if m < 8 else 25) * P, gate=lambda m: (8 + m if m < 8 else 24) * P,
                   down=lambda m: (16 + m if m < 8 else 26) * P, gates=13, acts=14)
    merge(kit, "m2", X, RES, 13)


def layer3(kit, dram):
    layer_norm(kit, "n3", X, XN, 3, 4)
    wkv_inputs(kit, "w3", XN, xx=2, r=3, kk=4, v_in=5, g=6, w=7, v=8, mix=9, t0=14, t1=15)
    wkv(kit, "w3", r=3, kk=4, v_in=5, v=8, w=7, y=9, rd=2, t0=10, t1=11, head_decay=12, tail_decay=13, key_even=14,
        key_odd=15, v_tok=16, states=10)
    group_norm(kit, "gn", 9, 3, 4, 6)
    project(kit, "o3", [(RES, "Wo", 9, None)])

    layer_norm(kit, "f1", XN, 3, 4, 5, "ln1_g", "ln1_b")
    attention(kit, "a3", 3, ("q3", "k3", "v3", "bq3", "bk3"), 3, q_stack=4, k_stack=8, values=12, work=14)
    add_bias(kit, "bv", 3, "bv3")
    project(kit, "fo", [(4, "o3", 3, None)])
    add(kit, "fx", 5, 4, XN, "bo3")
    layer_norm(kit, "f2", 5, 3, 6, 7, "ln2_g", "ln2_b")
    router(kit, "r3", 3, "gate3", "gate_b3", 8, "first", rows=6, stacked=7, work=8, tmp=9)
    spread_rows(kit, "sp3", 7, range(8), list(range(8, 16)))
    experts_relu(kit, "e3", dram, 3, list(range(8, 16)), 6, [16, 17])
    add_banks(kit, "fg", 4, 5)
    merge(kit, "m3", X, RES, 6, g=4)


def add_bias(kit, name, slot, bias):
    nc = kit.nc
    with Stage(kit, name) as st:
        block = st.block()

        @block.vector
        def _(dve):
            nc.vector.tensor_scalar(kit.slot(slot), kit.slot(slot), kit.w(bias), None, ALU.add)


def allocate(nc, ctx):
    def sb(name, shape, dt=F32):
        return ctx.enter_context(nc.sbuf_tensor(name, shape, dt))

    return Kit(nc, sb("slots", [P, SLOTS, TOK]), sb("small_sb", [P, SMALL.width]), sb("consts_sb", [P, CONSTS.width]),
               sb("experts", [P, EXPERT_COLS]), sb("sel_sb", [96, 40, P], BF16),
               ctx.enter_context(nc.psum_tensor("psum", [P, 8, CH], F32)), sb("scratch", [P, 1024]))


EXPERT_COLS = 6144


def recurrent_layers(nc, x, small, consts, sel, experts0, experts1, experts2, experts3, out):
    with ExitStack() as ctx:
        kit = allocate(nc, ctx)
        stored = ctx.enter_context(nc.semaphore("stored"))
        load_inputs(kit, x, small, consts, sel, X)
        layer0(kit, experts0)
        layer1(kit, experts1)
        layer2(kit, experts2)
        layer3(kit, experts3)
        store_output(kit, out, X, stored)



def rows128(a, p=128):
    out = np.zeros((128, a.shape[1]), a.dtype)
    out[:a.shape[0]] = a
    return out


def column(v):
    return np.reshape(v, (-1, 1))


def tiles(a):
    k = a.shape[0] // 128
    return np.reshape(np.transpose(np.reshape(a, (k, 128, a.shape[1])), (1, 0, 2)), (128, -1))


def small_weights(i):
    w = {
        "W_x": i["L0_attn_W_x"], "W_dt": i["L0_attn_W_dt"], "W_out": i["L0_attn_W_out"], "A_log": i["L0_attn_A_log"],
        "b_dt": column(i["L0_attn_b_dt"]), "D": column(i["L0_attn_D"]), "b_out": column(i["L0_attn_b_out"]),
        "tokens": i["L0_ffn_expert_tokens"].T,
        "e_b1": np.reshape(i["L0_ffn_b1"], (32, 128)).T, "e_b2": np.reshape(i["L0_ffn_b2"], (32, 128)).T,
        "e_b3": i["L0_ffn_b3"],
        "q1": i["L1_attn_Wq"], "k1": i["L1_attn_Wk"], "v1": i["L1_attn_Wv"], "o1": i["L1_attn_Wout"],
        "gate1": i["L1_ffn_gate_w"].T,
        "q2": i["L2_attn_Wq"].T, "v2": i["L2_attn_Wv"].T, "anomaly": i["L2_attn_anomaly_matrix"],
        "bq2": column(i["L2_attn_bq"]), "bv2": np.tile(i["L2_attn_bv"], (128, 1)),
        "router": i["L2_ffn_router_w"].T, "router_bias": np.tile(i["L2_ffn_router_bias"], (128, 1)),
        "maa_x": column(i["L3_attn_time_maa_x"]),
        "maa": np.stack([i[f"L3_attn_time_maa_{s}"] for s in "wkvrg"], 1),
        "maa_w1": i["L3_attn_time_maa_w1"],
        "maa_w2": np.reshape(np.transpose(i["L3_attn_time_maa_w2"], (1, 0, 2)), (32, 640)),
        "decay_w1": i["L3_attn_time_decay_w1"], "decay_w2": i["L3_attn_time_decay_w2"],
        "decay": column(i["L3_attn_time_decay"]), "faaaa": column(i["L3_attn_time_faaaa"]),
        "Wr": i["L3_attn_Wr"], "Wk": i["L3_attn_Wk"], "Wv": i["L3_attn_Wv"], "Wg": i["L3_attn_Wg"],
        "Wo": i["L3_attn_Wo"], "ln_w": column(i["L3_attn_ln_w"]), "ln_b": column(i["L3_attn_ln_b"]),
        "ln1_g": column(i["L3_ffn_ln1_g"]), "ln1_b": column(i["L3_ffn_ln1_b"]),
        "ln2_g": column(i["L3_ffn_ln2_g"]), "ln2_b": column(i["L3_ffn_ln2_b"]),
        "q3": i["L3_ffn_wq"], "k3": i["L3_ffn_wk"], "v3": i["L3_ffn_wv"], "o3": i["L3_ffn_wo"],
        "bq3": column(i["L3_ffn_bq"]), "bk3": column(i["L3_ffn_bk"]), "bv3": column(i["L3_ffn_bv"]),
        "bo3": column(i["L3_ffn_bo"]),
        "gate3": i["L3_ffn_gate_w"], "gate_b3": np.tile(i["L3_ffn_gate_b"], (128, 1)),
        "f_b1": np.reshape(i["L3_ffn_b1"], (32, 128)).T, "f_b2": i["L3_ffn_b2"],
    }
    return np.concatenate([rows128(w[name]) for name in SMALL.at], 1)


def constants():
    p = np.arange(128)
    head = (p[:, None] // WKV_HEAD == p[None, :] // WKV_HEAD).astype(np.float32)
    one = np.ones((128, 128), np.float32)
    c = {
        "ident": np.eye(128), "ones": one, "mean": one / 128, "head_ones": head, "head_mean": head / WKV_HEAD,
        "iota": np.tile(np.arange(16), (128, 1)), "even": column(p // WC % 2 == 0), "odd": column(p // WC % 2 == 1),
        "eps_1e5": one[:, :1] * 1e-5, "eps_scan": one[:, :1] * 1e-12, "eps_wkv": one[:, :1] * (1e-5 * 64),
        "start": np.tile(np.arange(16) == 0, (128, 1)), "zero": one[:, :1] * 0,
    }
    return np.concatenate([c[name].astype(np.float32) for name in CONSTS.at], 1)


def selectors():
    s = np.zeros((96, 40, 128), np.float32)
    for part in range(3):
        for e in range(32):
            s[32 * part + e, e, :] = 1
        for i in range(8):
            s[32 * part + 2 * i, 32 + i, :64] = 1
            s[32 * part + 2 * i + 1, 32 + i, 64:] = 1
    return np.reshape(s, (96, 40 * 128))


def expert_weights0(i):
    return np.stack([np.concatenate([i["L0_ffn_W1"][e], tiles(i["L0_ffn_W2"][e]), tiles(i["L0_ffn_W3"][e])], 1)
                     for e in range(8)])


def expert_weights1(i):
    return np.concatenate([np.concatenate([i["L1_ffn_w1"][e], i["L1_ffn_w3"][e], tiles(i["L1_ffn_w2"][e])], 1)
                           for e in range(8)], 1)


def expert_weights2(i):
    pairs = [np.concatenate([np.concatenate([i[f"L2_ffn_{n}_proj"][2 * m], i[f"L2_ffn_{n}_proj"][2 * m + 1]], 1)
                             for m in range(8)], 1) for n in ("up", "gate")]
    down = np.concatenate([np.concatenate([i["L2_ffn_down_proj"][2 * m], i["L2_ffn_down_proj"][2 * m + 1]], 0)
                           for m in range(8)], 1)
    return np.concatenate([*pairs, down, i["L2_ffn_sh_gate"].T, i["L2_ffn_sh_up"].T, i["L2_ffn_sh_down"].T], 1)


def expert_weights3(i):
    return np.stack([np.concatenate([i["L3_ffn_w1"][e], tiles(i["L3_ffn_w2"][e])], 1) for e in range(8)])


def kernel(**inputs):
    import concourse.bacc as bacc
    from concourse.bass_utils import run_bass_kernel_spmd

    i = {name: np.asarray(a) for name, a in inputs.items()}
    feeds = {
        "x_in": np.reshape(i["L0_attn_x"], (TOK, P)).T, "small_in": small_weights(i), "consts_in": constants(),
        "sel_in": selectors(), "experts0_in": expert_weights0(i), "experts1_in": expert_weights1(i),
        "experts2_in": expert_weights2(i), "experts3_in": expert_weights3(i),
    }
    feeds = {name: np.ascontiguousarray(a) for name, a in feeds.items()}
    nc = bacc.Bacc("TRN2", target_bir_lowering=False, num_devices=1)
    args = [nc.dram_tensor(name, a.shape, mybir.dt.from_np(a.dtype), kind="ExternalInput").ap() for name, a in feeds.items()]
    out = nc.dram_tensor("out_0_dram", (P, TOK), F32, kind="ExternalOutput").ap()
    recurrent_layers(nc, *args, out)
    r = run_bass_kernel_spmd(nc, [feeds], core_ids=[0])
    return np.ascontiguousarray(np.reshape(r.results[0]["out_0_dram"].T, (BATCH, SEQ, P)))
```

```python
from contextlib import ExitStack

import numpy as np
import concourse.bass as bass
from concourse import mybir

ALU = mybir.AluOpType
ACT = mybir.ActivationFunctionType
F32 = mybir.dt.float32
BF16 = mybir.dt.bfloat16
U32 = mybir.dt.uint32
AX = mybir.AxisListType

P = 128
BATCH, SEQ = 2, 1024
TOK = BATCH * SEQ
NT = TOK // P
CH = 512
NC = TOK // CH
SLOTS = 18
NSTATE = 16
HEADS, DH = 16, 8
WKV_HEAD = 64
WC = 16
NWC = TOK // WC


class Layout:

    def __init__(self, parts):
        self.at, self.width = {}, 0
        for name, p, n in parts:
            self.at[name] = (self.width, p, n)
            self.width += n


SMALL = Layout([
    ("W_x", 128, 96), ("W_dt", 64, 128), ("W_out", 128, 128), ("A_log", 128, 16), ("b_dt", 128, 1), ("D", 128, 1),
    ("b_out", 128, 1), ("tokens", 128, 8), ("e_b1", 128, 32), ("e_b2", 128, 32), ("e_b3", 128, 8),
    ("q1", 128, 128), ("k1", 128, 128), ("v1", 128, 128), ("o1", 128, 128), ("gate1", 128, 8),
    ("q2", 128, 128), ("v2", 128, 128), ("anomaly", 128, 128), ("bq2", 128, 1), ("bv2", 128, 128),
    ("router", 128, 16), ("router_bias", 128, 16),
    ("maa_x", 128, 1), ("maa", 128, 5), ("maa_w1", 128, 160), ("maa_w2", 32, 640), ("decay_w1", 128, 64),
    ("decay_w2", 64, 128), ("decay", 128, 1), ("faaaa", 128, 1), ("Wr", 128, 128), ("Wk", 128, 128),
    ("Wv", 128, 128), ("Wg", 128, 128), ("Wo", 128, 128), ("ln_w", 128, 1), ("ln_b", 128, 1),
    ("ln1_g", 128, 1), ("ln1_b", 128, 1), ("ln2_g", 128, 1), ("ln2_b", 128, 1), ("q3", 128, 128), ("k3", 128, 128),
    ("v3", 128, 128), ("o3", 128, 128), ("bq3", 128, 1), ("bk3", 128, 1), ("bv3", 128, 1), ("bo3", 128, 1),
    ("gate3", 128, 8), ("gate_b3", 128, 8), ("f_b1", 128, 32), ("f_b2", 8, 128),
])
CONSTS = Layout([
    ("ident", 128, 128), ("ones", 128, 128), ("mean", 128, 128), ("head_ones", 128, 128), ("head_mean", 128, 128),
    ("iota", 128, 16), ("even", 128, 1), ("odd", 128, 1), ("eps_1e5", 128, 1), ("eps_scan", 128, 1),
    ("eps_wkv", 128, 1), ("start", 128, 16), ("zero", 128, 1),
])


class Kit:

    def __init__(self, nc, slots, small, consts, experts, sel, psum, scratch):
        self.nc, self.slots, self.small, self.consts = nc, slots, small, consts
        self.experts, self.sel, self.psum, self.scratch = experts, sel, psum, scratch

    def slot(self, i):
        return self.slots[:, i, :]

    def chunk(self, i, c):
        return self.slots[:, i, c * CH:(c + 1) * CH]

    def w(self, name):
        a, p, n = SMALL.at[name]
        return self.small[0:p, a:a + n]

    def c(self, name):
        a, p, n = CONSTS.at[name]
        return self.consts[0:p, a:a + n]

    def bank(self, b):
        return self.psum[:, b, :]


class Stage:

    def __init__(self, kit, name):
        self.kit, self.name, self.stack, self.sems = kit, name, ExitStack(), []

    def __enter__(self):
        self.stack.__enter__()
        return self

    def sem(self, name):
        self.sems.append(self.kit.nc.alloc_semaphore(f"{self.name}_{name}"))
        return self.sems[-1]

    def block(self):
        return self.stack.enter_context(self.kit.nc.Block())

    def __exit__(self, *e):
        self.stack.__exit__(*e)
        if e[0] is None:
            for sem in self.sems:
                self.kit.nc.gpsimd.sem_clear(sem)
                self.kit.nc.release_semaphore(sem)


def spread(ap, n):
    return ap.unsqueeze(2).broadcast_to([ap.shape[0], ap.shape[1], n])



class Arrivals:

    def __init__(self, nc, ctx):
        def sems(name, n):
            return [ctx.enter_context(nc.semaphore(f"{name}{r}")) for r in range(n)]

        self.small, self.sel = sems("small_loaded", 1)[0], sems("sel_loaded", 1)[0]
        self.experts = [sems("experts0_loaded", 2), sems("experts1_loaded", 1), sems("experts2_loaded", 1),
                        sems("experts3_loaded", E3_RING)]


def load_inputs(kit, arrivals, x_dram, small_dram, consts_dram, sel_dram, x, sel_slot):
    with Stage(kit, "load") as st:
        x_loaded, consts_loaded = st.sem("x_loaded"), st.sem("consts_loaded")
        block = st.block()

        @block.sync
        def _(sp):
            sp.dma_start(kit.slot(x), x_dram).then_inc(x_loaded, 16)
            sp.dma_start(kit.small[:, :], small_dram).then_inc(arrivals.small, 16)
            sp.dma_start(flat_slots(kit, sel_slot, 3)[0:96, 0:40 * P], sel_dram).then_inc(arrivals.sel, 16)
            sp.wait_ge(x_loaded, 16)

        @block.scalar
        def _(act):
            act.dma_start(kit.consts[:, :], consts_dram).then_inc(consts_loaded, 16)
            act.wait_ge(consts_loaded, 16)


def await_small(kit, arrivals):
    with Stage(kit, "small") as st:
        block = st.block()

        @block.sync
        def _(sp):
            sp.wait_ge(arrivals.small, 16)


def cast_selectors(kit, arrivals, sel_slot):
    with Stage(kit, "sel") as st:
        block = st.block()

        @block.vector
        def _(dve):
            dve.wait_ge(arrivals.sel, 16)
            nc = kit.nc
            nc.vector.tensor_copy(kit.sel[:, :, :].rearrange("p a b -> p (a b)"), flat_slots(kit, sel_slot, 3)[0:96, 0:40 * P])


def start_experts(kit, name, sources, cols, landed):
    with Stage(kit, name) as st:
        block = st.block()

        @block.sync
        def _(sp):
            for r, source in enumerate(sources):
                sp.dma_start(kit.experts[:, r * cols:(r + 1) * cols], source).then_inc(landed[r], 16)


def store_output(kit, out_dram, x, stored):
    with Stage(kit, "store") as st:
        block = st.block()

        @block.sync
        def _(sp):
            sp.dma_start(out_dram, kit.slot(x)).then_inc(stored, 16)
            sp.wait_ge(stored, 16)



def layer_norm(kit, name, src, dst, square, stat, gamma=None, beta=None):
    nc = kit.nc
    with Stage(kit, name) as st:
        mean_ready, centered, squared, var_ready = map(st.sem, ("mean", "centered", "squared", "var"))
        std_ready, rstd_ready, diag_ready, bcast_ready = map(st.sem, ("std", "rstd", "diag", "bcast"))
        scaled = st.sem("scaled")
        std = kit.slot(stat)[:, 0:NT]
        rstd = kit.slot(stat)[:, NT:2 * NT]
        diag = kit.slot(square).rearrange("p (j q) -> p j q", q=P)
        block = st.block()

        @block.tensor
        def _(pe):
            for c in range(NC):
                nc.tensor.matmul(kit.bank(c), kit.c("mean"), kit.chunk(src, c), start=True, stop=True).then_inc(mean_ready, 1)
            for j in range(NT):
                pe.wait_ge(squared, j // 4 + 1)
                last = nc.tensor.matmul(kit.psum[:, 4, j:j + 1], kit.slot(square)[:, j * P:(j + 1) * P],
                                        kit.c("mean")[:, 0:1], start=True, stop=True)
            last.then_inc(var_ready, 1)
            pe.wait_ge(diag_ready, 1)
            for c in range(NC):
                nc.tensor.matmul(kit.bank(c), kit.c("ones"), kit.chunk(square, c), start=True, stop=True).then_inc(bcast_ready, 1)

        @block.vector
        def _(dve):
            for c in range(NC):
                dve.wait_ge(mean_ready, c + 1)
                nc.vector.tensor_tensor(kit.chunk(dst, c), kit.chunk(src, c), kit.bank(c), ALU.subtract).then_inc(centered, 1)
            dve.wait_ge(std_ready, 1)
            nc.vector.reciprocal(rstd, std).then_inc(rstd_ready, 1)
            dve.wait_ge(rstd_ready, 1)
            nc.vector.tensor_tensor(diag, kit.c("ident").unsqueeze(1).broadcast_to([P, NT, P]), spread(rstd, P),
                                    ALU.mult).then_inc(diag_ready, 1)
            for c in range(NC):
                dve.wait_ge(bcast_ready, c + 1)
                if gamma is None:
                    nc.vector.tensor_tensor(kit.chunk(dst, c), kit.chunk(dst, c), kit.bank(c), ALU.mult).then_inc(scaled, 1)
                else:
                    nc.vector.scalar_tensor_tensor(kit.chunk(dst, c), kit.bank(c), kit.w(gamma), kit.chunk(dst, c),
                                                   ALU.mult, ALU.mult).then_inc(scaled, 1)
                    dve.wait_ge(scaled, 2 * c + 1)
                    nc.vector.tensor_scalar(kit.chunk(dst, c), kit.chunk(dst, c), kit.w(beta), None,
                                            ALU.add).then_inc(scaled, 1)

        @block.scalar
        def _(act):
            for c in range(NC):
                act.wait_ge(centered, c + 1)
                nc.scalar.activation(kit.chunk(square, c), kit.chunk(dst, c), ACT.Square).then_inc(squared, 1)
            act.wait_ge(var_ready, 1)
            nc.scalar.activation(std, kit.psum[:, 4, 0:NT], ACT.Sqrt, bias=kit.c("eps_1e5")).then_inc(std_ready, 1)



def project(kit, name, jobs):
    nc = kit.nc
    with Stage(kit, name) as st:
        product, by_act, by_dve = map(st.sem, ("product", "by_act", "by_dve"))
        block = st.block()
        steps = [(job, c) for job in jobs for c in range(NC)]
        by_dve_alone = len(jobs) == 1 and jobs[0][4] is not None

        @block.tensor
        def _(pe):
            for i, ((dst, w, src, bias, plus), c) in enumerate(steps):
                if i >= 8:
                    pe.wait_ge(by_act if i % 2 == 0 else by_dve, (i - 8) // 2 + 1)
                nc.tensor.matmul(kit.bank(i % 8), kit.w(w), kit.chunk(src, c), start=True, stop=True).then_inc(product, 1)

        @block.scalar
        def _(act):
            for i, ((dst, w, src, bias, plus), c) in enumerate(steps):
                if i % 2 == 0 and not by_dve_alone:
                    act.wait_ge(product, i + 1)
                    nc.scalar.activation(kit.chunk(dst, c), kit.bank(i % 8), ACT.Identity,
                                         bias=kit.w(bias) if bias else 0.0).then_inc(by_act, 1)

        @block.vector
        def _(dve):
            for i, ((dst, w, src, bias, plus), c) in enumerate(steps):
                if by_dve_alone:
                    dve.wait_ge(product, i + 1)
                    nc.vector.scalar_tensor_tensor(kit.chunk(dst, c), kit.bank(i), kit.w(bias) if bias else 0.0,
                                                   kit.chunk(plus, c), ALU.add, ALU.add)
                elif i % 2 == 1:
                    dve.wait_ge(product, i + 1)
                    if bias:
                        nc.vector.tensor_scalar(kit.chunk(dst, c), kit.bank(i % 8), kit.w(bias), None, ALU.add).then_inc(by_dve, 1)
                    else:
                        nc.vector.tensor_copy(kit.chunk(dst, c), kit.bank(i % 8)).then_inc(by_dve, 1)



def scan_inputs(kit, xn, low, delta, du, suffix, y, rows, tmp):
    nc = kit.nc
    with Stage(kit, "scan_in") as st:
        proj, low_ready, bc_ready, z_ready, z_copied = map(st.sem, ("proj", "low", "bc", "z", "z_copied"))
        neg_abs, exped, logged, own, a_exp = map(st.sem, ("neg_abs", "exped", "logged", "own", "a_exp"))
        block = st.block()
        bc = kit.slot(rows)[0:32, :]

        @block.tensor
        def _(pe):
            for c in range(NC):
                nc.tensor.matmul(kit.bank(c)[0:64], kit.w("W_x")[:, 0:64], kit.chunk(xn, c), start=True, stop=True).then_inc(proj, 1)
            for c in range(NC):
                nc.tensor.matmul(kit.bank(4 + c)[0:32], kit.w("W_x")[:, 64:96], kit.chunk(xn, c), start=True, stop=True).then_inc(proj, 1)
            for c in range(NC):
                pe.wait_ge(low_ready, c + 1)
                nc.tensor.matmul(kit.bank(c), kit.w("W_dt"), kit.chunk(low, c)[0:64], start=True, stop=True).then_inc(z_ready, 1)

        @block.scalar
        def _(act):
            nc.scalar.preload_act_table_set("natural_log_exp_and_others")
            nc.scalar.activation(kit.scratch[:, 0:NSTATE], kit.w("A_log"), ACT.Exp).then_inc(a_exp, 1)
            for c in range(NC):
                act.wait_ge(proj, c + 1)
                nc.scalar.activation(kit.chunk(low, c)[0:64], kit.bank(c)[0:64], ACT.Copy).then_inc(low_ready, 1)
            for c in range(NC):
                act.wait_ge(z_ready, c + 1)
                nc.scalar.activation(kit.chunk(delta, c), kit.bank(c), ACT.Identity, bias=kit.w("b_dt")).then_inc(z_copied, 1)
            for c in range(NC):
                act.wait_ge(neg_abs, c + 1)
                nc.scalar.activation(kit.chunk(suffix, c), kit.chunk(suffix, c), ACT.Exp).then_inc(exped, 1)
                act.wait_ge(exped, c + 1)
                nc.scalar.activation(kit.chunk(suffix, c), kit.chunk(suffix, c), ACT.Ln, bias=kit.c("ones")[:, 0:1]).then_inc(logged, 1)

        @block.vector
        def _(dve):
            for c in range(NC):
                dve.wait_ge(proj, NC + c + 1)
                nc.vector.tensor_copy(kit.chunk(rows, c)[0:32], kit.bank(4 + c)[0:32]).then_inc(bc_ready, 1)
            dve.wait_ge(a_exp, 1)
            nc.vector.tensor_scalar(kit.scratch[:, 16:32], kit.scratch[:, 0:NSTATE], -1.0, None, ALU.mult)
            for c in range(NC):
                dve.wait_ge(z_copied, c + 1)
                nc.vector.scalar_tensor_tensor(kit.chunk(suffix, c), kit.chunk(delta, c), -1.0, kit.chunk(delta, c),
                                               ALU.mult, ALU.min).then_inc(neg_abs, 1)
            for c in range(NC):
                dve.wait_ge(logged, c + 1)
                nc.vector.scalar_tensor_tensor(kit.chunk(delta, c), kit.chunk(delta, c), 0.0, kit.chunk(suffix, c),
                                               ALU.max, ALU.add).then_inc(own, 1)
            dve.wait_ge(own, NC)
            for b in range(BATCH):
                a, z = b * SEQ, (b + 1) * SEQ
                nc.vector.tensor_tensor_scan(kit.slot(suffix)[:, a:z - 1][:, ::-1],
                                             kit.c("ones")[:, 0:1].broadcast_to([P, SEQ - 1]),
                                             kit.slot(delta)[:, a + 1:z][:, ::-1], 0.0, ALU.mult, ALU.add)
                nc.vector.memset(kit.slot(suffix)[:, z - 1:z], 0.0)
            nc.vector.tensor_tensor(kit.slot(du), kit.slot(delta), kit.slot(xn), ALU.mult)
            nc.vector.tensor_scalar(kit.slot(y), kit.slot(xn), kit.w("D"), None, ALU.mult)

    split_rows(kit, "scan_split", rows, 2 * NSTATE, low, tmp)


def split_rows(kit, name, src, n, dst, tmp):
    nc = kit.nc
    rows = kit.slot(src)[0:n, :]
    rest = kit.slot(tmp)[0:n, :]
    parts = kit.slot(dst).bitcast(BF16)
    middle = parts[0:n, TOK:2 * TOK]
    with Stage(kit, name) as st:
        own = st.sem("own")
        block = st.block()

        @block.vector
        def _(dve):
            if n < 32:
                nc.vector.memset(kit.slot(dst)[0:96, 0:TOK // 2], 0.0).then_inc(own, 1)
                dve.wait_ge(own, 1)
            o = 1 if n < 32 else 0
            nc.vector.tensor_copy(parts[0:n, 0:TOK], rows).then_inc(own, 1)
            dve.wait_ge(own, o + 1)
            nc.vector.tensor_tensor(rest, rows, parts[0:n, 0:TOK], ALU.subtract).then_inc(own, 1)
            dve.wait_ge(own, o + 2)
            nc.vector.tensor_copy(middle, rest).then_inc(own, 1)
            dve.wait_ge(own, o + 3)
            nc.vector.tensor_copy(parts[32:32 + n, 0:TOK], middle)
            nc.vector.tensor_tensor(parts[64:64 + n, 0:TOK], rest, middle, ALU.subtract)



def router(kit, name, src, gate, bias, experts, rule, rows, stacked, work, tmp):
    nc = kit.nc
    flat = kit.slot(work)

    def field(at, n):
        return flat[:, at:at + NT * n].rearrange("p (j n) -> p j n", n=n)

    score, total, best = field(0, experts), field(256, 1), field(272, 8)
    index = flat[:, 400:400 + NT * 8].bitcast(U32).rearrange("p (j n) -> p j n", n=8)
    index_f, first, second = field(528, 8), field(656, experts), field(912, experts)
    e2, w1, w2, weight = field(1168, 1), field(1184, 1), field(1200, 1), field(1216, experts)
    iota = kit.c("iota")[:, 0:experts].unsqueeze(1).broadcast_to([P, NT, experts])

    def wide(ap):
        return ap.broadcast_to([P, NT, experts])

    with Stage(kit, name) as st:
        logits, exp_in, exp_out, own = map(st.sem, ("logits", "exp_in", "exp_out", "own"))
        weights_ready, turned = map(st.sem, ("weights", "turned"))
        block = st.block()

        @block.tensor
        def _(pe):
            for j in range(NT):
                last = nc.tensor.matmul(kit.bank(0)[:, j * experts:(j + 1) * experts], kit.slot(src)[:, j * P:(j + 1) * P],
                                        kit.w(gate), start=True, stop=True)
            last.then_inc(logits, 1)
            pe.wait_ge(weights_ready, 1)
            for j in range(NT):
                last = nc.tensor.transpose(kit.bank(4 + j // 4)[0:experts, (j % 4) * P:(j % 4 + 1) * P], weight[:, j, :],
                                           kit.c("ident"))
            last.then_inc(turned, 1)

        @block.scalar
        def _(act):
            if rule in ("scores", "top"):
                act.wait_ge(exp_in, 1)
                what = score if rule == "scores" else e2
                nc.scalar.activation(what, what, ACT.Exp).then_inc(exp_out, 1)

        @block.vector
        def _(dve):
            done = [0]

            def then(instruction):
                done[0] += 1
                instruction.then_inc(own, 1)
                dve.wait_ge(own, done[0])

            dve.wait_ge(logits, 1)
            raw = kit.bank(0)[:, 0:NT * experts].rearrange("p (j n) -> p j n", n=experts)
            if bias:
                then(nc.vector.tensor_tensor(score, raw, kit.w(bias).unsqueeze(1).broadcast_to([P, NT, experts]), ALU.add))
            else:
                then(nc.vector.tensor_copy(score, raw))
            if rule == "scores":
                then(nc.vector.tensor_reduce(total, score, AX.X, ALU.max))
                nc.vector.tensor_tensor(score, score, wide(total), ALU.subtract).then_inc(exp_in, 1)
                dve.wait_ge(exp_out, 1)
                then(nc.vector.tensor_reduce(total, score, AX.X, ALU.add))
                then(nc.vector.reciprocal(total, total))
                then(nc.vector.tensor_tensor(score, score, wide(total), ALU.mult))
            for j in range(NT):
                last = nc.vector.max(best[:, j, :], score[:, j, :])
            then(last)
            for j in range(NT):
                last = nc.vector.max_index(index[:, j, :], best[:, j, :], score[:, j, :])
            then(last)
            then(nc.vector.tensor_copy(index_f, index))
            nc.vector.tensor_tensor(first, iota, wide(index_f[:, :, 0:1]), ALU.is_equal)
            then(nc.vector.tensor_tensor(second, iota, wide(index_f[:, :, 1:2]), ALU.is_equal))
            if rule == "half":
                then(nc.vector.tensor_tensor(first, first, second, ALU.add))
                nc.vector.tensor_scalar(weight, first, 0.5, None, ALU.mult).then_inc(weights_ready, 1)
            elif rule == "scores":
                then(nc.vector.tensor_tensor(first, first, second, ALU.add))
                nc.vector.tensor_tensor(weight, first, score, ALU.mult).then_inc(weights_ready, 1)
            elif rule == "top":
                nc.vector.tensor_tensor(e2, best[:, :, 1:2], best[:, :, 0:1], ALU.subtract).then_inc(exp_in, 1)
                dve.wait_ge(exp_out, 1)
                then(nc.vector.tensor_scalar(w1, e2, 1.0, None, ALU.add))
                then(nc.vector.reciprocal(w1, w1))
                then(nc.vector.tensor_tensor(w2, w1, e2, ALU.mult))
                nc.vector.tensor_tensor(first, first, wide(w1), ALU.mult)
                then(nc.vector.tensor_tensor(second, second, wide(w2), ALU.mult))
                nc.vector.tensor_tensor(weight, first, second, ALU.add).then_inc(weights_ready, 1)
            else:
                nc.vector.tensor_copy(weight, first).then_inc(weights_ready, 1)
            dve.wait_ge(turned, 1)
            nc.vector.tensor_copy(kit.slot(rows)[0:experts, :], kit.psum[0:experts, 4:8, :].rearrange("p a b -> p (a b)"))

    split_rows(kit, name + "_split", rows, experts, stacked, tmp)


def spread_rows(kit, name, stacked, matrices, outs):
    nc = kit.nc
    parts = kit.slot(stacked).bitcast(BF16)[0:96, 0:TOK]
    with Stage(kit, name) as st:
        spread_ready, by_act, by_dve = map(st.sem, ("spread", "by_act", "by_dve"))
        block = st.block()

        @block.tensor
        def _(pe):
            for i, m in enumerate(matrices):
                if i >= 2:
                    pe.wait_ge(by_act if i % 2 == 0 else by_dve, i // 2)
                for c in range(NC):
                    last = nc.tensor.matmul(kit.bank(4 * (i % 2) + c), kit.sel[0:96, m, :], parts[:, c * CH:(c + 1) * CH],
                                            start=True, stop=True)
                last.then_inc(spread_ready, 1)

        @block.scalar
        def _(act):
            for i in range(0, len(matrices), 2):
                act.wait_ge(spread_ready, i + 1)
                nc.scalar.activation(outs[i], kit.psum[:, 0:4, :].rearrange("p a b -> p (a b)"),
                                     ACT.Copy).then_inc(by_act, 1)

        @block.vector
        def _(dve):
            for i in range(1, len(matrices), 2):
                dve.wait_ge(spread_ready, i + 1)
                nc.vector.tensor_copy(outs[i], kit.psum[:, 4:8, :].rearrange("p a b -> p (a b)")).then_inc(by_dve, 1)



def merge(kit, name, x, s, tmp, g=None):
    nc = kit.nc
    with Stage(kit, name) as st:
        gated, own = map(st.sem, ("gated", "own"))
        block = st.block()

        @block.scalar
        def _(act):
            for c in range(NC):
                nc.scalar.activation(kit.chunk(tmp, c), kit.bank(4 + c) if g is None else kit.chunk(g, c), ACT.Silu).then_inc(gated, 1)

        @block.vector
        def _(dve):
            for c in range(NC):
                dve.wait_ge(gated, c + 1)
                nc.vector.tensor_tensor(kit.chunk(tmp, c), kit.chunk(tmp, c), kit.chunk(s, c), ALU.mult).then_inc(own, 1)
                dve.wait_ge(own, c + 1)
                nc.vector.tensor_tensor(kit.chunk(x, c), kit.chunk(x, c), kit.chunk(tmp, c), ALU.add)



HID = 512
HB = HID // P
E0_COLS = HID + HB * HID + HB * P
N_EXP0 = 8


def experts_and_scan(kit, dram, landed, xn, weights, acc, h1, h2, stacked, du, suffix, y, halves):
    nc = kit.nc
    steps = [(e, c) for e in range(N_EXP0) for c in range(NC)]
    n_steps = len(steps)
    assert n_steps == NSTATE * BATCH
    w1 = [kit.experts[:, b * E0_COLS:b * E0_COLS + HID] for b in range(2)]
    w2 = [kit.experts[:, b * E0_COLS + HID:b * E0_COLS + HID + HB * HID].rearrange("p (k n) -> p k n", n=HID) for b in range(2)]
    w3 = [kit.experts[:, (b + 1) * E0_COLS - HB * P:(b + 1) * E0_COLS].rearrange("p (k n) -> p k n", n=P) for b in range(2)]
    a_neg = kit.scratch[:, NSTATE:2 * NSTATE]
    gated = kit.scratch[:, CH:2 * CH]
    parts = kit.slot(stacked).bitcast(BF16)[0:96, 0:TOK]
    decay, inv, work, scan, tmp = halves
    spread_banks = kit.psum[:, 6:8, :].rearrange("p a b -> p (a b)")
    with Stage(kit, "e0") as st:
        hidden, gelu_done, expert_out, taken, own = map(st.sem, ("hidden", "gelu", "expert_out", "taken", "own"))
        b_spread, c_spread, decay_ready, log_ready, inv_ready = map(st.sem, ("b", "c", "decay", "log", "inv"))
        b_used, decayed, scanned, c_used, weighted, y_ready = map(st.sem, ("b_used", "decayed", "scanned", "c_used", "weighted", "y"))
        block = st.block()

        @block.sync
        def _(sp):
            for e in range(2, N_EXP0):
                sp.wait_ge(expert_out, NC * (e - 1))
                sp.dma_start(kit.experts[:, (e % 2) * E0_COLS:(e % 2 + 1) * E0_COLS], dram[e]).then_inc(landed[e % 2], 16)

        @block.tensor
        def _(pe):
            group = [0]

            def hidden_group(operands):
                g = group[0]
                if g >= 4:
                    pe.wait_ge(gelu_done, g - 3)
                for n, (lhs, rhs) in enumerate(operands):
                    last = nc.tensor.matmul(kit.bank(g % 4), lhs, rhs, start=n == 0, stop=n == len(operands) - 1)
                last.then_inc(hidden, 1)
                group[0] = g + 1

            def first(i):
                e, c = steps[i]
                if c == 0:
                    pe.wait_ge(landed[e % 2], 16 * (e // 2 + 1))
                for m in range(HB):
                    hidden_group([(w1[e % 2][:, m * P:(m + 1) * P], kit.chunk(xn, c))])

            def second(i):
                e, c = steps[i]
                pe.wait_ge(gelu_done, 8 * i if i else 4)
                for m in range(HB):
                    hidden_group([(w2[e % 2][:, k, m * P:(m + 1) * P], kit.chunk(h1[i % 2], k)) for k in range(HB)])

            def third(i):
                e, c = steps[i]
                pe.wait_ge(gelu_done, min(8 * (i + 1) + 4, 8 * n_steps))
                if i >= 2:
                    pe.wait_ge(taken, i - 1)
                for k in range(HB):
                    last = nc.tensor.matmul(kit.bank(4 + i % 2), w3[e % 2][:, k, :], kit.chunk(h2[i % 2], k), start=k == 0, stop=k == HB - 1)
                last.then_inc(expert_out, 1)

            def spread_row(i, row, done):
                for c in range(2):
                    at = i % 2 * SEQ + c * CH
                    last = nc.tensor.matmul(kit.bank(6 + c), kit.sel[0:96, row, :], parts[:, at:at + CH], start=True, stop=True)
                last.then_inc(done, 1)

            for i in range(n_steps + 2):
                if i < n_steps:
                    if i >= 1:
                        pe.wait_ge(c_used, i)
                    spread_row(i, i // 2, b_spread)
                    first(i)
                if 1 <= i <= n_steps:
                    second(i - 1)
                if i < n_steps:
                    pe.wait_ge(b_used, i + 1)
                    spread_row(i, NSTATE + i // 2, c_spread)
                if i >= 2:
                    third(i - 2)

        @block.scalar
        def _(act):
            group = [0]

            def gelu(out, bias):
                g = group[0]
                act.wait_ge(hidden, g + 1)
                nc.scalar.activation(out, kit.bank(g % 4), ACT.Gelu, bias=bias).then_inc(gelu_done, 1)
                group[0] = g + 1

            def decays(i):
                if i >= 1:
                    act.wait_ge(decayed, i)
                nc.scalar.preload_act_table_set("natural_log_exp_and_others")
                nc.scalar.activation(decay, kit.slot(suffix)[:, i % 2 * SEQ:(i % 2 + 1) * SEQ], ACT.Exp,
                                     scale=a_neg[:, i // 2:i // 2 + 1]).then_inc(decay_ready, 1)
                act.wait_ge(decay_ready, i + 1)
                if i >= 1:
                    act.wait_ge(weighted, i)
                nc.scalar.activation(inv, decay, ACT.Ln, bias=kit.c("eps_scan")).then_inc(log_ready, 1)
                act.wait_ge(log_ready, i + 1)
                nc.scalar.activation(inv, inv, ACT.Exp, scale=-1.0).then_inc(inv_ready, 1)

            for i in range(n_steps + 1):
                if i < n_steps:
                    e, c = steps[i]
                    for m in range(HB):
                        gelu(kit.chunk(h1[i % 2], m), kit.w("e_b1")[:, HB * e + m:HB * e + m + 1])
                for m in range(HB):
                    if i >= 1:
                        e, c = steps[i - 1]
                        gelu(kit.chunk(h2[(i - 1) % 2], m), kit.w("e_b2")[:, HB * e + m:HB * e + m + 1])
                    if m == 1 and i < n_steps:
                        decays(i)

        @block.vector
        def _(dve):
            def scan_step(i):
                at = i % 2 * SEQ
                dve.wait_ge(b_spread, i + 1)
                if i >= 1:
                    dve.wait_ge(weighted, i)
                nc.vector.tensor_tensor(work, kit.slot(du)[:, at:at + SEQ], spread_banks, ALU.mult).then_inc(b_used, 1)
                dve.wait_ge(b_used, i + 1)
                dve.wait_ge(decay_ready, i + 1)
                nc.vector.tensor_tensor(work, work, decay, ALU.mult).then_inc(decayed, 1)
                dve.wait_ge(decayed, i + 1)
                nc.vector.tensor_tensor_scan(scan, kit.c("ones")[:, 0:1].broadcast_to([P, SEQ]), work, 0.0,
                                             ALU.mult, ALU.add).then_inc(scanned, 1)
                dve.wait_ge(scanned, i + 1)
                dve.wait_ge(c_spread, i + 1)
                nc.vector.tensor_tensor(work, scan, spread_banks, ALU.mult).then_inc(c_used, 1)

            def gate(i):
                e, c = steps[i]
                dve.wait_ge(expert_out, i + 1)
                out = kit.chunk(acc, c) if e == 0 else gated
                if i > NC:
                    dve.wait_ge(own, i - NC)
                nc.vector.scalar_tensor_tensor(out, kit.bank(4 + i % 2), kit.w("e_b3")[:, e:e + 1],
                                               weights[e][:, c * CH:(c + 1) * CH], ALU.add, ALU.mult).then_inc(taken, 1)
                if e > 0:
                    dve.wait_ge(taken, i + 1)
                    nc.vector.tensor_tensor(kit.chunk(acc, c), kit.chunk(acc, c), gated, ALU.add).then_inc(own, 1)

            for i in range(n_steps + 3):
                if i < n_steps:
                    scan_step(i)
                if i >= 3:
                    gate(i - 3)

        @block.gpsimd
        def _(pool):
            for i in range(n_steps):
                at = i % 2 * SEQ
                pool.wait_ge(c_used, i + 1)
                pool.wait_ge(inv_ready, i + 1)
                if i >= 1:
                    pool.wait_ge(y_ready, i)
                nc.gpsimd.tensor_tensor(tmp, work, inv, ALU.mult).then_inc(weighted, 1)
                pool.wait_ge(weighted, i + 1)
                nc.gpsimd.tensor_tensor(kit.slot(y)[:, at:at + SEQ], kit.slot(y)[:, at:at + SEQ], tmp, ALU.add).then_inc(y_ready, 1)



PARTS = 3
BLOCK_ROWS = DH * PARTS
PAIR_ROWS = 96
FULL_ROWS = PAIR_ROWS + 3
STACKS = 12
SQ = 32
KT = SEQ // P


def flat_slots(kit, i, n):
    return kit.slots[:, i:i + n, :].rearrange("p a b -> p (a b)")


def attention(kit, name, xn, weights, out, q_stack, k_stack, sums, values, work):
    nc = kit.nc
    wq, wk, wv, bq, bk = weights
    q, k = work, work + 1
    project(kit, name + "_qk", [(q, wq, xn, bq, None), (k, wk, xn, bk, None)])

    qs = flat_slots(kit, q_stack, 3).bitcast(BF16).rearrange("p (r t) -> p r t", r=STACKS)
    ks = flat_slots(kit, k_stack, 3).bitcast(BF16).rearrange("p (r t) -> p r t", r=STACKS)
    v = flat_slots(kit, values, 2).rearrange("p (j h n) -> p j h n", h=HEADS, n=2 * DH)
    split = kit.experts[:, :].bitcast(BF16).rearrange("p (w s t) -> p w s t", w=2, s=3)

    with Stage(kit, name + "_prep") as st:
        tile_ready, ones_set, v_ready = map(st.sem, ("tile", "ones_set", "v"))
        high, mid, rest = map(st.sem, ("high", "mid", "rest"))
        block = st.block()

        @block.tensor
        def _(pe):
            for j in range(NT):
                nc.tensor.matmul(kit.bank(j // 4)[:, (j % 4) * P:(j % 4 + 1) * P], kit.slot(xn)[:, j * P:(j + 1) * P],
                                 kit.w(wv), start=True, stop=True).then_inc(tile_ready, 1)

        @block.scalar
        def _(act):
            for w, src in enumerate((q, k)):
                nc.scalar.activation(split[:, w, 0], kit.slot(src), ACT.Copy).then_inc(high, 1)
            for w, src in enumerate((q, k)):
                act.wait_ge(rest, w + 1)
                nc.scalar.activation(split[:, w, 1], kit.slot(src), ACT.Copy).then_inc(mid, 1)
            act.wait_ge(ones_set, 2)
            for g in range(4):
                act.wait_ge(tile_ready, 4 * g + 4)
                nc.scalar.activation(v[:, 4 * g:4 * g + 4, :, 0:DH], kit.bank(g).rearrange("p (j h n) -> p j h n", j=4, n=DH),
                                     ACT.Copy).then_inc(v_ready, 1)

        @block.vector
        def _(dve):
            for w, src in enumerate((q, k)):
                dve.wait_ge(high, w + 1)
                nc.vector.tensor_tensor(kit.slot(src), kit.slot(src), split[:, w, 0], ALU.subtract).then_inc(rest, 1)
            for w, src in enumerate((q, k)):
                dve.wait_ge(mid, w + 1)
                nc.vector.tensor_tensor(split[:, w, 2], kit.slot(src), split[:, w, 1], ALU.subtract)

        @block.gpsimd
        def _(pool):
            nc.gpsimd.memset(v, 1.0).then_inc(ones_set, 1)
            pool.wait_ge(ones_set, 1)
            nc.gpsimd.memset(ks[PAIR_ROWS:FULL_ROWS], 1.0).then_inc(ones_set, 1)
            nc.gpsimd.memset(ks[64:PAIR_ROWS], 0.0)
            nc.gpsimd.memset(qs[64:PAIR_ROWS], 0.0)

    scale = 1.0 / float(np.sqrt(np.float32(DH)))
    heads = [(b, h) for b in range(BATCH) for h in range(HEADS)]
    n_heads = len(heads)
    n_tiles = KT * n_heads
    QUAD = 4
    QUAD_TILES = QUAD * KT
    n_quads = n_heads // QUAD
    AHEAD = QUAD_TILES + KT
    RING = 2 * QUAD
    probs = flat_slots(kit, work, 4).rearrange("p (r t) -> p r t", t=SEQ)
    evac = kit.slot(sums).rearrange("p (r t) -> p r t", t=SEQ)
    den = kit.slot(sums + 1)
    half_max = kit.scratch[:, 0:4 * KT].rearrange("p (r n c) -> p r n c", n=KT, c=2)
    neg_max = kit.scratch[:, 32:32 + 2 * KT].rearrange("p (r n) -> p r n", n=KT)
    max_rest = kit.scratch[:, 64:64 + 2 * KT].rearrange("p (r n) -> p r n", n=KT)
    squares = kit.scratch[:, 128:256].bitcast(BF16).rearrange("p (w r n) -> p w r n", w=2, n=2 * SQ)
    max_parts, turned = squares[:, 0, :, 0:SQ], squares[:, 1, :, 0:SQ]
    with Stage(kit, name) as st:
        stacked = [st.sem(f"stacked{r}") for r in range(STACKS)]
        scores_a, maxed, combined, max_split, max_turned = map(st.sem, ("scores_a", "maxed", "combined", "max_split", "max_turned"))
        max_placed = [st.sem(f"placed{j}") for j in range(QUAD)]
        scores_b, exped, summed, evacuated, own = map(st.sem, ("scores_b", "exped", "summed", "evacuated", "own"))
        stored, inverted = [st.sem("stored0"), st.sem("stored1")], st.sem("inverted")
        block = st.block()
        banks_b = [kit.psum[:, 2 + 2 * r:4 + 2 * r, :].rearrange("p a b -> p (a b)") for r in range(2)]

        def tile_b(u):
            return u // QUAD_TILES * QUAD + u % QUAD, u % QUAD_TILES // QUAD

        def weigh(pe, g, part):
            i, t = tile_b(QUAD * g)
            c, at = part // 2, part % 2 * (CH // 2)
            if part == 0:
                pe.wait_ge(exped, QUAD * (g + 1))
            if t == 0 and i > 0:
                pe.wait_ge(evacuated, 2 * (i // QUAD) + c - 1)
            for j in range(QUAD):
                b, h = heads[i + j]
                last = nc.tensor.matmul(kit.bank(6 + c)[32 * j:32 * j + 32, at:at + CH // 2], v[:, KT * b + t, h // 2 * 2:h // 2 * 2 + 2, :],
                                        probs[:, (QUAD * g + j) % RING, c * CH + at:c * CH + at + CH // 2],
                                        start=t == 0 and at == 0, stop=t == KT - 1 and at > 0)
            last.then_inc(summed, 1)

        def take(act, quad, c):
            act.wait_ge(summed, QUAD * (KT * (quad + 1) - 1) + 2 * (c + 1))
            if quad >= 2:
                act.wait_ge(stored[quad % 2], 16 * 2 * QUAD * (quad // 2))
            nc.scalar.activation(evac[:, quad % 2, c * CH:(c + 1) * CH], kit.bank(6 + c), ACT.Copy).then_inc(evacuated, 1)

        @block.tensor
        def _(pe):
            def half_a(n, c):
                i, t = n // KT, n % KT
                r = i % STACKS
                if t == 0:
                    pe.wait_ge(stacked[r], 16 * 2 * PARTS * (i // STACKS + 1))
                if n >= 1:
                    pe.wait_ge(maxed, 2 * n + c - 1)
                nc.tensor.matmul(kit.bank(c), qs[0:PAIR_ROWS, r, t * P:(t + 1) * P],
                                 ks[0:PAIR_ROWS, r, c * CH:(c + 1) * CH], start=True, stop=True).then_inc(scores_a, 1)

            def full_b(u):
                i, t = tile_b(u)
                r = i % STACKS
                if t == 0:
                    pe.wait_ge(max_placed[i % QUAD], 16 * 4 * (i // QUAD + 1))
                if u >= 2:
                    pe.wait_ge(exped, u - 1)
                for c in range(2):
                    last = nc.tensor.matmul(banks_b[u % 2][:, c * CH:(c + 1) * CH], ks[0:FULL_ROWS, r, t * P:(t + 1) * P],
                                            qs[0:FULL_ROWS, r, c * CH:(c + 1) * CH], start=True, stop=True)
                last.then_inc(scores_b, 1)

            for n in range(n_tiles + AHEAD):
                u = n - AHEAD
                if n < n_tiles:
                    half_a(n, 0)
                if u >= 0:
                    full_b(u)
                if n < n_tiles:
                    half_a(n, 1)
                if u >= QUAD:
                    weigh(pe, u // QUAD - 1, u % QUAD)
            for part in range(QUAD):
                weigh(pe, n_tiles // QUAD - 1, part)

        @block.gpsimd
        def _(pool):
            for i in range(n_heads):
                r = i % 2
                part = [max_parts[:, r, KT * j:KT * j + KT] for j in range(PARTS)]
                pool.wait_ge(combined, i + 1)
                if i >= 2:
                    pool.wait_ge(max_turned, i - 1)
                nc.gpsimd.tensor_copy(part[0], neg_max[:, r]).then_inc(own, 1)
                pool.wait_ge(own, 3 * i + 1)
                nc.gpsimd.tensor_tensor(max_rest[:, r], neg_max[:, r], part[0], ALU.subtract).then_inc(own, 1)
                pool.wait_ge(own, 3 * i + 2)
                nc.gpsimd.tensor_copy(part[1], max_rest[:, r]).then_inc(own, 1)
                pool.wait_ge(own, 3 * i + 3)
                nc.gpsimd.tensor_tensor(part[2], max_rest[:, r], part[1], ALU.subtract).then_inc(max_split, 1)

        @block.vector
        def _(dve):
            def turn(i):
                dve.wait_ge(max_split, i + 1)
                if i >= 2:
                    dve.wait_ge(max_placed[(i - 2) % QUAD], 16 * 4 * ((i - 2) // QUAD + 1))
                nc.vector.transpose(turned[:, i % 2], max_parts[:, i % 2]).then_inc(max_turned, 1)

            nc.vector.memset(squares, 0.0)
            for i in range(n_heads):
                for t in range(KT):
                    if t == 3 and i >= 1:
                        turn(i - 1)
                    for c in range(2):
                        dve.wait_ge(scores_a, 2 * (KT * i + t) + c + 1)
                        nc.vector.tensor_reduce(half_max[:, i % 2, t, c:c + 1], kit.bank(c), AX.X, ALU.max, negate=True).then_inc(maxed, 1)
                dve.wait_ge(maxed, 2 * KT * (i + 1))
                if i >= 2:
                    dve.wait_ge(max_split, i - 1)
                nc.vector.tensor_tensor(neg_max[:, i % 2].unsqueeze(2), half_max[:, i % 2, :, 0:1], half_max[:, i % 2, :, 1:2], ALU.min).then_inc(combined, 1)
            turn(n_heads - 1)

            quads = HEADS // QUAD
            for step, (b, last, rows) in enumerate([(0, quads - 1, slice(0, P)), (1, 2 * quads - 2, slice(0, 96)),
                                                    (1, 2 * quads - 1, slice(96, P))]):
                for r in range(2):
                    dve.wait_ge(stored[r], 16 * 2 * QUAD * ((last - r) // 2 + 1))
                inv, sums_v = den[rows, b * SEQ:(b + 1) * SEQ], kit.slot(out)[rows, b * SEQ:(b + 1) * SEQ]
                nc.vector.reciprocal(inv, inv).then_inc(inverted, 1)
                dve.wait_ge(inverted, step + 1)
                nc.vector.tensor_tensor(sums_v, sums_v, inv, ALU.mult)

        @block.sync
        def _(sp):
            def stack(i):
                b, h = heads[i]
                if i >= STACKS:
                    sp.wait_ge(scores_b, QUAD_TILES * ((i - STACKS) // QUAD + 1))
                for j in range(PARTS):
                    rows = slice(BLOCK_ROWS * j, BLOCK_ROWS * (j + 1))
                    part = split[DH * h:DH * h + DH, 0, j:j + 1, b * SEQ:(b + 1) * SEQ].broadcast_to([DH, PARTS, SEQ])
                    sp.dma_start(qs[rows, i % STACKS, :], part).then_inc(stacked[i % STACKS], 16)
                    sp.dma_start(ks[rows, i % STACKS, :],
                                 split[DH * h:DH * h + DH, 1, :, b * SEQ:(b + 1) * SEQ]).then_inc(stacked[i % STACKS], 16)

            def store(quad):
                sp.wait_ge(evacuated, 2 * (quad + 1))
                for j in range(QUAD):
                    b, h = heads[QUAD * quad + j]
                    row = 32 * j + 16 * (h % 2)
                    for dst, r in ((kit.slot(out), row), (den, row + DH)):
                        sp.dma_start(dst[DH * h:DH * h + DH, b * SEQ:(b + 1) * SEQ], evac[r:r + DH, quad % 2]).then_inc(stored[quad % 2], 16)

            for i in range(QUAD):
                stack(i)
            for i in range(n_heads):
                sp.wait_ge(max_turned, i + 1)
                rows = qs[PAIR_ROWS:FULL_ROWS, i % STACKS, :].rearrange("p (n b t) -> p n b t", n=KT, t=SQ)
                for b in range(P // SQ):
                    sp.dma_start(rows[:, :, b, :], turned[SQ * b:SQ * b + PARTS * KT, i % 2]).then_inc(max_placed[i % QUAD], 16)
                if i + QUAD < n_heads:
                    stack(i + QUAD)
                if i >= 10 and i % QUAD == 2:
                    store((i - 10) // QUAD)
            for quad in range((n_heads - 11) // QUAD + 1, n_quads):
                store(quad)
            for r in range(2):
                sp.wait_ge(stored[r], 16 * 2 * QUAD * (n_quads // 2))

        @block.scalar
        def _(act):
            for u in range(n_tiles):
                act.wait_ge(scores_b, u + 1)
                if u >= RING:
                    act.wait_ge(summed, QUAD * ((u - RING) // QUAD + 1))
                nc.scalar.activation(probs[:, u % RING, :], banks_b[u % 2], ACT.Exp, scale=scale).then_inc(exped, 1)
                if u % QUAD_TILES in (2, 4) and u >= QUAD_TILES:
                    take(act, u // QUAD_TILES - 1, u % QUAD_TILES // 4)
            for c in range(2):
                take(act, n_quads - 1, c)



E1_HID = 256
E1_COLS = 3 * E1_HID


def experts_swiglu(kit, name, landed, xn, weights, blocks, up, gate, down, gates, acts):
    nc = kit.nc
    steps = [(m, c) for m in range(blocks) for c in range(NC)]
    with Stage(kit, name) as st:
        product, silu_done, gated, weighted = map(st.sem, ("product", "silu", "gated", "weighted"))
        block = st.block()

        def weight(a):
            return kit.experts[:, a:a + P]

        @block.tensor
        def _(pe):
            pe.wait_ge(landed, 16)
            for i in range(len(steps) + 2):
                if i < len(steps):
                    m, c = steps[i]
                    if i >= 2:
                        pe.wait_ge(gated, i - 1)
                    nc.tensor.matmul(kit.bank(2 * (i % 2)), weight(gate(m)), kit.chunk(xn, c), start=True, stop=True)
                    nc.tensor.matmul(kit.bank(2 * (i % 2) + 1), weight(up(m)), kit.chunk(xn, c), start=True,
                                     stop=True).then_inc(product, 1)
                if i >= 2:
                    m, c = steps[i - 2]
                    if weights(m) is None:
                        pe.wait_ge(gated, i - 1)
                    else:
                        pe.wait_ge(weighted, i - 1)
                    nc.tensor.matmul(kit.bank(4 + c), weight(down(m)), kit.chunk(acts, (i - 2) % 4), start=m == 0,
                                     stop=m == blocks - 1)

        @block.scalar
        def _(act):
            for i, (m, c) in enumerate(steps):
                act.wait_ge(product, i + 1)
                if i >= 4:
                    act.wait_ge(gated, i - 2)
                nc.scalar.activation(kit.chunk(gates, i % 4), kit.bank(2 * (i % 2)), ACT.Silu).then_inc(silu_done, 1)

        @block.vector
        def _(dve):
            for i, (m, c) in enumerate(steps):
                dve.wait_ge(silu_done, i + 1)
                w = weights(m)
                nc.vector.tensor_tensor(kit.chunk(gates, i % 4) if w is not None else kit.chunk(acts, i % 4), kit.chunk(gates, i % 4),
                                        kit.bank(2 * (i % 2) + 1), ALU.mult).then_inc(gated, 1)
                if w is not None:
                    dve.wait_ge(gated, i + 1)
                    nc.vector.tensor_tensor(kit.chunk(acts, i % 4), kit.chunk(gates, i % 4), kit.chunk(w, c), ALU.mult).then_inc(weighted, 1)



def norm_attention(kit, name, xn, out, square, scaled, q, tq, values, probs, turned, result):
    nc = kit.nc
    norm, inv, row_scale = (kit.scratch[:, a:a + NT] for a in (0, 16, 32))
    neg_max, row_sum, inv_sum = (kit.scratch[:, a:a + NT] for a in (48, 64, 80))
    diag = kit.slot(square).rearrange("p (j q) -> p j q", q=P)
    with Stage(kit, name + "_rows") as st:
        squared, sum_ready, norm_ready, diag_ready, bcast_ready, own = map(st.sem, ("squared", "sum", "norm", "diag", "bcast", "own"))
        block = st.block()

        @block.tensor
        def _(pe):
            for j in range(NT):
                pe.wait_ge(squared, j // 4 + 1)
                last = nc.tensor.matmul(kit.psum[:, 4, j:j + 1], kit.slot(square)[:, j * P:(j + 1) * P],
                                        kit.c("ones")[:, 0:1], start=True, stop=True)
            last.then_inc(sum_ready, 1)
            pe.wait_ge(diag_ready, 1)
            for c in range(NC):
                nc.tensor.matmul(kit.bank(c), kit.c("ones"), kit.chunk(square, c), start=True, stop=True).then_inc(bcast_ready, 1)

        @block.scalar
        def _(act):
            for c in range(NC):
                nc.scalar.activation(kit.chunk(square, c), kit.chunk(xn, c), ACT.Square).then_inc(squared, 1)
            act.wait_ge(sum_ready, 1)
            nc.scalar.activation(norm, kit.psum[:, 4, 0:NT], ACT.Sqrt).then_inc(norm_ready, 1)

        @block.vector
        def _(dve):
            dve.wait_ge(norm_ready, 1)
            nc.vector.tensor_scalar(inv, norm, 1e-9, None, ALU.add).then_inc(own, 1)
            dve.wait_ge(own, 1)
            nc.vector.reciprocal(inv, inv).then_inc(own, 1)
            dve.wait_ge(own, 2)
            nc.vector.tensor_tensor(diag, kit.c("ident").unsqueeze(1).broadcast_to([P, NT, P]), spread(inv, P),
                                    ALU.mult).then_inc(diag_ready, 1)
            for c in range(NC):
                dve.wait_ge(bcast_ready, c + 1)
                nc.vector.tensor_tensor(kit.chunk(scaled, c), kit.chunk(xn, c), kit.bank(c), ALU.mult)

    project(kit, name + "_q", [(q, "q2", scaled, "bq2", None)])
    project(kit, name + "_tq", [(tq, "anomaly", q, None, None)])
    scale = 1.0 / float(np.sqrt(np.float32(P)))
    v = kit.slot(values).rearrange("p (j n) -> p j n", n=P)
    p_ring = kit.slot(probs).rearrange("p (r t) -> p r t", t=SEQ)
    pt_ring = kit.slot(turned).rearrange("p (r t) -> p r t", t=SEQ)
    res = kit.slot(result).rearrange("p (j n) -> p j n", n=P)
    with Stage(kit, name + "_v") as st:
        v_ready = st.sem("v")
        block = st.block()

        @block.tensor
        def _(pe):
            for j in range(NT):
                nc.tensor.matmul(kit.bank(j // 4)[:, (j % 4) * P:(j % 4 + 1) * P], kit.slot(scaled)[:, j * P:(j + 1) * P],
                                 kit.w("v2"), start=True, stop=True).then_inc(v_ready, 1)

        @block.vector
        def _(dve):
            for g in range(4):
                dve.wait_ge(v_ready, 4 * g + 4)
                nc.vector.tensor_tensor(v[:, 4 * g:4 * g + 4, :], kit.bank(g).rearrange("p (j n) -> p j n", n=P),
                                        kit.w("bv2").unsqueeze(1).broadcast_to([P, 4, P]), ALU.add)

    with Stage(kit, name) as st:
        scores, maxed, bias_ready, exped, p_turned = map(st.sem, ("scores", "maxed", "bias", "exped", "p_turned"))
        pt_copied, ctx_ready, ctx_scaled, ctx_turned, copied, own = map(st.sem, ("pt", "ctx", "ctx_scaled", "ctx_turned", "copied", "own"))
        block = st.block()

        @block.tensor
        def _(pe):
            for i in range(NT + 3):
                if i < NT:
                    if i >= 2:
                        pe.wait_ge(exped, i - 1)
                    a = i // KT * SEQ
                    for c in range(2):
                        last = nc.tensor.matmul(kit.bank(2 * (i % 2) + c), kit.slot(q)[:, i * P:(i + 1) * P],
                                                kit.slot(tq)[:, a + c * CH:a + (c + 1) * CH], start=True, stop=True)
                    last.then_inc(scores, 1)
                if 1 <= i <= NT:
                    t = i - 1
                    pe.wait_ge(exped, t + 1)
                    if t >= 1:
                        pe.wait_ge(pt_copied, t)
                    for n in range(KT):
                        last = nc.tensor.transpose(kit.bank(4 + n // 4)[:, (n % 4) * P:(n % 4 + 1) * P],
                                                   p_ring[:, t % 2, n * P:(n + 1) * P], kit.c("ident"))
                    last.then_inc(p_turned, 1)
                if 2 <= i <= NT + 1:
                    t = i - 2
                    pe.wait_ge(pt_copied, t + 1)
                    if t >= 1:
                        pe.wait_ge(ctx_scaled, t)
                    for n in range(KT):
                        last = nc.tensor.matmul(kit.bank(6)[:, 0:P], pt_ring[:, t % 2, n * P:(n + 1) * P],
                                                v[:, t // KT * KT + n, :], start=n == 0, stop=n == KT - 1)
                    last.then_inc(ctx_ready, 1)
                if i >= 3:
                    t = i - 3
                    pe.wait_ge(ctx_scaled, t + 1)
                    if t >= 1:
                        pe.wait_ge(copied, t)
                    nc.tensor.transpose(kit.bank(7)[:, 0:P], res[:, t, :], kit.c("ident")).then_inc(ctx_turned, 1)

        @block.scalar
        def _(act):
            for i in range(NT + 3):
                if i < NT:
                    act.wait_ge(bias_ready, i + 1)
                    if i >= 2:
                        act.wait_ge(p_turned, i - 1)
                    nc.scalar.activation(p_ring[:, i % 2, :], kit.psum[:, 2 * (i % 2):2 * (i % 2) + 2, :].rearrange("p a b -> p (a b)"),
                                         ACT.Exp, bias=neg_max[:, i:i + 1], scale=scale, accum_out=row_sum[:, i:i + 1]).then_inc(exped, 1)
                if i >= 3:
                    t = i - 3
                    act.wait_ge(ctx_turned, t + 1)
                    nc.scalar.activation(kit.slot(out)[:, t * P:(t + 1) * P], kit.bank(7)[:, 0:P], ACT.Copy).then_inc(copied, 1)

        @block.vector
        def _(dve):
            for i in range(NT + 2):
                if i < NT:
                    dve.wait_ge(scores, i + 1)
                    nc.vector.tensor_reduce(neg_max[:, i:i + 1], kit.psum[:, 2 * (i % 2):2 * (i % 2) + 2, :].rearrange("p a b -> p (a b)"),
                                            AX.X, ALU.max, negate=True).then_inc(maxed, 1)
                    dve.wait_ge(maxed, i + 1)
                    nc.vector.tensor_scalar(neg_max[:, i:i + 1], neg_max[:, i:i + 1], scale, None, ALU.mult).then_inc(bias_ready, 1)
                if 1 <= i <= NT:
                    t = i - 1
                    dve.wait_ge(p_turned, t + 1)
                    if t >= 2:
                        dve.wait_ge(ctx_ready, t - 1)
                    nc.vector.tensor_copy(pt_ring[:, t % 2, :], kit.psum[:, 4:6, :].rearrange("p a b -> p (a b)")).then_inc(pt_copied, 1)
                if i >= 2:
                    t = i - 2
                    dve.wait_ge(ctx_ready, t + 1)
                    dve.wait_ge(exped, t + 1)
                    nc.vector.reciprocal(inv_sum[:, t:t + 1], row_sum[:, t:t + 1]).then_inc(own, 1)
                    dve.wait_ge(own, t + 1)
                    nc.vector.tensor_scalar(res[:, t, :], kit.bank(6)[:, 0:P], inv_sum[:, t:t + 1], norm[:, t:t + 1],
                                            ALU.mult, ALU.mult).then_inc(ctx_scaled, 1)



def wkv_inputs(kit, name, xn, xx, r, kk, v_in, g, w, v, mix, t0, t1):
    nc = kit.nc
    mixes = flat_slots(kit, mix, 5)
    with Stage(kit, name + "_mix") as st:
        own, mix_ready, tanh_ready = map(st.sem, ("own", "mix", "tanh"))
        m_ready, m_used = st.sem("m"), st.sem("m_used")
        block = st.block()
        targets = (w, kk, v_in, r, g)

        @block.vector
        def _(dve):
            for b in range(BATCH):
                a, z = b * SEQ, (b + 1) * SEQ
                nc.vector.tensor_tensor(kit.slot(xx)[:, a + 1:z], kit.slot(xn)[:, a:z - 1], kit.slot(xn)[:, a + 1:z], ALU.subtract)
                nc.vector.tensor_scalar(kit.slot(xx)[:, a:a + 1], kit.slot(xn)[:, a:a + 1], -1.0, None, ALU.mult).then_inc(own, 1)
            dve.wait_ge(own, 2)
            nc.vector.scalar_tensor_tensor(kit.slot(t0), kit.slot(xx), kit.w("maa_x"), kit.slot(xn), ALU.mult, ALU.add).then_inc(own, 1)
            for n in range(5 * NC):
                s, c = n // NC, n % NC
                dve.wait_ge(m_ready, n + 1)
                nc.vector.scalar_tensor_tensor(kit.chunk(targets[s], c), kit.bank(4 + n % 4), kit.w("maa")[:, s:s + 1], kit.chunk(xx, c),
                                               ALU.add, ALU.mult).then_inc(m_used, 1)
                dve.wait_ge(m_used, n + 1)
                nc.vector.tensor_tensor(kit.chunk(targets[s], c), kit.chunk(targets[s], c), kit.chunk(xn, c), ALU.add)

        @block.tensor
        def _(pe):
            pe.wait_ge(own, 3)
            for n in range(5 * NC + 4):
                if n < 5 * NC:
                    s, c = n // NC, n % NC
                    if n >= 4:
                        pe.wait_ge(tanh_ready, n - 3)
                    nc.tensor.matmul(kit.bank(n % 4)[0:32], kit.w("maa_w1")[:, 32 * s:32 * s + 32], kit.chunk(t0, c),
                                     start=True, stop=True).then_inc(mix_ready, 1)
                if n >= 4:
                    k = n - 4
                    s, c = k // NC, k % NC
                    pe.wait_ge(tanh_ready, k + 1)
                    if k >= 4:
                        pe.wait_ge(m_used, k - 3)
                    nc.tensor.matmul(kit.bank(4 + k % 4), kit.w("maa_w2")[:, P * s:P * s + P],
                                     mixes[0:32, k * CH:(k + 1) * CH], start=True, stop=True).then_inc(m_ready, 1)

        @block.scalar
        def _(act):
            for n in range(5 * NC):
                act.wait_ge(mix_ready, n + 1)
                nc.scalar.activation(mixes[0:32, n * CH:(n + 1) * CH], kit.bank(n % 4)[0:32], ACT.Tanh).then_inc(tanh_ready, 1)

    with Stage(kit, name + "_decay") as st:
        low, tanh_done, full, exp_done = map(st.sem, ("low", "tanh", "full", "exp"))
        block = st.block()

        @block.tensor
        def _(pe):
            for c in range(NC):
                nc.tensor.matmul(kit.bank(c)[0:64], kit.w("decay_w1"), kit.chunk(w, c), start=True, stop=True).then_inc(low, 1)
            for c in range(NC):
                pe.wait_ge(tanh_done, c + 1)
                nc.tensor.matmul(kit.bank(4 + c), kit.w("decay_w2"), kit.chunk(t1, c)[0:64], start=True, stop=True).then_inc(full, 1)

        @block.scalar
        def _(act):
            for c in range(NC):
                act.wait_ge(low, c + 1)
                nc.scalar.activation(kit.chunk(t1, c)[0:64], kit.bank(c)[0:64], ACT.Tanh).then_inc(tanh_done, 1)
            for c in range(NC):
                act.wait_ge(full, c + 1)
                nc.scalar.activation(kit.chunk(w, c), kit.bank(4 + c), ACT.Exp, bias=kit.w("decay")).then_inc(exp_done, 1)
                act.wait_ge(exp_done, 2 * c + 1)
                nc.scalar.activation(kit.chunk(w, c), kit.chunk(w, c), ACT.Exp, scale=-1.0).then_inc(exp_done, 1)

    project(kit, name + "_rkvg", [(r, "Wr", r, None, None), (kk, "Wk", kk, None, None), (v, "Wv", v_in, None, None),
                                  (g, "Wg", g, None, None)])


def wkv(kit, name, r, kk, v_in, v, w, y, rd, t0, t1, head_decay, tail_decay, key_even, key_odd, v_tok, states):
    nc = kit.nc

    def by_chunk(slot):
        return kit.slot(slot).rearrange("p (n t) -> p n t", t=WC)

    R, K, V, W_, Y, RD, T0, T1 = map(by_chunk, (r, kk, v, w, y, rd, t0, t1))
    PER = NWC // NC

    with Stage(kit, name + "_near") as st:
        pair, spread_ready, used, own = map(st.sem, ("pair", "spread", "used", "own"))
        e_free = st.sem("e_free")
        block = st.block()

        @block.vector
        def _(dve):
            done = [0]

            def then(instruction):
                done[0] += 1
                instruction.then_inc(own, 1)
                dve.wait_ge(own, done[0])

            def produce(d):
                T = (T0, T1)[d % 2]
                if d == 0:
                    nc.vector.scalar_tensor_tensor(T[:, :, :], R[:, :, :], kit.w("faaaa"), K[:, :, :], ALU.mult, ALU.mult).then_inc(pair, 1)
                    return
                if d == 1:
                    then(nc.vector.tensor_copy(RD[:, :, 1:], R[:, :, 1:]))
                else:
                    then(nc.vector.tensor_tensor(RD[:, :, d:], RD[:, :, d:], W_[:, :, 1:WC - d + 1], ALU.mult))
                nc.vector.tensor_tensor(T[:, :, d:], RD[:, :, d:], K[:, :, 0:WC - d], ALU.mult).then_inc(pair, 1)

            produce(0)
            for d in range(WC):
                dve.wait_ge(spread_ready, d + 1)
                if d + 1 < WC:
                    produce(d + 1)
                n = WC - d
                bank = kit.psum[:, 4 * (d % 2):4 * (d % 2) + 4, 0:PER * n].rearrange("p b (m t) -> p b m t", t=n)
                T = (T0, T1)[d % 2]
                Tv, Vv = (kit_slot.rearrange("p (b m) t -> p b m t", b=NC) for kit_slot in (T[:, :, d:], V[:, :, 0:n]))
                for b in range(NC):
                    last = nc.vector.tensor_tensor(Tv[:, b], bank[:, b], Vv[:, b], ALU.mult)
                last.then_inc(used, 1)
                dve.wait_ge(used, d + 1)
                if d == 0:
                    nc.vector.tensor_copy(kit.slot(y), kit.slot(t0))
                else:
                    nc.vector.tensor_tensor(Y[:, :, d:], Y[:, :, d:], T[:, :, d:], ALU.add)

        @block.tensor
        def _(pe):
            for d in range(WC):
                n = WC - d
                T = (T0, T1)[d % 2]
                pe.wait_ge(pair, d + 1)
                if d >= 2:
                    pe.wait_ge(used, d - 1)
                for c in range(NC):
                    last = nc.tensor.matmul(kit.bank(4 * (d % 2) + c)[:, 0:PER * n], kit.c("head_ones"),
                                            T[:, c * PER:(c + 1) * PER, d:], start=True, stop=True)
                last.then_inc(spread_ready, 1)

    HD, TD = by_chunk(head_decay), by_chunk(tail_decay)
    ke = kit.slot(key_even).rearrange("p (j n) -> p j n", n=P)
    ko = kit.slot(key_odd).rearrange("p (j n) -> p j n", n=P)
    vt = kit.slot(v_tok).rearrange("p (j n) -> p j n", n=P)
    whole = kit.scratch[:, 0:NWC]
    with Stage(kit, name + "_far") as st:
        own, turned, turned_used, v_ready, keys_ready = map(st.sem, ("own", "turned", "turned_used", "v", "keys"))
        block = st.block()

        @block.vector
        def _(dve):
            done = [0]

            def then(instruction):
                done[0] += 1
                instruction.then_inc(own, 1)
                dve.wait_ge(own, done[0])

            then(nc.vector.tensor_copy(T0[:, :, 1:], W_[:, :, 0:WC - 1]))
            then(nc.vector.memset(T0[:, :, 0:1], 0.0))
            starts = kit.c("start").unsqueeze(1).broadcast_to([P, NWC, WC])
            then(nc.vector.tensor_copy(T1[:, :, :], starts))
            then(nc.vector.tensor_tensor_scan(kit.slot(head_decay), kit.slot(t0), kit.slot(t1), 0.0, ALU.mult, ALU.add))
            nc.vector.tensor_tensor(whole.unsqueeze(2), HD[:, :, WC - 1:WC], W_[:, :, WC - 1:WC], ALU.mult)
            then(nc.vector.tensor_tensor(kit.slot(rd), kit.slot(r), kit.slot(head_decay), ALU.mult))
            then(nc.vector.tensor_copy(T0[:, :, 0:WC - 1], W_[:, :, 1:WC]))
            then(nc.vector.memset(T0[:, :, WC - 1:WC], 0.0))
            then(nc.vector.tensor_copy(T1[:, :, ::-1], starts))
            then(nc.vector.tensor_tensor_scan(kit.slot(tail_decay)[:, ::-1], kit.slot(t0)[:, ::-1], kit.slot(t1)[:, ::-1],
                                              0.0, ALU.mult, ALU.add))
            nc.vector.tensor_tensor(kit.slot(kk), kit.slot(kk), kit.slot(tail_decay), ALU.mult).then_inc(keys_ready, 1)
            for g in range(4):
                dve.wait_ge(turned, 4 * g + 4)
                bank = kit.bank(g).rearrange("p (j n) -> p j n", n=P)
                nc.vector.tensor_scalar(ke[:, 4 * g:4 * g + 4, :], bank, kit.c("even"), None, ALU.mult)
                nc.vector.tensor_scalar(ko[:, 4 * g:4 * g + 4, :], bank, kit.c("odd"), None, ALU.mult)

        @block.tensor
        def _(pe):
            for j in range(NT):
                nc.tensor.matmul(kit.bank(4 + j // 4)[:, (j % 4) * P:(j % 4 + 1) * P], kit.slot(v_in)[:, j * P:(j + 1) * P],
                                 kit.w("Wv"), start=True, stop=True).then_inc(v_ready, 1)
            pe.wait_ge(keys_ready, 1)
            for j in range(NT):
                nc.tensor.transpose(kit.bank(j // 4)[:, (j % 4) * P:(j % 4 + 1) * P], kit.slot(kk)[:, j * P:(j + 1) * P],
                                    kit.c("ident")).then_inc(turned, 1)

        @block.scalar
        def _(act):
            for g in range(4):
                act.wait_ge(v_ready, 4 * g + 4)
                nc.scalar.activation(vt[:, 4 * g:4 * g + 4, :], kit.bank(4 + g).rearrange("p (j n) -> p j n", n=P), ACT.Copy)

    state = flat_slots(kit, states, 4).rearrange("p (n i) -> p n i", i=WKV_HEAD)
    GROUP = 8
    with Stage(kit, name + "_state") as st:
        kv_ready, state_ready, first_state, state_own = map(st.sem, ("kv", "state", "first", "state_own"))
        block = st.block()

        def kv(j, n):
            return kit.bank(4 * (j % 2) + n // 2)[:, 64 * (n % 2):64 * (n % 2) + 64]

        @block.tensor
        def _(pe):
            for j in range(NT):
                if j >= 2:
                    pe.wait_ge(state_ready, j - 1)
                for n in range(GROUP):
                    rows = slice(32 * (n // 2), 32 * (n // 2) + 32)
                    keys = (ke, ko)[n % 2]
                    for h in range(2):
                        head = slice(64 * h, 64 * h + 64)
                        last = nc.tensor.matmul(kv(j, n)[head], keys[rows, j, head], vt[rows, j, head], start=True, stop=True)
                last.then_inc(kv_ready, 1)

        @block.vector
        def _(dve):
            own = 0
            for b in range(BATCH):
                nc.vector.memset(state[:, b * (NWC // 2), :], 0.0).then_inc(first_state, 1)
            dve.wait_ge(first_state, BATCH)
            for j in range(NT):
                dve.wait_ge(kv_ready, j + 1)
                final = GROUP - 2 if (j + 1) % KT == 0 else GROUP - 1
                for n in range(final + 1):
                    c = j * GROUP + n
                    update = nc.vector.scalar_tensor_tensor(state[:, c + 1, :], state[:, c, :], whole[:, c:c + 1],
                                                            kv(j, n), ALU.mult, ALU.add)
                    if n < final:
                        update.then_inc(state_own, 1)
                        own += 1
                        dve.wait_ge(state_own, own)
                    else:
                        update.then_inc(state_ready, 1)
                        dve.wait_ge(state_ready, j + 1)

    with Stage(kit, name + "_read") as st:
        y_ready = st.sem("y")
        block = st.block()

        @block.tensor
        def _(pe):
            for c in range(NC):
                for n in range(PER):
                    for h in range(2):
                        rows = slice(64 * h, 64 * h + 64)
                        last = nc.tensor.matmul(kit.bank(c)[rows, n * WC:n * WC + WC], state[rows, c * PER + n, :],
                                                kit.chunk(rd, c)[rows, n * WC:n * WC + WC], start=True, stop=True)
                last.then_inc(y_ready, 1)

        @block.vector
        def _(dve):
            for c in range(NC):
                dve.wait_ge(y_ready, c + 1)
                nc.vector.tensor_tensor(kit.chunk(y, c), kit.chunk(y, c), kit.bank(c), ALU.add)


def group_norm(kit, name, y, square, stat, g):
    nc = kit.nc
    with Stage(kit, name) as st:
        mean_ready, centered, squared, var_ready, std_ready, own = map(st.sem, ("mean", "centered", "squared", "var", "std", "own"))
        silu_done = st.sem("silu")
        block = st.block()

        @block.tensor
        def _(pe):
            for c in range(NC):
                nc.tensor.matmul(kit.bank(c), kit.c("head_mean"), kit.chunk(y, c), start=True, stop=True).then_inc(mean_ready, 1)
            for c in range(NC):
                pe.wait_ge(squared, c + 1)
                nc.tensor.matmul(kit.bank(4 + c), kit.c("head_mean"), kit.chunk(square, c), start=True, stop=True).then_inc(var_ready, 1)

        @block.scalar
        def _(act):
            for c in range(NC):
                act.wait_ge(centered, c + 1)
                nc.scalar.activation(kit.chunk(square, c), kit.chunk(y, c), ACT.Square).then_inc(squared, 1)
            for c in range(NC):
                act.wait_ge(var_ready, c + 1)
                nc.scalar.activation(kit.chunk(stat, c), kit.bank(4 + c), ACT.Sqrt, bias=kit.c("eps_wkv")).then_inc(std_ready, 1)
            for c in range(NC):
                nc.scalar.activation(kit.chunk(g, c), kit.chunk(g, c), ACT.Silu).then_inc(silu_done, 1)

        @block.vector
        def _(dve):
            done = [0]

            def then(instruction):
                done[0] += 1
                instruction.then_inc(own, 1)
                dve.wait_ge(own, done[0])

            for c in range(NC):
                dve.wait_ge(mean_ready, c + 1)
                nc.vector.tensor_tensor(kit.chunk(y, c), kit.chunk(y, c), kit.bank(c), ALU.subtract).then_inc(centered, 1)
            for c in range(NC):
                dve.wait_ge(std_ready, c + 1)
                then(nc.vector.reciprocal(kit.chunk(stat, c), kit.chunk(stat, c)))
                then(nc.vector.scalar_tensor_tensor(kit.chunk(y, c), kit.chunk(y, c), kit.w("ln_w"), kit.chunk(stat, c), ALU.mult, ALU.mult))
                dve.wait_ge(silu_done, c + 1)
                nc.vector.scalar_tensor_tensor(kit.chunk(y, c), kit.chunk(y, c), kit.w("ln_b"), kit.chunk(g, c), ALU.add, ALU.mult)



E3_COLS = HID + HB * P
E3_RING = 6


def experts_relu(kit, name, dram, landed, xn, weights, rows, hidden_slots):
    nc = kit.nc
    n_exp = 8
    steps = [(e, c) for e in range(n_exp) for c in range(NC)]

    def w1(e, m):
        a = e % E3_RING * E3_COLS + m * P
        return kit.experts[:, a:a + P]

    def w2(e, k):
        return w1(e, HB + k)

    with Stage(kit, name) as st:
        hidden, relu_done, weighted, expert_done = map(st.sem, ("hidden", "relu", "weighted", "expert_done"))
        block = st.block()

        @block.sync
        def _(sp):
            for e in range(E3_RING, n_exp):
                r = e % E3_RING
                sp.wait_ge(expert_done, e - E3_RING + 1)
                sp.dma_start(kit.experts[:, r * E3_COLS:(r + 1) * E3_COLS], dram[e]).then_inc(landed[r], 16)

        @block.tensor
        def _(pe):
            for i in range(len(steps) + 1):
                if i < len(steps):
                    e, c = steps[i]
                    if c == 0:
                        pe.wait_ge(landed[e % E3_RING], 16 * (e // E3_RING + 1))
                    for m in range(HB):
                        if i >= 1:
                            pe.wait_ge(relu_done, HB * (i - 1) + m + 1)
                        nc.tensor.matmul(kit.bank(m), w1(e, m), kit.chunk(xn, c), start=True, stop=True).then_inc(hidden, 1)
                if i >= 1:
                    e, c = steps[i - 1]
                    pe.wait_ge(weighted, i)
                    if e == 0:
                        nc.tensor.matmul(kit.bank(4 + c), kit.w("f_b2"), kit.chunk(rows, c)[0:n_exp], start=True, stop=False)
                    for k in range(HB):
                        last = nc.tensor.matmul(kit.bank(4 + c), w2(e, k), kit.chunk(hidden_slots[(i - 1) % 2], k), start=False,
                                                stop=e == n_exp - 1 and k == HB - 1)
                    if c == NC - 1:
                        last.then_inc(expert_done, 1)

        @block.scalar
        def _(act):
            for i, (e, c) in enumerate(steps):
                for m in range(HB):
                    act.wait_ge(hidden, HB * i + m + 1)
                    nc.scalar.activation(kit.chunk(hidden_slots[i % 2], m), kit.bank(m), ACT.Relu,
                                         bias=kit.w("f_b1")[:, HB * e + m:HB * e + m + 1]).then_inc(relu_done, 1)

        @block.vector
        def _(dve):
            for i, (e, c) in enumerate(steps):
                dve.wait_ge(relu_done, HB * (i + 1))
                h = kit.slot(hidden_slots[i % 2]).rearrange("p (m t) -> p m t", t=CH)
                nc.vector.tensor_tensor(h, h, kit.chunk(weights[e], c).unsqueeze(1).broadcast_to([P, HB, CH]),
                                        ALU.mult).then_inc(weighted, 1)


def add_banks(kit, name, dst, a):
    nc = kit.nc
    with Stage(kit, name) as st:
        block = st.block()

        @block.vector
        def _(dve):
            nc.vector.tensor_tensor(kit.slot(dst), kit.slot(a), kit.psum[:, 4:8, :].rearrange("p a b -> p (a b)"), ALU.add)



X, XN, RES = 0, 1, 2
WEIGHTS = list(range(5, 13))
SEL_SLOT = 15


def layer0(kit, dram, arrivals):
    landed = arrivals.experts[0]
    start_experts(kit, "x0", [dram[0], dram[1]], E0_COLS, landed)
    layer_norm(kit, "n0", X, XN, 3, 4)
    await_small(kit, arrivals)
    weights = [kit.slot(3 + e // 2).bitcast(BF16)[:, e % 2 * TOK:(e % 2 + 1) * TOK] for e in range(N_EXP0)]
    router(kit, "r0", XN, "tokens", None, 8, "half", rows=7, stacked=8, work=9, tmp=10)
    cast_selectors(kit, arrivals, SEL_SLOT)
    spread_rows(kit, "sp0", 8, range(8), weights)
    scan_inputs(kit, XN, low=14, delta=7, du=13, suffix=11, y=12, rows=15, tmp=16)
    halves = flat_slots(kit, 15, 3)
    experts_and_scan(kit, dram, landed, XN, weights, acc=2, h1=[7, 8], h2=[9, 10], stacked=14, du=13, suffix=11, y=12,
                     halves=[halves[:, a * SEQ:(a + 1) * SEQ] for a in range(5)])
    project(kit, "scan_out", [(3, "W_out", 12, "b_out", None)])
    merge(kit, "m0", X, 3, 4, g=2)


def layer1(kit, dram, landed):
    layer_norm(kit, "n1", X, XN, 3, 4)
    attention(kit, "a1", XN, ("q1", "k1", "v1", None, None), RES, q_stack=3, k_stack=6, sums=9, values=11, work=13)
    start_experts(kit, "x1", [dram], 8 * E1_COLS, landed)
    project(kit, "o1", [(3, "o1", RES, None, XN)])
    router(kit, "r1", XN, "gate1", None, 8, "scores", rows=2, stacked=4, work=5, tmp=6)
    spread_rows(kit, "sp1", 4, range(8), [kit.slot(i) for i in WEIGHTS])
    experts_swiglu(kit, "e1", landed[0], XN, lambda m: WEIGHTS[m // 2], 16,
                   up=lambda m: m // 2 * E1_COLS + E1_HID + m % 2 * P, gate=lambda m: m // 2 * E1_COLS + m % 2 * P,
                   down=lambda m: m // 2 * E1_COLS + 2 * E1_HID + m % 2 * P, gates=13, acts=14)
    merge(kit, "m1", X, 3, 13)


def layer2(kit, dram, landed):
    start_experts(kit, "x2", [dram], 27 * P, landed)
    layer_norm(kit, "n2", X, XN, 3, 4)
    norm_attention(kit, "a2", XN, RES, 3, 4, 5, 6, 7, 8, 9, 10)
    router(kit, "r2", XN, "router", "router_bias", 16, "top", rows=3, stacked=4, work=5, tmp=6)
    spread_rows(kit, "sp2", 4, range(32, 40), [kit.slot(i) for i in WEIGHTS])
    experts_swiglu(kit, "e2", landed[0], XN, lambda m: WEIGHTS[m] if m < 8 else None, 9,
                   up=lambda m: (m if m < 8 else 25) * P, gate=lambda m: (8 + m if m < 8 else 24) * P,
                   down=lambda m: (16 + m if m < 8 else 26) * P, gates=13, acts=14)
    merge(kit, "m2", X, RES, 13)


def layer3(kit, dram, landed):
    layer_norm(kit, "n3", X, XN, 3, 4)
    wkv_inputs(kit, "w3", XN, xx=2, r=3, kk=4, v_in=5, g=6, w=7, v=8, mix=9, t0=14, t1=15)
    wkv(kit, "w3", r=3, kk=4, v_in=5, v=8, w=7, y=9, rd=2, t0=10, t1=11, head_decay=12, tail_decay=13, key_even=14,
        key_odd=15, v_tok=16, states=10)
    group_norm(kit, "gn", 9, 3, 4, 6)
    project(kit, "o3", [(RES, "Wo", 9, None, None)])

    layer_norm(kit, "f1", XN, 3, 4, 5, "ln1_g", "ln1_b")
    attention(kit, "a3", 3, ("q3", "k3", "v3", "bq3", "bk3"), 3, q_stack=4, k_stack=7, sums=10, values=12, work=14)
    start_experts(kit, "x3", [dram[e] for e in range(E3_RING)], E3_COLS, landed)
    add_bias(kit, "bv", 3, "bv3")
    project(kit, "fo", [(5, "o3", 3, "bo3", XN)])
    layer_norm(kit, "f2", 5, 3, 6, 7, "ln2_g", "ln2_b")
    router(kit, "r3", 3, "gate3", "gate_b3", 8, "first", rows=6, stacked=7, work=8, tmp=9)
    spread_rows(kit, "sp3", 7, range(8), [kit.slot(i) for i in range(8, 16)])
    experts_relu(kit, "e3", dram, landed, 3, list(range(8, 16)), 6, [16, 17])
    add_banks(kit, "fg", 4, 5)
    merge(kit, "m3", X, RES, 6, g=4)


def add_bias(kit, name, slot, bias):
    nc = kit.nc
    with Stage(kit, name) as st:
        block = st.block()

        @block.vector
        def _(dve):
            nc.vector.tensor_scalar(kit.slot(slot), kit.slot(slot), kit.w(bias), None, ALU.add)


def allocate(nc, ctx):
    def sb(name, shape, dt=F32):
        return ctx.enter_context(nc.sbuf_tensor(name, shape, dt))

    return Kit(nc, sb("slots", [P, SLOTS, TOK]), sb("small_sb", [P, SMALL.width]), sb("consts_sb", [P, CONSTS.width]),
               sb("experts", [P, EXPERT_COLS]), sb("sel_sb", [96, 40, P], BF16),
               ctx.enter_context(nc.psum_tensor("psum", [P, 8, CH], F32)), sb("scratch", [P, 1024]))


EXPERT_COLS = 6144


def recurrent_layers(nc, x, small, consts, sel, experts0, experts1, experts2, experts3, out):
    with ExitStack() as ctx:
        kit = allocate(nc, ctx)
        stored = ctx.enter_context(nc.semaphore("stored"))
        arrivals = Arrivals(nc, ctx)
        load_inputs(kit, arrivals, x, small, consts, sel, X, SEL_SLOT)
        layer0(kit, experts0, arrivals)
        layer1(kit, experts1, arrivals.experts[1])
        layer2(kit, experts2, arrivals.experts[2])
        layer3(kit, experts3, arrivals.experts[3])
        store_output(kit, out, X, stored)



def rows128(a, p=128):
    out = np.zeros((128, a.shape[1]), a.dtype)
    out[:a.shape[0]] = a
    return out


def column(v):
    return np.reshape(v, (-1, 1))


def tiles(a):
    k = a.shape[0] // 128
    return np.reshape(np.transpose(np.reshape(a, (k, 128, a.shape[1])), (1, 0, 2)), (128, -1))


def small_weights(i):
    w = {
        "W_x": i["L0_attn_W_x"], "W_dt": i["L0_attn_W_dt"], "W_out": i["L0_attn_W_out"], "A_log": i["L0_attn_A_log"],
        "b_dt": column(i["L0_attn_b_dt"]), "D": column(i["L0_attn_D"]), "b_out": column(i["L0_attn_b_out"]),
        "tokens": i["L0_ffn_expert_tokens"].T,
        "e_b1": np.reshape(i["L0_ffn_b1"], (32, 128)).T, "e_b2": np.reshape(i["L0_ffn_b2"], (32, 128)).T,
        "e_b3": i["L0_ffn_b3"].T,
        "q1": i["L1_attn_Wq"], "k1": i["L1_attn_Wk"], "v1": i["L1_attn_Wv"], "o1": i["L1_attn_Wout"],
        "gate1": i["L1_ffn_gate_w"].T,
        "q2": i["L2_attn_Wq"].T, "v2": i["L2_attn_Wv"].T, "anomaly": i["L2_attn_anomaly_matrix"],
        "bq2": column(i["L2_attn_bq"]), "bv2": np.tile(i["L2_attn_bv"], (128, 1)),
        "router": i["L2_ffn_router_w"].T, "router_bias": np.tile(i["L2_ffn_router_bias"], (128, 1)),
        "maa_x": column(i["L3_attn_time_maa_x"]),
        "maa": np.stack([i[f"L3_attn_time_maa_{s}"] for s in "wkvrg"], 1),
        "maa_w1": i["L3_attn_time_maa_w1"],
        "maa_w2": np.reshape(np.transpose(i["L3_attn_time_maa_w2"], (1, 0, 2)), (32, 640)),
        "decay_w1": i["L3_attn_time_decay_w1"], "decay_w2": i["L3_attn_time_decay_w2"],
        "decay": column(i["L3_attn_time_decay"]), "faaaa": column(i["L3_attn_time_faaaa"]),
        "Wr": i["L3_attn_Wr"], "Wk": i["L3_attn_Wk"], "Wv": i["L3_attn_Wv"], "Wg": i["L3_attn_Wg"],
        "Wo": i["L3_attn_Wo"], "ln_w": column(i["L3_attn_ln_w"]), "ln_b": column(i["L3_attn_ln_b"]),
        "ln1_g": column(i["L3_ffn_ln1_g"]), "ln1_b": column(i["L3_ffn_ln1_b"]),
        "ln2_g": column(i["L3_ffn_ln2_g"]), "ln2_b": column(i["L3_ffn_ln2_b"]),
        "q3": i["L3_ffn_wq"], "k3": i["L3_ffn_wk"], "v3": i["L3_ffn_wv"], "o3": i["L3_ffn_wo"],
        "bq3": column(i["L3_ffn_bq"]), "bk3": column(i["L3_ffn_bk"]), "bv3": column(i["L3_ffn_bv"]),
        "bo3": column(i["L3_ffn_bo"]),
        "gate3": i["L3_ffn_gate_w"], "gate_b3": np.tile(i["L3_ffn_gate_b"], (128, 1)),
        "f_b1": np.reshape(i["L3_ffn_b1"], (32, 128)).T, "f_b2": i["L3_ffn_b2"],
    }
    return np.concatenate([rows128(w[name]) for name in SMALL.at], 1)


def constants():
    p = np.arange(128)
    head = (p[:, None] // WKV_HEAD == p[None, :] // WKV_HEAD).astype(np.float32)
    one = np.ones((128, 128), np.float32)
    c = {
        "ident": np.eye(128), "ones": one, "mean": one / 128, "head_ones": head, "head_mean": head / WKV_HEAD,
        "iota": np.tile(np.arange(16), (128, 1)), "even": column(p // WC % 2 == 0), "odd": column(p // WC % 2 == 1),
        "eps_1e5": one[:, :1] * 1e-5, "eps_scan": one[:, :1] * 1e-12, "eps_wkv": one[:, :1] * (1e-5 * 64),
        "start": np.tile(np.arange(16) == 0, (128, 1)), "zero": one[:, :1] * 0,
    }
    return np.concatenate([c[name].astype(np.float32) for name in CONSTS.at], 1)


def selectors():
    s = np.zeros((96, 40, 128), np.float32)
    for part in range(3):
        for e in range(32):
            s[32 * part + e, e, :] = 1
        for i in range(8):
            s[32 * part + 2 * i, 32 + i, :64] = 1
            s[32 * part + 2 * i + 1, 32 + i, 64:] = 1
    return np.reshape(s, (96, 40 * 128))


def expert_weights0(i):
    return np.stack([np.concatenate([i["L0_ffn_W1"][e], tiles(i["L0_ffn_W2"][e]), tiles(i["L0_ffn_W3"][e])], 1)
                     for e in range(8)])


def expert_weights1(i):
    return np.concatenate([np.concatenate([i["L1_ffn_w1"][e], i["L1_ffn_w3"][e], tiles(i["L1_ffn_w2"][e])], 1)
                           for e in range(8)], 1)


def expert_weights2(i):
    pairs = [np.concatenate([np.concatenate([i[f"L2_ffn_{n}_proj"][2 * m], i[f"L2_ffn_{n}_proj"][2 * m + 1]], 1)
                             for m in range(8)], 1) for n in ("up", "gate")]
    down = np.concatenate([np.concatenate([i["L2_ffn_down_proj"][2 * m], i["L2_ffn_down_proj"][2 * m + 1]], 0)
                           for m in range(8)], 1)
    return np.concatenate([*pairs, down, i["L2_ffn_sh_gate"].T, i["L2_ffn_sh_up"].T, i["L2_ffn_sh_down"].T], 1)


def expert_weights3(i):
    return np.stack([np.concatenate([i["L3_ffn_w1"][e], tiles(i["L3_ffn_w2"][e])], 1) for e in range(8)])


def kernel(**inputs):
    import concourse.bacc as bacc
    from concourse.bass_utils import run_bass_kernel_spmd

    i = {name: np.asarray(a) for name, a in inputs.items()}
    feeds = {
        "x_in": np.reshape(i["L0_attn_x"], (TOK, P)).T, "small_in": small_weights(i), "consts_in": constants(),
        "sel_in": selectors(), "experts0_in": expert_weights0(i), "experts1_in": expert_weights1(i),
        "experts2_in": expert_weights2(i), "experts3_in": expert_weights3(i),
    }
    feeds = {name: np.ascontiguousarray(a) for name, a in feeds.items()}
    nc = bacc.Bacc("TRN2", target_bir_lowering=False, num_devices=1)
    args = [nc.dram_tensor(name, a.shape, mybir.dt.from_np(a.dtype), kind="ExternalInput").ap() for name, a in feeds.items()]
    out = nc.dram_tensor("out_0_dram", (P, TOK), F32, kind="ExternalOutput").ap()
    recurrent_layers(nc, *args, out)
    r = run_bass_kernel_spmd(nc, [feeds], core_ids=[0])
    return np.ascontiguousarray(np.reshape(r.results[0]["out_0_dram"].T, (BATCH, SEQ, P)))
```

```python
from contextlib import ExitStack

import numpy as np
import concourse.bass as bass
from concourse import mybir

ALU = mybir.AluOpType
ACT = mybir.ActivationFunctionType
F32 = mybir.dt.float32
BF16 = mybir.dt.bfloat16
U32 = mybir.dt.uint32
AX = mybir.AxisListType

P = 128
BATCH, SEQ = 2, 1024
TOK = BATCH * SEQ
NT = TOK // P
CH = 512
NC = TOK // CH
SLOTS = 18
NSTATE = 16
HEADS, DH = 16, 8
WKV_HEAD = 64
WC = 16
NWC = TOK // WC


class Layout:

    def __init__(self, parts):
        self.at, self.width = {}, 0
        for name, p, n in parts:
            self.at[name] = (self.width, p, n)
            self.width += n


SMALL = Layout([
    ("W_x", 128, 96), ("W_dt", 64, 128), ("W_out", 128, 128), ("A_log", 128, 16), ("b_dt", 128, 1), ("D", 128, 1),
    ("b_out", 128, 1), ("tokens", 128, 8), ("e_b1", 128, 32), ("e_b2", 128, 32), ("e_b3", 128, 8),
    ("q1", 128, 128), ("k1", 128, 128), ("v1", 128, 128), ("o1", 128, 128), ("gate1", 128, 8),
    ("q2", 128, 128), ("v2", 128, 128), ("anomaly", 128, 128), ("bq2", 128, 1), ("bv2", 128, 128),
    ("router", 128, 16), ("router_bias", 128, 16),
    ("maa_x", 128, 1), ("maa", 128, 5), ("maa_w1", 128, 160), ("maa_w2", 128, 512), ("maa_w2_g", 32, 128), ("decay_w1", 128, 64),
    ("decay_w2", 64, 128), ("decay", 128, 1), ("faaaa", 128, 1), ("Wr", 128, 128), ("Wk", 128, 128),
    ("Wv", 128, 128), ("Wg", 128, 128), ("Wo", 128, 128), ("ln_w", 128, 1), ("ln_b", 128, 1),
    ("ln1_g", 128, 1), ("ln1_b", 128, 1), ("ln2_g", 128, 1), ("ln2_b", 128, 1), ("q3", 128, 128), ("k3", 128, 128),
    ("v3", 128, 128), ("o3", 128, 128), ("bq3", 128, 1), ("bk3", 128, 1), ("bv3", 128, 1), ("bo3", 128, 1),
    ("gate3", 128, 8), ("gate_b3", 128, 8), ("f_b1", 128, 32), ("f_b2", 8, 128),
])
CONSTS = Layout([
    ("ident", 128, 128), ("ones", 128, 128), ("mean", 128, 128), ("head_ones", 128, 128), ("head_mean", 128, 128),
    ("iota", 128, 16), ("even", 128, 1), ("odd", 128, 1), ("eps_1e5", 128, 1), ("eps_scan", 128, 1),
    ("eps_wkv", 128, 1), ("start", 128, 16), ("zero", 128, 1),
])


class Kit:

    def __init__(self, nc, slots, small, consts, experts, sel, psum, scratch):
        self.nc, self.slots, self.small, self.consts = nc, slots, small, consts
        self.experts, self.sel, self.psum, self.scratch = experts, sel, psum, scratch

    def slot(self, i):
        return self.slots[:, i, :]

    def chunk(self, i, c):
        return self.slots[:, i, c * CH:(c + 1) * CH]

    def w(self, name):
        a, p, n = SMALL.at[name]
        return self.small[0:p, a:a + n]

    def c(self, name):
        a, p, n = CONSTS.at[name]
        return self.consts[0:p, a:a + n]

    def bank(self, b):
        return self.psum[:, b, :]


class Stage:

    def __init__(self, kit, name):
        self.kit, self.name, self.stack, self.sems = kit, name, ExitStack(), []

    def __enter__(self):
        self.stack.__enter__()
        return self

    def sem(self, name):
        self.sems.append(self.kit.nc.alloc_semaphore(f"{self.name}_{name}"))
        return self.sems[-1]

    def block(self):
        return self.stack.enter_context(self.kit.nc.Block())

    def __exit__(self, *e):
        self.stack.__exit__(*e)
        if e[0] is None:
            for sem in self.sems:
                self.kit.nc.gpsimd.sem_clear(sem)
                self.kit.nc.release_semaphore(sem)


def spread(ap, n):
    return ap.unsqueeze(2).broadcast_to([ap.shape[0], ap.shape[1], n])



class Arrivals:

    def __init__(self, nc, ctx):
        def sems(name, n):
            return [ctx.enter_context(nc.semaphore(f"{name}{r}")) for r in range(n)]

        self.small, self.sel = sems("small_loaded", 1)[0], sems("sel_loaded", 1)[0]
        self.experts = [sems("experts0_loaded", 2), sems("experts1_loaded", 1), sems("experts2_loaded", 1),
                        sems("experts3_loaded", E3_RING)]


def load_inputs(kit, arrivals, x_dram, small_dram, consts_dram, sel_dram, x, sel_slot):
    with Stage(kit, "load") as st:
        x_loaded, consts_loaded = st.sem("x_loaded"), st.sem("consts_loaded")
        block = st.block()

        @block.sync
        def _(sp):
            sp.dma_start(kit.slot(x), x_dram).then_inc(x_loaded, 16)
            sp.dma_start(kit.small[:, :], small_dram).then_inc(arrivals.small, 16)
            sp.dma_start(flat_slots(kit, sel_slot, 3)[0:96, 0:40 * P], sel_dram).then_inc(arrivals.sel, 16)
            sp.wait_ge(x_loaded, 16)

        @block.scalar
        def _(act):
            act.dma_start(kit.consts[:, :], consts_dram).then_inc(consts_loaded, 16)
            act.wait_ge(consts_loaded, 16)


def await_small(kit, arrivals):
    with Stage(kit, "small") as st:
        block = st.block()

        @block.sync
        def _(sp):
            sp.wait_ge(arrivals.small, 16)


def cast_selectors(kit, arrivals, sel_slot):
    with Stage(kit, "sel") as st:
        block = st.block()

        @block.vector
        def _(dve):
            dve.wait_ge(arrivals.sel, 16)
            nc = kit.nc
            nc.vector.tensor_copy(kit.sel[:, :, :].rearrange("p a b -> p (a b)"), flat_slots(kit, sel_slot, 3)[0:96, 0:40 * P])


def start_experts(kit, name, sources, cols, landed):
    with Stage(kit, name) as st:
        block = st.block()

        @block.sync
        def _(sp):
            for r, source in enumerate(sources):
                sp.dma_start(kit.experts[:, r * cols:(r + 1) * cols], source).then_inc(landed[r], 16)


def store_output(kit, out_dram, x, stored):
    with Stage(kit, "store") as st:
        block = st.block()

        @block.sync
        def _(sp):
            sp.dma_start(out_dram, kit.slot(x)).then_inc(stored, 16)
            sp.wait_ge(stored, 16)



def layer_norm(kit, name, src, dst, square, stat, gamma=None, beta=None):
    nc = kit.nc
    with Stage(kit, name) as st:
        mean_ready, centered, squared, var_ready = map(st.sem, ("mean", "centered", "squared", "var"))
        std_ready, rstd_ready, diag_ready, bcast_ready = map(st.sem, ("std", "rstd", "diag", "bcast"))
        scaled = st.sem("scaled")
        std = kit.slot(stat)[:, 0:NT]
        rstd = kit.slot(stat)[:, NT:2 * NT]
        diag = kit.slot(square).rearrange("p (j q) -> p j q", q=P)
        block = st.block()

        @block.tensor
        def _(pe):
            for c in range(NC):
                nc.tensor.matmul(kit.bank(c), kit.c("mean"), kit.chunk(src, c), start=True, stop=True).then_inc(mean_ready, 1)
            for j in range(NT):
                pe.wait_ge(squared, j // 4 + 1)
                last = nc.tensor.matmul(kit.psum[:, 4, j:j + 1], kit.slot(square)[:, j * P:(j + 1) * P],
                                        kit.c("mean")[:, 0:1], start=True, stop=True)
            last.then_inc(var_ready, 1)
            pe.wait_ge(diag_ready, 1)
            for c in range(NC):
                nc.tensor.matmul(kit.bank(c), kit.c("ones"), kit.chunk(square, c), start=True, stop=True).then_inc(bcast_ready, 1)

        @block.vector
        def _(dve):
            for c in range(NC):
                dve.wait_ge(mean_ready, c + 1)
                nc.vector.tensor_tensor(kit.chunk(dst, c), kit.chunk(src, c), kit.bank(c), ALU.subtract).then_inc(centered, 1)
            dve.wait_ge(std_ready, 1)
            nc.vector.reciprocal(rstd, std).then_inc(rstd_ready, 1)
            dve.wait_ge(rstd_ready, 1)
            nc.vector.tensor_tensor(diag, kit.c("ident").unsqueeze(1).broadcast_to([P, NT, P]), spread(rstd, P),
                                    ALU.mult).then_inc(diag_ready, 1)
            for c in range(NC):
                dve.wait_ge(bcast_ready, c + 1)
                if gamma is None:
                    nc.vector.tensor_tensor(kit.chunk(dst, c), kit.chunk(dst, c), kit.bank(c), ALU.mult).then_inc(scaled, 1)
                else:
                    nc.vector.scalar_tensor_tensor(kit.chunk(dst, c), kit.bank(c), kit.w(gamma), kit.chunk(dst, c),
                                                   ALU.mult, ALU.mult).then_inc(scaled, 1)
                    dve.wait_ge(scaled, 2 * c + 1)
                    nc.vector.tensor_scalar(kit.chunk(dst, c), kit.chunk(dst, c), kit.w(beta), None,
                                            ALU.add).then_inc(scaled, 1)

        @block.scalar
        def _(act):
            for c in range(NC):
                act.wait_ge(centered, c + 1)
                nc.scalar.activation(kit.chunk(square, c), kit.chunk(dst, c), ACT.Square).then_inc(squared, 1)
            act.wait_ge(var_ready, 1)
            nc.scalar.activation(std, kit.psum[:, 4, 0:NT], ACT.Sqrt, bias=kit.c("eps_1e5")).then_inc(std_ready, 1)



def project(kit, name, jobs, fills=()):
    nc = kit.nc
    with Stage(kit, name) as st:
        product, by_act, by_dve, filled = map(st.sem, ("product", "by_act", "by_dve", "filled"))
        block = st.block()
        steps = [(job, c) for job in jobs for c in range(NC)]
        by_dve_alone = len(jobs) == 1 and jobs[0][4] is not None

        @block.gpsimd
        def _(pool):
            for i, (memory, value) in enumerate(fills):
                if i >= 1:
                    pool.wait_ge(filled, i)
                nc.gpsimd.memset(memory, value).then_inc(filled, 1)

        @block.tensor
        def _(pe):
            for i, ((dst, w, src, bias, plus), c) in enumerate(steps):
                if i >= 8:
                    pe.wait_ge(by_act if i % 2 == 0 else by_dve, (i - 8) // 2 + 1)
                nc.tensor.matmul(kit.bank(i % 8), kit.w(w), kit.chunk(src, c), start=True, stop=True).then_inc(product, 1)

        @block.scalar
        def _(act):
            for i, ((dst, w, src, bias, plus), c) in enumerate(steps):
                if i % 2 == 0 and not by_dve_alone:
                    act.wait_ge(product, i + 1)
                    nc.scalar.activation(kit.chunk(dst, c), kit.bank(i % 8), ACT.Identity,
                                         bias=kit.w(bias) if bias else 0.0).then_inc(by_act, 1)

        @block.vector
        def _(dve):
            for i, ((dst, w, src, bias, plus), c) in enumerate(steps):
                if by_dve_alone:
                    dve.wait_ge(product, i + 1)
                    nc.vector.scalar_tensor_tensor(kit.chunk(dst, c), kit.bank(i), kit.w(bias) if bias else 0.0,
                                                   kit.chunk(plus, c), ALU.add, ALU.add)
                elif i % 2 == 1:
                    dve.wait_ge(product, i + 1)
                    if bias:
                        nc.vector.tensor_scalar(kit.chunk(dst, c), kit.bank(i % 8), kit.w(bias), None, ALU.add).then_inc(by_dve, 1)
                    else:
                        nc.vector.tensor_copy(kit.chunk(dst, c), kit.bank(i % 8)).then_inc(by_dve, 1)



def scan_inputs(kit, xn, low, delta, suffix, rows):
    nc = kit.nc
    with Stage(kit, "scan_in") as st:
        proj, low_ready, bc_ready, z_ready, z_copied = map(st.sem, ("proj", "low", "bc", "z", "z_copied"))
        neg_abs, exped, logged, own, a_exp = map(st.sem, ("neg_abs", "exped", "logged", "own", "a_exp"))
        block = st.block()
        bc = kit.slot(rows)[0:32, :]

        @block.tensor
        def _(pe):
            for c in range(NC):
                nc.tensor.matmul(kit.bank(c)[0:64], kit.w("W_x")[:, 0:64], kit.chunk(xn, c), start=True, stop=True).then_inc(proj, 1)
            for c in range(NC):
                nc.tensor.matmul(kit.bank(4 + c)[0:32], kit.w("W_x")[:, 64:96], kit.chunk(xn, c), start=True, stop=True).then_inc(proj, 1)
            for c in range(NC):
                pe.wait_ge(low_ready, c + 1)
                nc.tensor.matmul(kit.bank(c), kit.w("W_dt"), kit.chunk(low, c)[0:64], start=True, stop=True).then_inc(z_ready, 1)

        @block.scalar
        def _(act):
            nc.scalar.preload_act_table_set("natural_log_exp_and_others")
            nc.scalar.activation(kit.scratch[:, 0:NSTATE], kit.w("A_log"), ACT.Exp).then_inc(a_exp, 1)
            for c in range(NC):
                act.wait_ge(proj, c + 1)
                nc.scalar.activation(kit.chunk(low, c)[0:64], kit.bank(c)[0:64], ACT.Copy).then_inc(low_ready, 1)
            for c in range(NC):
                act.wait_ge(z_ready, c + 1)
                nc.scalar.activation(kit.chunk(delta, c), kit.bank(c), ACT.Identity, bias=kit.w("b_dt")).then_inc(z_copied, 1)
            for c in range(NC):
                act.wait_ge(neg_abs, c + 1)
                nc.scalar.activation(kit.chunk(suffix, c), kit.chunk(suffix, c), ACT.Exp).then_inc(exped, 1)
                act.wait_ge(exped, c + 1)
                nc.scalar.activation(kit.chunk(suffix, c), kit.chunk(suffix, c), ACT.Ln, bias=kit.c("ones")[:, 0:1]).then_inc(logged, 1)

        @block.vector
        def _(dve):
            for c in range(NC):
                dve.wait_ge(proj, NC + c + 1)
                nc.vector.tensor_copy(kit.chunk(rows, c)[0:32], kit.bank(4 + c)[0:32]).then_inc(bc_ready, 1)
            dve.wait_ge(a_exp, 1)
            nc.vector.tensor_scalar(kit.scratch[:, 16:32], kit.scratch[:, 0:NSTATE], -1.0, None, ALU.mult)
            for c in range(NC):
                dve.wait_ge(z_copied, c + 1)
                nc.vector.scalar_tensor_tensor(kit.chunk(suffix, c), kit.chunk(delta, c), -1.0, kit.chunk(delta, c),
                                               ALU.mult, ALU.min).then_inc(neg_abs, 1)
            for c in range(NC):
                dve.wait_ge(logged, c + 1)
                nc.vector.scalar_tensor_tensor(kit.chunk(delta, c), kit.chunk(delta, c), 0.0, kit.chunk(suffix, c),
                                               ALU.max, ALU.add).then_inc(own, 1)



def router(kit, name, src, gate, bias, experts, rule, rows, stacked, work, tmp):
    nc = kit.nc
    flat = kit.slot(work)

    def field(at, n):
        return flat[:, at:at + NT * n].rearrange("p (j n) -> p j n", n=n)

    score, total, best = field(0, experts), field(256, 1), field(272, 8)
    index = flat[:, 400:400 + NT * 8].bitcast(U32).rearrange("p (j n) -> p j n", n=8)
    index_f, first, second = field(528, 8), field(656, experts), field(912, experts)
    e2, w1, w2, weight = field(1168, 1), field(1184, 1), field(1200, 1), field(1216, experts)
    iota = kit.c("iota")[:, 0:experts].unsqueeze(1).broadcast_to([P, NT, experts])

    def wide(ap):
        return ap.broadcast_to([P, NT, experts])

    padded = kit.slot(tmp)[:, 0:NT * 96].rearrange("p (j n) -> p j n", n=96)
    part = [padded[:, :, 32 * s:32 * s + experts] for s in range(3)]
    part_bf16 = field(1472, experts).bitcast(BF16)[:, :, 0:experts]
    rest = field(1728, experts)
    stacks = kit.slot(stacked).bitcast(BF16)[0:96, 0:TOK]
    exact = rule in ("half", "first")

    with Stage(kit, name) as st:
        logits, exp_in, exp_out, own = map(st.sem, ("logits", "exp_in", "exp_out", "own"))
        padded_ready, weights_ready, turned = map(st.sem, ("padded", "weights", "turned"))
        block = st.block()

        @block.gpsimd
        def _(pool):
            nc.gpsimd.memset(padded, 0.0).then_inc(padded_ready, 1)

        @block.tensor
        def _(pe):
            for j in range(NT):
                last = nc.tensor.matmul(kit.bank(0)[:, j * experts:(j + 1) * experts], kit.slot(src)[:, j * P:(j + 1) * P],
                                        kit.w(gate), start=True, stop=True)
            last.then_inc(logits, 1)
            pe.wait_ge(weights_ready, 1)
            for j in range(NT):
                nc.tensor.transpose(kit.bank(4 + j // 4)[0:96, (j % 4) * P:(j % 4 + 1) * P], padded[:, j, :],
                                    kit.c("ident")).then_inc(turned, 1)

        @block.scalar
        def _(act):
            if rule in ("scores", "top"):
                act.wait_ge(exp_in, 1)
                what = score if rule == "scores" else e2
                nc.scalar.activation(what, what, ACT.Exp).then_inc(exp_out, 1)
            act.wait_ge(turned, NT // 2)
            nc.scalar.activation(stacks[:, 0:SEQ], kit.psum[0:96, 4:6, :].rearrange("p a b -> p (a b)"), ACT.Copy)
            if rows is not None:
                nc.scalar.activation(kit.slot(rows)[0:experts, 0:SEQ], kit.psum[0:experts, 4:6, :].rearrange("p a b -> p (a b)"), ACT.Copy)

        @block.vector
        def _(dve):
            done = [0]

            def then(instruction):
                done[0] += 1
                instruction.then_inc(own, 1)
                dve.wait_ge(own, done[0])

            dve.wait_ge(logits, 1)
            raw = kit.bank(0)[:, 0:NT * experts].rearrange("p (j n) -> p j n", n=experts)
            if bias:
                then(nc.vector.tensor_tensor(score, raw, kit.w(bias).unsqueeze(1).broadcast_to([P, NT, experts]), ALU.add))
            else:
                then(nc.vector.tensor_copy(score, raw))
            if rule == "scores":
                then(nc.vector.tensor_reduce(total, score, AX.X, ALU.max))
                nc.vector.tensor_tensor(score, score, wide(total), ALU.subtract).then_inc(exp_in, 1)
                dve.wait_ge(exp_out, 1)
                then(nc.vector.tensor_reduce(total, score, AX.X, ALU.add))
                then(nc.vector.reciprocal(total, total))
                then(nc.vector.tensor_tensor(score, score, wide(total), ALU.mult))
            for j in range(NT):
                last = nc.vector.max(best[:, j, :], score[:, j, :])
            then(last)
            for j in range(NT):
                last = nc.vector.max_index(index[:, j, :], best[:, j, :], score[:, j, :])
            then(last)
            then(nc.vector.tensor_copy(index_f, index))
            nc.vector.tensor_tensor(first, iota, wide(index_f[:, :, 0:1]), ALU.is_equal)
            then(nc.vector.tensor_tensor(second, iota, wide(index_f[:, :, 1:2]), ALU.is_equal))
            if rule == "half":
                then(nc.vector.tensor_tensor(first, first, second, ALU.add))
                dve.wait_ge(padded_ready, 1)
                nc.vector.tensor_scalar(part[0], first, 0.5, None, ALU.mult).then_inc(weights_ready, 1)
            elif rule == "scores":
                then(nc.vector.tensor_tensor(first, first, second, ALU.add))
                then(nc.vector.tensor_tensor(weight, first, score, ALU.mult))
            elif rule == "top":
                nc.vector.tensor_tensor(e2, best[:, :, 1:2], best[:, :, 0:1], ALU.subtract).then_inc(exp_in, 1)
                dve.wait_ge(exp_out, 1)
                then(nc.vector.tensor_scalar(w1, e2, 1.0, None, ALU.add))
                then(nc.vector.reciprocal(w1, w1))
                then(nc.vector.tensor_tensor(w2, w1, e2, ALU.mult))
                nc.vector.tensor_tensor(first, first, wide(w1), ALU.mult)
                then(nc.vector.tensor_tensor(second, second, wide(w2), ALU.mult))
                then(nc.vector.tensor_tensor(weight, first, second, ALU.add))
            else:
                dve.wait_ge(padded_ready, 1)
                nc.vector.tensor_copy(part[0], first).then_inc(weights_ready, 1)
            if not exact:
                then(nc.vector.tensor_copy(part_bf16, weight))
                dve.wait_ge(padded_ready, 1)
                nc.vector.tensor_copy(part[0], part_bf16)
                then(nc.vector.tensor_tensor(rest, weight, part_bf16, ALU.subtract))
                then(nc.vector.tensor_copy(part_bf16, rest))
                nc.vector.tensor_copy(part[1], part_bf16)
                nc.vector.tensor_tensor(part[2], rest, part_bf16, ALU.subtract).then_inc(weights_ready, 1)
            dve.wait_ge(turned, NT)
            nc.vector.tensor_copy(stacks[:, SEQ:TOK], kit.psum[0:96, 6:8, :].rearrange("p a b -> p (a b)"))
            if rows is not None:
                nc.vector.tensor_copy(kit.slot(rows)[0:experts, SEQ:TOK], kit.psum[0:experts, 6:8, :].rearrange("p a b -> p (a b)"))


def spread_rows(kit, name, stacked, matrices, outs):
    nc = kit.nc
    parts = kit.slot(stacked).bitcast(BF16)[0:96, 0:TOK]
    with Stage(kit, name) as st:
        spread_ready, by_act, by_dve = map(st.sem, ("spread", "by_act", "by_dve"))
        block = st.block()

        @block.tensor
        def _(pe):
            for i, m in enumerate(matrices):
                if i >= 2:
                    pe.wait_ge(by_act if i % 2 == 0 else by_dve, i // 2)
                for c in range(NC):
                    last = nc.tensor.matmul(kit.bank(4 * (i % 2) + c), kit.sel[0:96, m, :], parts[:, c * CH:(c + 1) * CH],
                                            start=True, stop=True)
                last.then_inc(spread_ready, 1)

        @block.scalar
        def _(act):
            for i in range(0, len(matrices), 2):
                act.wait_ge(spread_ready, i + 1)
                nc.scalar.activation(outs[i], kit.psum[:, 0:4, :].rearrange("p a b -> p (a b)"),
                                     ACT.Copy).then_inc(by_act, 1)

        @block.vector
        def _(dve):
            for i in range(1, len(matrices), 2):
                dve.wait_ge(spread_ready, i + 1)
                nc.vector.tensor_copy(outs[i], kit.psum[:, 4:8, :].rearrange("p a b -> p (a b)")).then_inc(by_dve, 1)



def merge(kit, name, x, s, tmp, g=None):
    nc = kit.nc
    with Stage(kit, name) as st:
        gated, own = map(st.sem, ("gated", "own"))
        block = st.block()

        @block.scalar
        def _(act):
            for c in range(NC):
                nc.scalar.activation(kit.chunk(tmp, c), kit.bank(4 + c) if g is None else kit.chunk(g, c), ACT.Silu).then_inc(gated, 1)

        @block.vector
        def _(dve):
            for c in range(NC):
                dve.wait_ge(gated, c + 1)
                nc.vector.tensor_tensor(kit.chunk(tmp, c), kit.chunk(tmp, c), kit.chunk(s, c), ALU.mult).then_inc(own, 1)
                dve.wait_ge(own, c + 1)
                nc.vector.tensor_tensor(kit.chunk(x, c), kit.chunk(x, c), kit.chunk(tmp, c), ALU.add)



HID = 512
HB = HID // P
E0_COLS = HID + HB * HID + HB * P
N_EXP0 = 8


def experts_and_scan(kit, dram, landed, xn, weights, acc, h1, h2, delta, rows, stacked, rest, du, suffix, y, halves):
    nc = kit.nc
    steps = [(e, c) for e in range(N_EXP0) for c in range(NC)]
    n_steps = len(steps)
    assert n_steps == NSTATE * BATCH
    w1 = [kit.experts[:, b * E0_COLS:b * E0_COLS + HID] for b in range(2)]
    w2 = [kit.experts[:, b * E0_COLS + HID:b * E0_COLS + HID + HB * HID].rearrange("p (k n) -> p k n", n=HID) for b in range(2)]
    w3 = [kit.experts[:, (b + 1) * E0_COLS - HB * P:(b + 1) * E0_COLS].rearrange("p (k n) -> p k n", n=P) for b in range(2)]
    a_neg = kit.scratch[:, NSTATE:2 * NSTATE]
    gated = kit.scratch[:, CH:2 * CH]
    parts = kit.slot(stacked).bitcast(BF16)[0:96, 0:TOK]
    decay, inv, work, scan, tmp = halves
    n_bc = 2 * NSTATE
    bc, rest = kit.slot(rows)[0:n_bc], kit.slot(rest)[0:n_bc]
    middle = kit.slot(stacked).bitcast(BF16)[0:n_bc, TOK:2 * TOK]
    sequences = [slice(0, SEQ), slice(SEQ, TOK)]
    spread_banks = kit.psum[:, 6:8, :].rearrange("p a b -> p (a b)")
    with Stage(kit, "e0") as st:
        hidden, gelu_done, expert_out, taken, own = map(st.sem, ("hidden", "gelu", "expert_out", "taken", "own"))
        b_spread, c_spread, decay_ready, log_ready, inv_ready = map(st.sem, ("b", "c", "decay", "log", "inv"))
        high_ready, rest_ready, middle_ready, low_ready, du_ready, prepared = map(st.sem, ("high", "rest", "middle", "low", "du", "prepared"))
        b_used, decayed, scanned, c_used, weighted, y_ready = map(st.sem, ("b_used", "decayed", "scanned", "c_used", "weighted", "y"))
        block = st.block()

        @block.sync
        def _(sp):
            for e in range(2, N_EXP0):
                sp.wait_ge(expert_out, NC * (e - 1))
                sp.dma_start(kit.experts[:, (e % 2) * E0_COLS:(e % 2 + 1) * E0_COLS], dram[e]).then_inc(landed[e % 2], 16)

        @block.tensor
        def _(pe):
            group = [0]

            def hidden_group(operands):
                g = group[0]
                if g >= 4:
                    pe.wait_ge(gelu_done, g - 3)
                for n, (lhs, rhs) in enumerate(operands):
                    last = nc.tensor.matmul(kit.bank(g % 4), lhs, rhs, start=n == 0, stop=n == len(operands) - 1)
                last.then_inc(hidden, 1)
                group[0] = g + 1

            def first(i):
                e, c = steps[i]
                if c == 0:
                    pe.wait_ge(landed[e % 2], 16 * (e // 2 + 1))
                for m in range(HB):
                    hidden_group([(w1[e % 2][:, m * P:(m + 1) * P], kit.chunk(xn, c))])

            def second(i):
                e, c = steps[i]
                pe.wait_ge(gelu_done, 8 * i if i else 4)
                for m in range(HB):
                    hidden_group([(w2[e % 2][:, k, m * P:(m + 1) * P], kit.chunk(h1[i % 2], k)) for k in range(HB)])

            def third(i):
                e, c = steps[i]
                pe.wait_ge(gelu_done, min(8 * (i + 1) + 4, 8 * n_steps))
                if i >= 2:
                    pe.wait_ge(taken, i - 1)
                for k in range(HB):
                    last = nc.tensor.matmul(kit.bank(4 + i % 2), w3[e % 2][:, k, :], kit.chunk(h2[i % 2], k), start=k == 0, stop=k == HB - 1)
                last.then_inc(expert_out, 1)

            def spread_row(i, row, done):
                for c in range(2):
                    at = i % 2 * SEQ + c * CH
                    last = nc.tensor.matmul(kit.bank(6 + c), kit.sel[0:96, row, :], parts[:, at:at + CH], start=True, stop=True)
                last.then_inc(done, 1)

            for i in range(n_steps + 2):
                k = i - 2
                if k == 0:
                    pe.wait_ge(middle_ready, 2 * BATCH)
                    pe.wait_ge(low_ready, BATCH)
                if 0 <= k < n_steps:
                    if k >= 1:
                        pe.wait_ge(c_used, k)
                    spread_row(k, k // 2, b_spread)
                if i < n_steps:
                    first(i)
                if 1 <= i <= n_steps:
                    second(i - 1)
                if 0 <= k < n_steps:
                    pe.wait_ge(b_used, k + 1)
                    spread_row(k, NSTATE + k // 2, c_spread)
                if i >= 2:
                    third(i - 2)

        @block.scalar
        def _(act):
            group = [0]

            def gelu(out, bias):
                g = group[0]
                act.wait_ge(hidden, g + 1)
                nc.scalar.activation(out, kit.bank(g % 4), ACT.Gelu, bias=bias).then_inc(gelu_done, 1)
                group[0] = g + 1

            def stack_parts():
                for t in sequences:
                    nc.scalar.activation(parts[0:n_bc, t], bc[:, t], ACT.Copy).then_inc(high_ready, 1)
                for b, t in enumerate(sequences):
                    act.wait_ge(rest_ready, b + 1)
                    nc.scalar.activation(middle[:, t], rest[:, t], ACT.Copy).then_inc(middle_ready, 1)
                for t in sequences:
                    nc.scalar.activation(parts[n_bc:2 * n_bc, t], rest[:, t], ACT.Copy).then_inc(middle_ready, 1)

            def decays(i):
                if i >= 1:
                    act.wait_ge(decayed, i)
                nc.scalar.preload_act_table_set("natural_log_exp_and_others")
                nc.scalar.activation(decay, kit.slot(suffix)[:, i % 2 * SEQ:(i % 2 + 1) * SEQ], ACT.Exp,
                                     scale=a_neg[:, i // 2:i // 2 + 1]).then_inc(decay_ready, 1)
                act.wait_ge(decay_ready, i + 1)
                if i >= 1:
                    act.wait_ge(weighted, i)
                nc.scalar.activation(inv, decay, ACT.Ln, bias=kit.c("eps_scan")).then_inc(log_ready, 1)
                act.wait_ge(log_ready, i + 1)
                nc.scalar.activation(inv, inv, ACT.Exp, scale=-1.0).then_inc(inv_ready, 1)

            for i in range(n_steps + 2):
                if i < n_steps:
                    e, c = steps[i]
                    for m in range(HB):
                        gelu(kit.chunk(h1[i % 2], m), kit.w("e_b1")[:, HB * e + m:HB * e + m + 1])
                if i == 0:
                    stack_parts()
                if i == 2:
                    act.wait_ge(prepared, 1)
                for m in range(HB):
                    if 1 <= i <= n_steps:
                        e, c = steps[i - 1]
                        gelu(kit.chunk(h2[(i - 1) % 2], m), kit.w("e_b2")[:, HB * e + m:HB * e + m + 1])
                    if m == 1 and i >= 2:
                        decays(i - 2)

        @block.vector
        def _(dve):
            def scan_step(i):
                at = i % 2 * SEQ
                dve.wait_ge(b_spread, i + 1)
                if i >= 1:
                    dve.wait_ge(weighted, i)
                nc.vector.tensor_tensor(work, kit.slot(du)[:, at:at + SEQ], spread_banks, ALU.mult).then_inc(b_used, 1)
                dve.wait_ge(b_used, i + 1)
                dve.wait_ge(decay_ready, i + 1)
                nc.vector.tensor_tensor(work, work, decay, ALU.mult).then_inc(decayed, 1)
                dve.wait_ge(decayed, i + 1)
                nc.vector.tensor_tensor_scan(scan, kit.c("ones")[:, 0:1].broadcast_to([P, SEQ]), work, 0.0,
                                             ALU.mult, ALU.add).then_inc(scanned, 1)
                dve.wait_ge(scanned, i + 1)
                dve.wait_ge(c_spread, i + 1)
                nc.vector.tensor_tensor(work, scan, spread_banks, ALU.mult).then_inc(c_used, 1)

            def gate(i):
                e, c = steps[i]
                dve.wait_ge(expert_out, i + 1)
                out = kit.chunk(acc, c) if e == 0 else gated
                if i > NC:
                    dve.wait_ge(own, i - NC)
                nc.vector.scalar_tensor_tensor(out, kit.bank(4 + i % 2), kit.w("e_b3")[:, e:e + 1],
                                               weights[e][:, c * CH:(c + 1) * CH], ALU.add, ALU.mult).then_inc(taken, 1)
                if e > 0:
                    dve.wait_ge(taken, i + 1)
                    nc.vector.tensor_tensor(kit.chunk(acc, c), kit.chunk(acc, c), gated, ALU.add).then_inc(own, 1)

            for b, t in enumerate(sequences):
                dve.wait_ge(high_ready, b + 1)
                nc.vector.tensor_tensor(rest[:, t], bc[:, t], parts[0:n_bc, t], ALU.subtract).then_inc(rest_ready, 1)
            for b, t in enumerate(sequences):
                nc.vector.tensor_tensor_scan(kit.slot(suffix)[:, t.start:t.stop - 1][:, ::-1],
                                             kit.c("ones")[:, 0:1].broadcast_to([P, SEQ - 1]),
                                             kit.slot(delta)[:, t.start + 1:t.stop][:, ::-1], 0.0, ALU.mult, ALU.add)
                nc.vector.memset(kit.slot(suffix)[:, t.stop - 1:t.stop], 0.0)
            for b, t in enumerate(sequences):
                dve.wait_ge(middle_ready, b + 1)
                nc.vector.tensor_tensor(parts[2 * n_bc:3 * n_bc, t], rest[:, t], middle[:, t], ALU.subtract).then_inc(low_ready, 1)
            dve.wait_ge(middle_ready, 2 * BATCH)
            nc.vector.tensor_tensor(kit.slot(du), kit.slot(delta), kit.slot(xn), ALU.mult).then_inc(du_ready, 1)
            nc.vector.tensor_scalar(kit.slot(y), kit.slot(xn), kit.w("D"), None, ALU.mult).then_inc(prepared, 1)
            for sem, count in ((low_ready, BATCH), (du_ready, 1), (prepared, 1)):
                dve.wait_ge(sem, count)
            for i in range(n_steps + 2):
                if i >= 2:
                    gate(i - 2)
                if 1 <= i <= n_steps:
                    scan_step(i - 1)

        @block.gpsimd
        def _(pool):
            for i in range(n_steps):
                at = i % 2 * SEQ
                pool.wait_ge(c_used, i + 1)
                pool.wait_ge(inv_ready, i + 1)
                if i == 0:
                    pool.wait_ge(prepared, 1)
                if i >= 1:
                    pool.wait_ge(y_ready, i)
                nc.gpsimd.tensor_tensor(tmp, work, inv, ALU.mult).then_inc(weighted, 1)
                pool.wait_ge(weighted, i + 1)
                nc.gpsimd.tensor_tensor(kit.slot(y)[:, at:at + SEQ], kit.slot(y)[:, at:at + SEQ], tmp, ALU.add).then_inc(y_ready, 1)



PARTS = 3
BLOCK_ROWS = DH * PARTS
PAIR_ROWS = 96
FULL_ROWS = PAIR_ROWS + 3
BF16_ONES = float(np.array([0x3F803F80], np.uint32).view(np.float32)[0])
STACKS = 12
SQ = 32
KT = SEQ // P


def flat_slots(kit, i, n):
    return kit.slots[:, i:i + n, :].rearrange("p a b -> p (a b)")


def attention(kit, name, xn, weights, out, q_stack, k_stack, sums, values, work):
    nc = kit.nc
    wq, wk, wv, bq, bk = weights
    q, k = work, work + 1
    qs_f32, ks_f32 = flat_slots(kit, q_stack, 3), flat_slots(kit, k_stack, 3)
    qs, ks = (f32.bitcast(BF16).rearrange("p (r t) -> p r t", r=STACKS) for f32 in (qs_f32, ks_f32))
    v = flat_slots(kit, values, 2).rearrange("p (j h n) -> p j h n", h=HEADS, n=2 * DH)
    project(kit, name + "_qk", [(q, wq, xn, bq, None), (k, wk, xn, bk, None)],
            fills=[(v, 1.0), (ks_f32[64:FULL_ROWS], BF16_ONES)])
    split = kit.experts[:, :].bitcast(BF16).rearrange("p (w s t) -> p w s t", w=2, s=3)

    with Stage(kit, name + "_prep") as st:
        tile_ready, v_ready = map(st.sem, ("tile", "v"))
        high, mid, rest = map(st.sem, ("high", "mid", "rest"))
        block = st.block()

        @block.tensor
        def _(pe):
            for j in range(NT):
                nc.tensor.matmul(kit.bank(j // 4)[:, (j % 4) * P:(j % 4 + 1) * P], kit.slot(xn)[:, j * P:(j + 1) * P],
                                 kit.w(wv), start=True, stop=True).then_inc(tile_ready, 1)

        @block.scalar
        def _(act):
            for w, src in enumerate((q, k)):
                nc.scalar.activation(split[:, w, 0], kit.slot(src), ACT.Copy).then_inc(high, 1)
            for w, src in enumerate((q, k)):
                act.wait_ge(rest, w + 1)
                nc.scalar.activation(split[:, w, 1], kit.slot(src), ACT.Copy).then_inc(mid, 1)
            for g in range(4):
                act.wait_ge(tile_ready, 4 * g + 4)
                nc.scalar.activation(v[:, 4 * g:4 * g + 4, :, 0:DH], kit.bank(g).rearrange("p (j h n) -> p j h n", j=4, n=DH),
                                     ACT.Copy).then_inc(v_ready, 1)

        @block.vector
        def _(dve):
            for w, src in enumerate((q, k)):
                dve.wait_ge(high, w + 1)
                nc.vector.tensor_tensor(kit.slot(src), kit.slot(src), split[:, w, 0], ALU.subtract).then_inc(rest, 1)
            for w, src in enumerate((q, k)):
                dve.wait_ge(mid, w + 1)
                nc.vector.tensor_tensor(split[:, w, 2], kit.slot(src), split[:, w, 1], ALU.subtract)

        @block.gpsimd
        def _(pool):
            nc.gpsimd.memset(qs_f32[64:PAIR_ROWS], 0.0)

    scale = 1.0 / float(np.sqrt(np.float32(DH)))
    heads = [(b, h) for b in range(BATCH) for h in range(HEADS)]
    n_heads = len(heads)
    n_tiles = KT * n_heads
    QUAD = 4
    QUAD_TILES = QUAD * KT
    n_quads = n_heads // QUAD
    AHEAD = QUAD_TILES + KT // 2
    RING = 2 * QUAD
    probs = flat_slots(kit, work, 4).rearrange("p (r t) -> p r t", t=SEQ)
    evac = kit.slot(sums).rearrange("p (r t) -> p r t", t=SEQ)
    den = kit.slot(sums + 1)
    half_max = kit.scratch[:, 0:4 * KT].rearrange("p (r n c) -> p r n c", n=KT, c=2)
    neg_max = kit.scratch[:, 32:32 + 2 * KT].rearrange("p (r n) -> p r n", n=KT)
    max_rest = kit.scratch[:, 64:64 + 2 * KT].rearrange("p (r n) -> p r n", n=KT)
    squares = kit.scratch[:, 128:256].bitcast(BF16).rearrange("p (w r n) -> p w r n", w=2, n=2 * SQ)
    max_parts, turned = squares[:, 0, :, 0:SQ], squares[:, 1, :, 0:SQ]
    with Stage(kit, name) as st:
        stacked = [st.sem(f"stacked{r}") for r in range(STACKS)]
        scores_a, maxed, combined, max_split, max_turned = map(st.sem, ("scores_a", "maxed", "combined", "max_split", "max_turned"))
        max_placed = [st.sem(f"placed{j}") for j in range(QUAD)]
        scores_b, exped, summed, evacuated, own = map(st.sem, ("scores_b", "exped", "summed", "evacuated", "own"))
        stored, inverted = [st.sem("stored0"), st.sem("stored1")], st.sem("inverted")
        block = st.block()
        banks_b = [kit.psum[:, 2 + 2 * r:4 + 2 * r, :].rearrange("p a b -> p (a b)") for r in range(2)]

        def tile_b(u):
            return u // QUAD_TILES * QUAD + u % QUAD, u % QUAD_TILES // QUAD

        def weigh(pe, g, part):
            i, t = tile_b(QUAD * g)
            c, at = part // 2, part % 2 * (CH // 2)
            if part == 0:
                pe.wait_ge(exped, QUAD * (g + 1))
            if t == 0 and i > 0:
                pe.wait_ge(evacuated, 2 * (i // QUAD) + c - 1)
            for j in range(QUAD):
                b, h = heads[i + j]
                last = nc.tensor.matmul(kit.bank(6 + c)[32 * j:32 * j + 32, at:at + CH // 2], v[:, KT * b + t, h // 2 * 2:h // 2 * 2 + 2, :],
                                        probs[:, (QUAD * g + j) % RING, c * CH + at:c * CH + at + CH // 2],
                                        start=t == 0 and at == 0, stop=t == KT - 1 and at > 0)
            last.then_inc(summed, 1)

        def take(act, quad, c):
            act.wait_ge(summed, QUAD * (KT * (quad + 1) - 1) + 2 * (c + 1))
            if quad >= 2:
                act.wait_ge(stored[quad % 2], 16 * 2 * QUAD * (quad // 2))
            nc.scalar.activation(evac[:, quad % 2, c * CH:(c + 1) * CH], kit.bank(6 + c), ACT.Copy).then_inc(evacuated, 1)

        @block.tensor
        def _(pe):
            def half_a(n, c):
                i, t = n // KT, n % KT
                r = i % STACKS
                if t == 0:
                    pe.wait_ge(stacked[r], 16 * 2 * PARTS * (i // STACKS + 1))
                if n >= 1:
                    pe.wait_ge(maxed, 2 * n + c - 1)
                nc.tensor.matmul(kit.bank(c), qs[0:PAIR_ROWS, r, t * P:(t + 1) * P],
                                 ks[0:PAIR_ROWS, r, c * CH:(c + 1) * CH], start=True, stop=True).then_inc(scores_a, 1)

            def full_b(u):
                i, t = tile_b(u)
                r = i % STACKS
                if t == 0:
                    pe.wait_ge(max_placed[i % QUAD], 16 * 4 * (i // QUAD + 1))
                if u >= 2:
                    pe.wait_ge(exped, u - 1)
                for c in range(2):
                    last = nc.tensor.matmul(banks_b[u % 2][:, c * CH:(c + 1) * CH], ks[0:FULL_ROWS, r, t * P:(t + 1) * P],
                                            qs[0:FULL_ROWS, r, c * CH:(c + 1) * CH], start=True, stop=True)
                last.then_inc(scores_b, 1)

            for n in range(n_tiles + AHEAD):
                u = n - AHEAD
                if n < n_tiles:
                    half_a(n, 0)
                if u >= 0:
                    full_b(u)
                if n < n_tiles:
                    half_a(n, 1)
                if u >= QUAD:
                    weigh(pe, u // QUAD - 1, u % QUAD)
            for part in range(QUAD):
                weigh(pe, n_tiles // QUAD - 1, part)

        @block.gpsimd
        def _(pool):
            for i in range(n_heads):
                r = i % 2
                part = [max_parts[:, r, KT * j:KT * j + KT] for j in range(PARTS)]
                pool.wait_ge(combined, i + 1)
                if i >= 2:
                    pool.wait_ge(max_turned, i - 1)
                nc.gpsimd.tensor_copy(part[0], neg_max[:, r]).then_inc(own, 1)
                pool.wait_ge(own, 3 * i + 1)
                nc.gpsimd.tensor_tensor(max_rest[:, r], neg_max[:, r], part[0], ALU.subtract).then_inc(own, 1)
                pool.wait_ge(own, 3 * i + 2)
                nc.gpsimd.tensor_copy(part[1], max_rest[:, r]).then_inc(own, 1)
                pool.wait_ge(own, 3 * i + 3)
                nc.gpsimd.tensor_tensor(part[2], max_rest[:, r], part[1], ALU.subtract).then_inc(max_split, 1)

        @block.vector
        def _(dve):
            def turn(i):
                dve.wait_ge(max_split, i + 1)
                if i >= 2:
                    dve.wait_ge(max_placed[(i - 2) % QUAD], 16 * 4 * ((i - 2) // QUAD + 1))
                nc.vector.transpose(turned[:, i % 2], max_parts[:, i % 2]).then_inc(max_turned, 1)

            nc.vector.memset(squares, 0.0)
            for i in range(n_heads):
                for t in range(KT):
                    if t == 2 and i >= 1:
                        turn(i - 1)
                    for c in range(2):
                        dve.wait_ge(scores_a, 2 * (KT * i + t) + c + 1)
                        nc.vector.tensor_reduce(half_max[:, i % 2, t, c:c + 1], kit.bank(c), AX.X, ALU.max, negate=True).then_inc(maxed, 1)
                dve.wait_ge(maxed, 2 * KT * (i + 1))
                if i >= 2:
                    dve.wait_ge(max_split, i - 1)
                nc.vector.tensor_tensor(neg_max[:, i % 2].unsqueeze(2), half_max[:, i % 2, :, 0:1], half_max[:, i % 2, :, 1:2], ALU.min).then_inc(combined, 1)
            turn(n_heads - 1)

            quads = HEADS // QUAD
            for step, (b, last, rows) in enumerate([(0, quads - 1, slice(0, P)), (1, 2 * quads - 2, slice(0, 96)),
                                                    (1, 2 * quads - 1, slice(96, P))]):
                for r in range(2):
                    dve.wait_ge(stored[r], 16 * 2 * QUAD * ((last - r) // 2 + 1))
                inv, sums_v = den[rows, b * SEQ:(b + 1) * SEQ], kit.slot(out)[rows, b * SEQ:(b + 1) * SEQ]
                nc.vector.reciprocal(inv, inv).then_inc(inverted, 1)
                dve.wait_ge(inverted, step + 1)
                nc.vector.tensor_tensor(sums_v, sums_v, inv, ALU.mult)

        @block.sync
        def _(sp):
            def stack(i):
                b, h = heads[i]
                if i >= STACKS:
                    sp.wait_ge(scores_b, QUAD_TILES * ((i - STACKS) // QUAD + 1))
                for j in range(PARTS):
                    rows = slice(BLOCK_ROWS * j, BLOCK_ROWS * (j + 1))
                    part = split[DH * h:DH * h + DH, 0, j:j + 1, b * SEQ:(b + 1) * SEQ].broadcast_to([DH, PARTS, SEQ])
                    sp.dma_start(qs[rows, i % STACKS, :], part).then_inc(stacked[i % STACKS], 16)
                    sp.dma_start(ks[rows, i % STACKS, :],
                                 split[DH * h:DH * h + DH, 1, :, b * SEQ:(b + 1) * SEQ]).then_inc(stacked[i % STACKS], 16)

            def store(quad):
                sp.wait_ge(evacuated, 2 * (quad + 1))
                for j in range(QUAD):
                    b, h = heads[QUAD * quad + j]
                    row = 32 * j + 16 * (h % 2)
                    for dst, r in ((kit.slot(out), row), (den, row + DH)):
                        sp.dma_start(dst[DH * h:DH * h + DH, b * SEQ:(b + 1) * SEQ], evac[r:r + DH, quad % 2]).then_inc(stored[quad % 2], 16)

            for i in range(QUAD):
                stack(i)
            for i in range(n_heads):
                sp.wait_ge(max_turned, i + 1)
                rows = qs[PAIR_ROWS:FULL_ROWS, i % STACKS, :].rearrange("p (n b t) -> p n b t", n=KT, t=SQ)
                for b in range(P // SQ):
                    sp.dma_start(rows[:, :, b, :], turned[SQ * b:SQ * b + PARTS * KT, i % 2]).then_inc(max_placed[i % QUAD], 16)
                if i + QUAD < n_heads:
                    stack(i + QUAD)
                if i >= 10 and i % QUAD == 2:
                    store((i - 10) // QUAD)
            for quad in range((n_heads - 11) // QUAD + 1, n_quads):
                store(quad)
            for r in range(2):
                sp.wait_ge(stored[r], 16 * 2 * QUAD * (n_quads // 2))

        @block.scalar
        def _(act):
            for u in range(n_tiles):
                act.wait_ge(scores_b, u + 1)
                if u >= RING:
                    act.wait_ge(summed, QUAD * ((u - RING) // QUAD + 1))
                nc.scalar.activation(probs[:, u % RING, :], banks_b[u % 2], ACT.Exp, scale=scale).then_inc(exped, 1)
                if u % QUAD_TILES in (2, 4) and u >= QUAD_TILES:
                    take(act, u // QUAD_TILES - 1, u % QUAD_TILES // 4)
            for c in range(2):
                take(act, n_quads - 1, c)



E1_HID = 256
E1_COLS = 3 * E1_HID


def experts_swiglu(kit, name, landed, xn, weights, blocks, up, gate, down, gates, acts):
    nc = kit.nc
    steps = [(m, c) for m in range(blocks) for c in range(NC)]
    with Stage(kit, name) as st:
        product, silu_done, gated, weighted = map(st.sem, ("product", "silu", "gated", "weighted"))
        block = st.block()

        def weight(a):
            return kit.experts[:, a:a + P]

        @block.tensor
        def _(pe):
            pe.wait_ge(landed, 16)
            for i in range(len(steps) + 2):
                if i < len(steps):
                    m, c = steps[i]
                    if i >= 2:
                        pe.wait_ge(gated, i - 1)
                    nc.tensor.matmul(kit.bank(2 * (i % 2)), weight(gate(m)), kit.chunk(xn, c), start=True, stop=True)
                    nc.tensor.matmul(kit.bank(2 * (i % 2) + 1), weight(up(m)), kit.chunk(xn, c), start=True,
                                     stop=True).then_inc(product, 1)
                if i >= 2:
                    m, c = steps[i - 2]
                    if weights(m) is None:
                        pe.wait_ge(gated, i - 1)
                    else:
                        pe.wait_ge(weighted, i - 1)
                    nc.tensor.matmul(kit.bank(4 + c), weight(down(m)), kit.chunk(acts, (i - 2) % 4), start=m == 0,
                                     stop=m == blocks - 1)

        @block.scalar
        def _(act):
            for i, (m, c) in enumerate(steps):
                act.wait_ge(product, i + 1)
                if i >= 4:
                    act.wait_ge(gated, i - 2)
                nc.scalar.activation(kit.chunk(gates, i % 4), kit.bank(2 * (i % 2)), ACT.Silu).then_inc(silu_done, 1)

        @block.vector
        def _(dve):
            for i, (m, c) in enumerate(steps):
                dve.wait_ge(silu_done, i + 1)
                w = weights(m)
                nc.vector.tensor_tensor(kit.chunk(gates, i % 4) if w is not None else kit.chunk(acts, i % 4), kit.chunk(gates, i % 4),
                                        kit.bank(2 * (i % 2) + 1), ALU.mult).then_inc(gated, 1)
                if w is not None:
                    dve.wait_ge(gated, i + 1)
                    nc.vector.tensor_tensor(kit.chunk(acts, i % 4), kit.chunk(gates, i % 4), kit.chunk(w, c), ALU.mult).then_inc(weighted, 1)



def norm_attention(kit, name, xn, out, square, scaled, q, tq, values, probs, turned, result):
    nc = kit.nc
    norm, inv, row_scale = (kit.scratch[:, a:a + NT] for a in (0, 16, 32))
    neg_max, row_sum, inv_sum = (kit.scratch[:, a:a + NT] for a in (48, 64, 80))
    diag = kit.slot(square).rearrange("p (j q) -> p j q", q=P)
    with Stage(kit, name + "_rows") as st:
        squared, sum_ready, norm_ready, diag_ready, bcast_ready, own = map(st.sem, ("squared", "sum", "norm", "diag", "bcast", "own"))
        block = st.block()

        @block.tensor
        def _(pe):
            for j in range(NT):
                pe.wait_ge(squared, j // 4 + 1)
                last = nc.tensor.matmul(kit.psum[:, 4, j:j + 1], kit.slot(square)[:, j * P:(j + 1) * P],
                                        kit.c("ones")[:, 0:1], start=True, stop=True)
            last.then_inc(sum_ready, 1)
            pe.wait_ge(diag_ready, 1)
            for c in range(NC):
                nc.tensor.matmul(kit.bank(c), kit.c("ones"), kit.chunk(square, c), start=True, stop=True).then_inc(bcast_ready, 1)

        @block.scalar
        def _(act):
            for c in range(NC):
                nc.scalar.activation(kit.chunk(square, c), kit.chunk(xn, c), ACT.Square).then_inc(squared, 1)
            act.wait_ge(sum_ready, 1)
            nc.scalar.activation(norm, kit.psum[:, 4, 0:NT], ACT.Sqrt).then_inc(norm_ready, 1)

        @block.vector
        def _(dve):
            dve.wait_ge(norm_ready, 1)
            nc.vector.tensor_scalar(inv, norm, 1e-9, None, ALU.add).then_inc(own, 1)
            dve.wait_ge(own, 1)
            nc.vector.reciprocal(inv, inv).then_inc(own, 1)
            dve.wait_ge(own, 2)
            nc.vector.tensor_tensor(diag, kit.c("ident").unsqueeze(1).broadcast_to([P, NT, P]), spread(inv, P),
                                    ALU.mult).then_inc(diag_ready, 1)
            for c in range(NC):
                dve.wait_ge(bcast_ready, c + 1)
                nc.vector.tensor_tensor(kit.chunk(scaled, c), kit.chunk(xn, c), kit.bank(c), ALU.mult)

    project(kit, name + "_q", [(q, "q2", scaled, "bq2", None)])
    project(kit, name + "_tq", [(tq, "anomaly", q, None, None)])
    scale = 1.0 / float(np.sqrt(np.float32(P)))
    v = kit.slot(values).rearrange("p (j n) -> p j n", n=P)
    p_ring = kit.slot(probs).rearrange("p (r t) -> p r t", t=SEQ)
    pt_ring = kit.slot(turned).rearrange("p (r t) -> p r t", t=SEQ)
    res = kit.slot(result).rearrange("p (j n) -> p j n", n=P)
    with Stage(kit, name + "_v") as st:
        v_ready = st.sem("v")
        block = st.block()

        @block.tensor
        def _(pe):
            for j in range(NT):
                nc.tensor.matmul(kit.bank(j // 4)[:, (j % 4) * P:(j % 4 + 1) * P], kit.slot(scaled)[:, j * P:(j + 1) * P],
                                 kit.w("v2"), start=True, stop=True).then_inc(v_ready, 1)

        @block.vector
        def _(dve):
            for g in range(4):
                dve.wait_ge(v_ready, 4 * g + 4)
                nc.vector.tensor_tensor(v[:, 4 * g:4 * g + 4, :], kit.bank(g).rearrange("p (j n) -> p j n", n=P),
                                        kit.w("bv2").unsqueeze(1).broadcast_to([P, 4, P]), ALU.add)

    with Stage(kit, name) as st:
        scores, maxed, bias_ready, exped, p_turned = map(st.sem, ("scores", "maxed", "bias", "exped", "p_turned"))
        pt_copied, ctx_ready, ctx_scaled, ctx_turned, copied, own = map(st.sem, ("pt", "ctx", "ctx_scaled", "ctx_turned", "copied", "own"))
        block = st.block()

        @block.tensor
        def _(pe):
            for i in range(NT + 3):
                if i < NT:
                    if i >= 2:
                        pe.wait_ge(exped, i - 1)
                    a = i // KT * SEQ
                    for c in range(2):
                        last = nc.tensor.matmul(kit.bank(2 * (i % 2) + c), kit.slot(q)[:, i * P:(i + 1) * P],
                                                kit.slot(tq)[:, a + c * CH:a + (c + 1) * CH], start=True, stop=True)
                    last.then_inc(scores, 1)
                if 1 <= i <= NT:
                    t = i - 1
                    pe.wait_ge(exped, t + 1)
                    if t >= 1:
                        pe.wait_ge(pt_copied, t)
                    for n in range(KT):
                        last = nc.tensor.transpose(kit.bank(4 + n // 4)[:, (n % 4) * P:(n % 4 + 1) * P],
                                                   p_ring[:, t % 2, n * P:(n + 1) * P], kit.c("ident"))
                    last.then_inc(p_turned, 1)
                if 2 <= i <= NT + 1:
                    t = i - 2
                    pe.wait_ge(pt_copied, t + 1)
                    if t >= 1:
                        pe.wait_ge(ctx_scaled, t)
                    for n in range(KT):
                        last = nc.tensor.matmul(kit.bank(6)[:, 0:P], pt_ring[:, t % 2, n * P:(n + 1) * P],
                                                v[:, t // KT * KT + n, :], start=n == 0, stop=n == KT - 1)
                    last.then_inc(ctx_ready, 1)
                if i >= 3:
                    t = i - 3
                    pe.wait_ge(ctx_scaled, t + 1)
                    if t >= 1:
                        pe.wait_ge(copied, t)
                    nc.tensor.transpose(kit.bank(7)[:, 0:P], res[:, t, :], kit.c("ident")).then_inc(ctx_turned, 1)

        @block.scalar
        def _(act):
            for i in range(NT + 3):
                if i < NT:
                    act.wait_ge(bias_ready, i + 1)
                    if i >= 2:
                        act.wait_ge(p_turned, i - 1)
                    nc.scalar.activation(p_ring[:, i % 2, :], kit.psum[:, 2 * (i % 2):2 * (i % 2) + 2, :].rearrange("p a b -> p (a b)"),
                                         ACT.Exp, bias=neg_max[:, i:i + 1], scale=scale, accum_out=row_sum[:, i:i + 1]).then_inc(exped, 1)
                if i >= 3:
                    t = i - 3
                    act.wait_ge(ctx_turned, t + 1)
                    nc.scalar.activation(kit.slot(out)[:, t * P:(t + 1) * P], kit.bank(7)[:, 0:P], ACT.Copy).then_inc(copied, 1)

        @block.vector
        def _(dve):
            for i in range(NT + 2):
                if i < NT:
                    dve.wait_ge(scores, i + 1)
                    nc.vector.tensor_reduce(neg_max[:, i:i + 1], kit.psum[:, 2 * (i % 2):2 * (i % 2) + 2, :].rearrange("p a b -> p (a b)"),
                                            AX.X, ALU.max, negate=True).then_inc(maxed, 1)
                    dve.wait_ge(maxed, i + 1)
                    nc.vector.tensor_scalar(neg_max[:, i:i + 1], neg_max[:, i:i + 1], scale, None, ALU.mult).then_inc(bias_ready, 1)
                if 1 <= i <= NT:
                    t = i - 1
                    dve.wait_ge(p_turned, t + 1)
                    if t >= 2:
                        dve.wait_ge(ctx_ready, t - 1)
                    nc.vector.tensor_copy(pt_ring[:, t % 2, :], kit.psum[:, 4:6, :].rearrange("p a b -> p (a b)")).then_inc(pt_copied, 1)
                if i >= 2:
                    t = i - 2
                    dve.wait_ge(ctx_ready, t + 1)
                    dve.wait_ge(exped, t + 1)
                    nc.vector.reciprocal(inv_sum[:, t:t + 1], row_sum[:, t:t + 1]).then_inc(own, 1)
                    dve.wait_ge(own, t + 1)
                    nc.vector.tensor_scalar(res[:, t, :], kit.bank(6)[:, 0:P], inv_sum[:, t:t + 1], norm[:, t:t + 1],
                                            ALU.mult, ALU.mult).then_inc(ctx_scaled, 1)



def wkv_inputs(kit, name, xn, xx, r, kk, v_in, g, w, v, mix, t0, t1):
    nc = kit.nc
    with Stage(kit, name + "_mix") as st:
        own, mix_ready, tanh_ready = map(st.sem, ("own", "mix", "tanh"))
        m_ready, m_used = st.sem("m"), st.sem("m_used")
        block = st.block()
        targets = (w, kk, v_in, r, g)

        @block.vector
        def _(dve):
            for b in range(BATCH):
                a, z = b * SEQ, (b + 1) * SEQ
                nc.vector.tensor_tensor(kit.slot(xx)[:, a + 1:z], kit.slot(xn)[:, a:z - 1], kit.slot(xn)[:, a + 1:z], ALU.subtract)
                nc.vector.tensor_scalar(kit.slot(xx)[:, a:a + 1], kit.slot(xn)[:, a:a + 1], -1.0, None, ALU.mult).then_inc(own, 1)
            dve.wait_ge(own, 2)
            nc.vector.scalar_tensor_tensor(kit.slot(t0), kit.slot(xx), kit.w("maa_x"), kit.slot(xn), ALU.mult, ALU.add).then_inc(own, 1)
            for n in range(5 * NC):
                s, c = n // NC, n % NC
                dve.wait_ge(m_ready, n + 1)
                nc.vector.scalar_tensor_tensor(kit.chunk(targets[s], c), kit.bank(4 + n % 4), kit.w("maa")[:, s:s + 1], kit.chunk(xx, c),
                                               ALU.add, ALU.mult).then_inc(m_used, 1)
                dve.wait_ge(m_used, n + 1)
                nc.vector.tensor_tensor(kit.chunk(targets[s], c), kit.chunk(targets[s], c), kit.chunk(xn, c), ALU.add)

        @block.tensor
        def _(pe):
            pe.wait_ge(own, 3)
            for n in range(2 * NC):
                c = n % NC
                if n >= NC:
                    pe.wait_ge(tanh_ready, c + 1)
                m = P if n < NC else 32
                nc.tensor.matmul(kit.bank(c)[0:m], kit.w("maa_w1")[:, n // NC * P:n // NC * P + m], kit.chunk(t0, c),
                                 start=True, stop=True).then_inc(mix_ready, 1)
            for n in range(5 * NC):
                s, c = n // NC, n % NC
                pe.wait_ge(tanh_ready, NC * (s // 4) + c + 1)
                if n >= 4:
                    pe.wait_ge(m_used, n - 3)
                weight, k = (kit.w("maa_w2")[:, P * s:P * s + P], P) if s < 4 else (kit.w("maa_w2_g"), 32)
                nc.tensor.matmul(kit.bank(4 + n % 4), weight, kit.chunk(mix + s // 4, c)[0:k], start=True, stop=True).then_inc(m_ready, 1)

        @block.scalar
        def _(act):
            for n in range(2 * NC):
                m, c = (P if n < NC else 32), n % NC
                act.wait_ge(mix_ready, n + 1)
                nc.scalar.activation(kit.chunk(mix + n // NC, c)[0:m], kit.bank(c)[0:m], ACT.Tanh).then_inc(tanh_ready, 1)

    with Stage(kit, name + "_decay") as st:
        low, tanh_done, full, exp_done = map(st.sem, ("low", "tanh", "full", "exp"))
        block = st.block()

        @block.tensor
        def _(pe):
            for c in range(NC):
                nc.tensor.matmul(kit.bank(c)[0:64], kit.w("decay_w1"), kit.chunk(w, c), start=True, stop=True).then_inc(low, 1)
            for c in range(NC):
                pe.wait_ge(tanh_done, c + 1)
                nc.tensor.matmul(kit.bank(4 + c), kit.w("decay_w2"), kit.chunk(t1, c)[0:64], start=True, stop=True).then_inc(full, 1)

        @block.scalar
        def _(act):
            for c in range(NC):
                act.wait_ge(low, c + 1)
                nc.scalar.activation(kit.chunk(t1, c)[0:64], kit.bank(c)[0:64], ACT.Tanh).then_inc(tanh_done, 1)
            for c in range(NC):
                act.wait_ge(full, c + 1)
                nc.scalar.activation(kit.chunk(w, c), kit.bank(4 + c), ACT.Exp, bias=kit.w("decay")).then_inc(exp_done, 1)
                act.wait_ge(exp_done, 2 * c + 1)
                nc.scalar.activation(kit.chunk(w, c), kit.chunk(w, c), ACT.Exp, scale=-1.0).then_inc(exp_done, 1)

    project(kit, name + "_rkvg", [(r, "Wr", r, None, None), (kk, "Wk", kk, None, None), (v, "Wv", v_in, None, None),
                                  (g, "Wg", g, None, None)])


def wkv(kit, name, r, kk, v_in, v, w, y, rd, t0, t1, head_decay, tail_decay, key_even, key_odd, v_tok, states):
    nc = kit.nc

    def by_chunk(slot):
        return kit.slot(slot).rearrange("p (n t) -> p n t", t=WC)

    R, K, V, W_, Y, RD, T0, T1 = map(by_chunk, (r, kk, v, w, y, rd, t0, t1))
    ring = [T0, T1, by_chunk(head_decay), by_chunk(tail_decay)]
    PER = NWC // NC

    with Stage(kit, name + "_near") as st:
        pair, spread_ready, used, own = map(st.sem, ("pair", "spread", "used", "own"))
        added = st.sem("added")
        block = st.block()

        @block.vector
        def _(dve):
            done = [0]

            def then(instruction):
                done[0] += 1
                instruction.then_inc(own, 1)
                dve.wait_ge(own, done[0])

            def produce(d):
                T = ring[d % 4]
                if d >= 4:
                    dve.wait_ge(added, d - 3)
                if d == 0:
                    nc.vector.scalar_tensor_tensor(T[:, :, :], R[:, :, :], kit.w("faaaa"), K[:, :, :], ALU.mult, ALU.mult).then_inc(pair, 1)
                    return
                if d == 1:
                    then(nc.vector.tensor_copy(RD[:, :, 1:], R[:, :, 1:]))
                else:
                    dve.wait_ge(pair, d)
                    then(nc.vector.tensor_tensor(RD[:, :, d:], RD[:, :, d:], W_[:, :, 1:WC - d + 1], ALU.mult))
                nc.vector.tensor_tensor(T[:, :, d:], RD[:, :, d:], K[:, :, 0:WC - d], ALU.mult).then_inc(pair, 1)

            produce(0)
            produce(1)
            for d in range(WC):
                if d + 2 < WC:
                    produce(d + 2)
                dve.wait_ge(spread_ready, d + 1)
                n = WC - d
                bank = kit.psum[:, 4 * (d % 2):4 * (d % 2) + 4, 0:PER * n].rearrange("p b (m t) -> p b m t", t=n)
                T = ring[d % 4]
                Tv, Vv = (kit_slot.rearrange("p (b m) t -> p b m t", b=NC) for kit_slot in (T[:, :, d:], V[:, :, 0:n]))
                nc.vector.tensor_tensor(Tv, bank, Vv, ALU.mult).then_inc(used, 1)

        @block.gpsimd
        def _(pool):
            for d in range(WC):
                T = ring[d % 4]
                pool.wait_ge(used, d + 1)
                if d == 0:
                    nc.gpsimd.tensor_copy(kit.slot(y), kit.slot(t0)).then_inc(added, 1)
                else:
                    pool.wait_ge(added, d)
                    nc.gpsimd.tensor_tensor(Y[:, :, d:], Y[:, :, d:], T[:, :, d:], ALU.add).then_inc(added, 1)

        @block.tensor
        def _(pe):
            for d in range(WC):
                n = WC - d
                T = ring[d % 4]
                pe.wait_ge(pair, d + 1)
                if d >= 2:
                    pe.wait_ge(used, d - 1)
                for c in range(NC):
                    last = nc.tensor.matmul(kit.bank(4 * (d % 2) + c)[:, 0:PER * n], kit.c("head_ones"),
                                            T[:, c * PER:(c + 1) * PER, d:], start=True, stop=True)
                last.then_inc(spread_ready, 1)

    HD, TD = by_chunk(head_decay), by_chunk(tail_decay)
    ke = kit.slot(key_even).rearrange("p (j n) -> p j n", n=P)
    ko = kit.slot(key_odd).rearrange("p (j n) -> p j n", n=P)
    vt = kit.slot(v_tok).rearrange("p (j n) -> p j n", n=P)
    whole = kit.scratch[:, 0:NWC]
    with Stage(kit, name + "_far") as st:
        own, turned, turned_used, v_ready, keys_ready = map(st.sem, ("own", "turned", "turned_used", "v", "keys"))
        block = st.block()

        @block.vector
        def _(dve):
            done = [0]

            def then(instruction):
                done[0] += 1
                instruction.then_inc(own, 1)
                dve.wait_ge(own, done[0])

            then(nc.vector.tensor_copy(T0[:, :, 1:], W_[:, :, 0:WC - 1]))
            then(nc.vector.memset(T0[:, :, 0:1], 0.0))
            starts = kit.c("start").unsqueeze(1).broadcast_to([P, NWC, WC])
            then(nc.vector.tensor_copy(T1[:, :, :], starts))
            then(nc.vector.tensor_tensor_scan(kit.slot(head_decay), kit.slot(t0), kit.slot(t1), 0.0, ALU.mult, ALU.add))
            nc.vector.tensor_tensor(whole.unsqueeze(2), HD[:, :, WC - 1:WC], W_[:, :, WC - 1:WC], ALU.mult)
            then(nc.vector.tensor_tensor(kit.slot(rd), kit.slot(r), kit.slot(head_decay), ALU.mult))
            then(nc.vector.tensor_copy(T0[:, :, 0:WC - 1], W_[:, :, 1:WC]))
            then(nc.vector.memset(T0[:, :, WC - 1:WC], 0.0))
            then(nc.vector.tensor_copy(T1[:, :, ::-1], starts))
            then(nc.vector.tensor_tensor_scan(kit.slot(tail_decay)[:, ::-1], kit.slot(t0)[:, ::-1], kit.slot(t1)[:, ::-1],
                                              0.0, ALU.mult, ALU.add))
            nc.vector.tensor_tensor(kit.slot(kk), kit.slot(kk), kit.slot(tail_decay), ALU.mult).then_inc(keys_ready, 1)
            for g in range(4):
                dve.wait_ge(turned, 4 * g + 4)
                bank = kit.bank(g).rearrange("p (j n) -> p j n", n=P)
                nc.vector.tensor_scalar(ke[:, 4 * g:4 * g + 4, :], bank, kit.c("even"), None, ALU.mult)
                nc.vector.tensor_scalar(ko[:, 4 * g:4 * g + 4, :], bank, kit.c("odd"), None, ALU.mult)

        @block.tensor
        def _(pe):
            for j in range(NT):
                nc.tensor.matmul(kit.bank(4 + j // 4)[:, (j % 4) * P:(j % 4 + 1) * P], kit.slot(v_in)[:, j * P:(j + 1) * P],
                                 kit.w("Wv"), start=True, stop=True).then_inc(v_ready, 1)
            pe.wait_ge(keys_ready, 1)
            for j in range(NT):
                nc.tensor.transpose(kit.bank(j // 4)[:, (j % 4) * P:(j % 4 + 1) * P], kit.slot(kk)[:, j * P:(j + 1) * P],
                                    kit.c("ident")).then_inc(turned, 1)

        @block.scalar
        def _(act):
            for g in range(4):
                act.wait_ge(v_ready, 4 * g + 4)
                nc.scalar.activation(vt[:, 4 * g:4 * g + 4, :], kit.bank(4 + g).rearrange("p (j n) -> p j n", n=P), ACT.Copy)

    state = flat_slots(kit, states, 4).rearrange("p (n i) -> p n i", i=WKV_HEAD)
    GROUP = 4
    GROUPS = NWC // GROUP
    with Stage(kit, name + "_state") as st:
        kv_ready, state_ready, first_state, state_own, y_ready = map(st.sem, ("kv", "state", "first", "state_own", "y"))
        block = st.block()

        def kv(g, n):
            return kit.bank(2 * (g % 2) + n // 2)[:, 64 * (n % 2):64 * (n % 2) + 64]

        @block.tensor
        def _(pe):
            def read(g):
                pe.wait_ge(state_ready, g + 1)
                for n in range(GROUP):
                    c = g * GROUP + n
                    at = c % PER * WC
                    for h in range(2):
                        rows = slice(64 * h, 64 * h + 64)
                        last = nc.tensor.matmul(kit.bank(4 + c // PER)[rows, at:at + WC], state[rows, c, :],
                                                kit.slot(rd)[rows, c * WC:(c + 1) * WC], start=True, stop=True)
                last.then_inc(y_ready, 1)

            for g in range(GROUPS):
                if g >= 2:
                    pe.wait_ge(state_ready, g - 1)
                for n in range(GROUP):
                    row = 64 * (g % 2) + 32 * (n // 2)
                    keys = (ke, ko)[n % 2]
                    for h in range(2):
                        head = slice(64 * h, 64 * h + 64)
                        last = nc.tensor.matmul(kv(g, n)[head], keys[row:row + 32, g // 2, head], vt[row:row + 32, g // 2, head],
                                                start=True, stop=True)
                last.then_inc(kv_ready, 1)
                if g >= 2:
                    read(g - 2)
            read(GROUPS - 2)
            read(GROUPS - 1)

        @block.vector
        def _(dve):
            own = 0
            for b in range(BATCH):
                nc.vector.memset(state[:, b * (NWC // 2), :], 0.0).then_inc(first_state, 1)
            dve.wait_ge(first_state, BATCH)
            for g in range(GROUPS):
                dve.wait_ge(kv_ready, g + 1)
                final = GROUP - 2 if (g + 1) % (GROUPS // BATCH) == 0 else GROUP - 1
                for n in range(final + 1):
                    c = g * GROUP + n
                    update = nc.vector.scalar_tensor_tensor(state[:, c + 1, :], state[:, c, :], whole[:, c:c + 1],
                                                            kv(g, n), ALU.mult, ALU.add)
                    if n < final:
                        update.then_inc(state_own, 1)
                        own += 1
                        dve.wait_ge(state_own, own)
                    else:
                        update.then_inc(state_ready, 1)
                        dve.wait_ge(state_ready, g + 1)
            for c in range(NC):
                dve.wait_ge(y_ready, GROUPS // NC * (c + 1))
                nc.vector.tensor_tensor(kit.chunk(y, c), kit.chunk(y, c), kit.bank(4 + c), ALU.add)


def group_norm(kit, name, y, square, stat, g):
    nc = kit.nc
    with Stage(kit, name) as st:
        mean_ready, centered, squared, var_ready, std_ready, own = map(st.sem, ("mean", "centered", "squared", "var", "std", "own"))
        silu_done = st.sem("silu")
        block = st.block()

        @block.tensor
        def _(pe):
            for c in range(NC):
                nc.tensor.matmul(kit.bank(c), kit.c("head_mean"), kit.chunk(y, c), start=True, stop=True).then_inc(mean_ready, 1)
            for c in range(NC):
                pe.wait_ge(squared, c + 1)
                nc.tensor.matmul(kit.bank(4 + c), kit.c("head_mean"), kit.chunk(square, c), start=True, stop=True).then_inc(var_ready, 1)

        @block.scalar
        def _(act):
            for c in range(NC):
                act.wait_ge(centered, c + 1)
                nc.scalar.activation(kit.chunk(square, c), kit.chunk(y, c), ACT.Square).then_inc(squared, 1)
            for c in range(NC):
                act.wait_ge(var_ready, c + 1)
                nc.scalar.activation(kit.chunk(stat, c), kit.bank(4 + c), ACT.Sqrt, bias=kit.c("eps_wkv")).then_inc(std_ready, 1)
            for c in range(NC):
                nc.scalar.activation(kit.chunk(g, c), kit.chunk(g, c), ACT.Silu).then_inc(silu_done, 1)

        @block.vector
        def _(dve):
            done = [0]

            def then(instruction):
                done[0] += 1
                instruction.then_inc(own, 1)
                dve.wait_ge(own, done[0])

            for c in range(NC):
                dve.wait_ge(mean_ready, c + 1)
                nc.vector.tensor_tensor(kit.chunk(y, c), kit.chunk(y, c), kit.bank(c), ALU.subtract).then_inc(centered, 1)
            for c in range(NC):
                dve.wait_ge(std_ready, c + 1)
                then(nc.vector.reciprocal(kit.chunk(stat, c), kit.chunk(stat, c)))
                then(nc.vector.scalar_tensor_tensor(kit.chunk(y, c), kit.chunk(y, c), kit.w("ln_w"), kit.chunk(stat, c), ALU.mult, ALU.mult))
                dve.wait_ge(silu_done, c + 1)
                nc.vector.scalar_tensor_tensor(kit.chunk(y, c), kit.chunk(y, c), kit.w("ln_b"), kit.chunk(g, c), ALU.add, ALU.mult)



E3_COLS = HID + HB * P
E3_RING = 6


def experts_relu(kit, name, dram, landed, xn, weights, rows, hidden_slots):
    nc = kit.nc
    n_exp = 8
    steps = [(e, c) for e in range(n_exp) for c in range(NC)]

    def w1(e, m):
        a = e % E3_RING * E3_COLS + m * P
        return kit.experts[:, a:a + P]

    def w2(e, k):
        return w1(e, HB + k)

    with Stage(kit, name) as st:
        hidden, relu_done, weighted, expert_done = map(st.sem, ("hidden", "relu", "weighted", "expert_done"))
        block = st.block()

        @block.sync
        def _(sp):
            for e in range(E3_RING, n_exp):
                r = e % E3_RING
                sp.wait_ge(expert_done, e - E3_RING + 1)
                sp.dma_start(kit.experts[:, r * E3_COLS:(r + 1) * E3_COLS], dram[e]).then_inc(landed[r], 16)

        @block.tensor
        def _(pe):
            for i in range(len(steps) + 1):
                if i < len(steps):
                    e, c = steps[i]
                    if c == 0:
                        pe.wait_ge(landed[e % E3_RING], 16 * (e // E3_RING + 1))
                    for m in range(HB):
                        if i >= 1:
                            pe.wait_ge(relu_done, HB * (i - 1) + m + 1)
                        nc.tensor.matmul(kit.bank(m), w1(e, m), kit.chunk(xn, c), start=True, stop=True).then_inc(hidden, 1)
                if i >= 1:
                    e, c = steps[i - 1]
                    pe.wait_ge(weighted, i)
                    if e == 0:
                        nc.tensor.matmul(kit.bank(4 + c), kit.w("f_b2"), kit.chunk(rows, c)[0:n_exp], start=True, stop=False)
                    for k in range(HB):
                        last = nc.tensor.matmul(kit.bank(4 + c), w2(e, k), kit.chunk(hidden_slots[(i - 1) % 2], k), start=False,
                                                stop=e == n_exp - 1 and k == HB - 1)
                    if c == NC - 1:
                        last.then_inc(expert_done, 1)

        @block.scalar
        def _(act):
            for i, (e, c) in enumerate(steps):
                for m in range(HB):
                    act.wait_ge(hidden, HB * i + m + 1)
                    nc.scalar.activation(kit.chunk(hidden_slots[i % 2], m), kit.bank(m), ACT.Relu,
                                         bias=kit.w("f_b1")[:, HB * e + m:HB * e + m + 1]).then_inc(relu_done, 1)

        @block.vector
        def _(dve):
            for i, (e, c) in enumerate(steps):
                dve.wait_ge(relu_done, HB * (i + 1))
                h = kit.slot(hidden_slots[i % 2]).rearrange("p (m t) -> p m t", t=CH)
                nc.vector.tensor_tensor(h, h, kit.chunk(weights[e], c).unsqueeze(1).broadcast_to([P, HB, CH]),
                                        ALU.mult).then_inc(weighted, 1)


def add_banks(kit, name, dst, a):
    nc = kit.nc
    with Stage(kit, name) as st:
        block = st.block()

        @block.vector
        def _(dve):
            nc.vector.tensor_tensor(kit.slot(dst), kit.slot(a), kit.psum[:, 4:8, :].rearrange("p a b -> p (a b)"), ALU.add)



X, XN, RES = 0, 1, 2
WEIGHTS = list(range(5, 13))
SEL_SLOT = 15


def layer0(kit, dram, arrivals):
    landed = arrivals.experts[0]
    start_experts(kit, "x0", [dram[0], dram[1]], E0_COLS, landed)
    layer_norm(kit, "n0", X, XN, 3, 4)
    await_small(kit, arrivals)
    weights = [kit.slot(3 + e // 2).bitcast(BF16)[:, e % 2 * TOK:(e % 2 + 1) * TOK] for e in range(N_EXP0)]
    router(kit, "r0", XN, "tokens", None, 8, "half", rows=None, stacked=8, work=9, tmp=10)
    cast_selectors(kit, arrivals, SEL_SLOT)
    spread_rows(kit, "sp0", 8, range(8), weights)
    scan_inputs(kit, XN, low=14, delta=10, suffix=11, rows=15)
    halves = flat_slots(kit, 15, 3)
    experts_and_scan(kit, dram, landed, XN, weights, acc=2, h1=[7, 8], h2=[9, 10], delta=10, rows=15, stacked=14, rest=16,
                     du=13, suffix=11, y=12, halves=[halves[:, a * SEQ:(a + 1) * SEQ] for a in range(5)])
    project(kit, "scan_out", [(3, "W_out", 12, "b_out", None)])
    merge(kit, "m0", X, 3, 4, g=2)


def layer1(kit, dram, landed):
    layer_norm(kit, "n1", X, XN, 3, 4)
    attention(kit, "a1", XN, ("q1", "k1", "v1", None, None), RES, q_stack=3, k_stack=6, sums=9, values=11, work=13)
    start_experts(kit, "x1", [dram], 8 * E1_COLS, landed)
    project(kit, "o1", [(3, "o1", RES, None, XN)])
    router(kit, "r1", XN, "gate1", None, 8, "scores", rows=None, stacked=4, work=5, tmp=6)
    spread_rows(kit, "sp1", 4, range(8), [kit.slot(i) for i in WEIGHTS])
    experts_swiglu(kit, "e1", landed[0], XN, lambda m: WEIGHTS[m // 2], 16,
                   up=lambda m: m // 2 * E1_COLS + E1_HID + m % 2 * P, gate=lambda m: m // 2 * E1_COLS + m % 2 * P,
                   down=lambda m: m // 2 * E1_COLS + 2 * E1_HID + m % 2 * P, gates=13, acts=14)
    merge(kit, "m1", X, 3, 13)


def layer2(kit, dram, landed):
    start_experts(kit, "x2", [dram], 27 * P, landed)
    layer_norm(kit, "n2", X, XN, 3, 4)
    norm_attention(kit, "a2", XN, RES, 3, 4, 5, 6, 7, 8, 9, 10)
    router(kit, "r2", XN, "router", "router_bias", 16, "top", rows=None, stacked=4, work=5, tmp=6)
    spread_rows(kit, "sp2", 4, range(32, 40), [kit.slot(i) for i in WEIGHTS])
    experts_swiglu(kit, "e2", landed[0], XN, lambda m: WEIGHTS[m] if m < 8 else None, 9,
                   up=lambda m: (m if m < 8 else 25) * P, gate=lambda m: (8 + m if m < 8 else 24) * P,
                   down=lambda m: (16 + m if m < 8 else 26) * P, gates=13, acts=14)
    merge(kit, "m2", X, RES, 13)


def layer3(kit, dram, landed):
    layer_norm(kit, "n3", X, XN, 3, 4)
    wkv_inputs(kit, "w3", XN, xx=2, r=3, kk=4, v_in=5, g=6, w=7, v=8, mix=9, t0=14, t1=15)
    wkv(kit, "w3", r=3, kk=4, v_in=5, v=8, w=7, y=9, rd=2, t0=10, t1=11, head_decay=12, tail_decay=13, key_even=14,
        key_odd=15, v_tok=16, states=10)
    group_norm(kit, "gn", 9, 3, 4, 6)
    project(kit, "o3", [(RES, "Wo", 9, None, None)])

    layer_norm(kit, "f1", XN, 3, 4, 5, "ln1_g", "ln1_b")
    attention(kit, "a3", 3, ("q3", "k3", "v3", "bq3", "bk3"), 3, q_stack=4, k_stack=7, sums=10, values=12, work=14)
    start_experts(kit, "x3", [dram[e] for e in range(E3_RING)], E3_COLS, landed)
    add_bias(kit, "bv", 3, "bv3")
    project(kit, "fo", [(5, "o3", 3, "bo3", XN)])
    layer_norm(kit, "f2", 5, 3, 6, 7, "ln2_g", "ln2_b")
    router(kit, "r3", 3, "gate3", "gate_b3", 8, "first", rows=6, stacked=7, work=8, tmp=9)
    spread_rows(kit, "sp3", 7, range(8), [kit.slot(i) for i in range(8, 16)])
    experts_relu(kit, "e3", dram, landed, 3, list(range(8, 16)), 6, [16, 17])
    add_banks(kit, "fg", 4, 5)
    merge(kit, "m3", X, RES, 6, g=4)


def add_bias(kit, name, slot, bias):
    nc = kit.nc
    with Stage(kit, name) as st:
        block = st.block()

        @block.vector
        def _(dve):
            nc.vector.tensor_scalar(kit.slot(slot), kit.slot(slot), kit.w(bias), None, ALU.add)


def allocate(nc, ctx):
    def sb(name, shape, dt=F32):
        return ctx.enter_context(nc.sbuf_tensor(name, shape, dt))

    return Kit(nc, sb("slots", [P, SLOTS, TOK]), sb("small_sb", [P, SMALL.width]), sb("consts_sb", [P, CONSTS.width]),
               sb("experts", [P, EXPERT_COLS]), sb("sel_sb", [96, 40, P], BF16),
               ctx.enter_context(nc.psum_tensor("psum", [P, 8, CH], F32)), sb("scratch", [P, 1024]))


EXPERT_COLS = 6144


def recurrent_layers(nc, x, small, consts, sel, experts0, experts1, experts2, experts3, out):
    with ExitStack() as ctx:
        kit = allocate(nc, ctx)
        stored = ctx.enter_context(nc.semaphore("stored"))
        arrivals = Arrivals(nc, ctx)
        load_inputs(kit, arrivals, x, small, consts, sel, X, SEL_SLOT)
        layer0(kit, experts0, arrivals)
        layer1(kit, experts1, arrivals.experts[1])
        layer2(kit, experts2, arrivals.experts[2])
        layer3(kit, experts3, arrivals.experts[3])
        store_output(kit, out, X, stored)



def rows128(a, p=128):
    out = np.zeros((128, a.shape[1]), a.dtype)
    out[:a.shape[0]] = a
    return out


def block_rows(a):
    s, d, n = a.shape
    out = np.zeros((s, d, s, n), a.dtype)
    for i in range(s):
        out[i, :, i] = a[i]
    return out.reshape(s * d, s * n)


def column(v):
    return np.reshape(v, (-1, 1))


def tiles(a):
    k = a.shape[0] // 128
    return np.reshape(np.transpose(np.reshape(a, (k, 128, a.shape[1])), (1, 0, 2)), (128, -1))


def small_weights(i):
    w = {
        "W_x": i["L0_attn_W_x"], "W_dt": i["L0_attn_W_dt"], "W_out": i["L0_attn_W_out"], "A_log": i["L0_attn_A_log"],
        "b_dt": column(i["L0_attn_b_dt"]), "D": column(i["L0_attn_D"]), "b_out": column(i["L0_attn_b_out"]),
        "tokens": i["L0_ffn_expert_tokens"].T,
        "e_b1": np.reshape(i["L0_ffn_b1"], (32, 128)).T, "e_b2": np.reshape(i["L0_ffn_b2"], (32, 128)).T,
        "e_b3": i["L0_ffn_b3"].T,
        "q1": i["L1_attn_Wq"], "k1": i["L1_attn_Wk"], "v1": i["L1_attn_Wv"], "o1": i["L1_attn_Wout"],
        "gate1": i["L1_ffn_gate_w"].T,
        "q2": i["L2_attn_Wq"].T, "v2": i["L2_attn_Wv"].T, "anomaly": i["L2_attn_anomaly_matrix"],
        "bq2": column(i["L2_attn_bq"]), "bv2": np.tile(i["L2_attn_bv"], (128, 1)),
        "router": i["L2_ffn_router_w"].T, "router_bias": np.tile(i["L2_ffn_router_bias"], (128, 1)),
        "maa_x": column(i["L3_attn_time_maa_x"]),
        "maa": np.stack([i[f"L3_attn_time_maa_{s}"] for s in "wkvrg"], 1),
        "maa_w1": i["L3_attn_time_maa_w1"],
        "maa_w2": block_rows(i["L3_attn_time_maa_w2"][0:4]), "maa_w2_g": i["L3_attn_time_maa_w2"][4],
        "decay_w1": i["L3_attn_time_decay_w1"], "decay_w2": i["L3_attn_time_decay_w2"],
        "decay": column(i["L3_attn_time_decay"]), "faaaa": column(i["L3_attn_time_faaaa"]),
        "Wr": i["L3_attn_Wr"], "Wk": i["L3_attn_Wk"], "Wv": i["L3_attn_Wv"], "Wg": i["L3_attn_Wg"],
        "Wo": i["L3_attn_Wo"], "ln_w": column(i["L3_attn_ln_w"]), "ln_b": column(i["L3_attn_ln_b"]),
        "ln1_g": column(i["L3_ffn_ln1_g"]), "ln1_b": column(i["L3_ffn_ln1_b"]),
        "ln2_g": column(i["L3_ffn_ln2_g"]), "ln2_b": column(i["L3_ffn_ln2_b"]),
        "q3": i["L3_ffn_wq"], "k3": i["L3_ffn_wk"], "v3": i["L3_ffn_wv"], "o3": i["L3_ffn_wo"],
        "bq3": column(i["L3_ffn_bq"]), "bk3": column(i["L3_ffn_bk"]), "bv3": column(i["L3_ffn_bv"]),
        "bo3": column(i["L3_ffn_bo"]),
        "gate3": i["L3_ffn_gate_w"], "gate_b3": np.tile(i["L3_ffn_gate_b"], (128, 1)),
        "f_b1": np.reshape(i["L3_ffn_b1"], (32, 128)).T, "f_b2": i["L3_ffn_b2"],
    }
    return np.concatenate([rows128(w[name]) for name in SMALL.at], 1)


def constants():
    p = np.arange(128)
    head = (p[:, None] // WKV_HEAD == p[None, :] // WKV_HEAD).astype(np.float32)
    one = np.ones((128, 128), np.float32)
    c = {
        "ident": np.eye(128), "ones": one, "mean": one / 128, "head_ones": head, "head_mean": head / WKV_HEAD,
        "iota": np.tile(np.arange(16), (128, 1)), "even": column(p // WC % 2 == 0), "odd": column(p // WC % 2 == 1),
        "eps_1e5": one[:, :1] * 1e-5, "eps_scan": one[:, :1] * 1e-12, "eps_wkv": one[:, :1] * (1e-5 * 64),
        "start": np.tile(np.arange(16) == 0, (128, 1)), "zero": one[:, :1] * 0,
    }
    return np.concatenate([c[name].astype(np.float32) for name in CONSTS.at], 1)


def selectors():
    s = np.zeros((96, 40, 128), np.float32)
    for part in range(3):
        for e in range(32):
            s[32 * part + e, e, :] = 1
        for i in range(8):
            s[32 * part + 2 * i, 32 + i, :64] = 1
            s[32 * part + 2 * i + 1, 32 + i, 64:] = 1
    return np.reshape(s, (96, 40 * 128))


def expert_weights0(i):
    return np.stack([np.concatenate([i["L0_ffn_W1"][e], tiles(i["L0_ffn_W2"][e]), tiles(i["L0_ffn_W3"][e])], 1)
                     for e in range(8)])


def expert_weights1(i):
    return np.concatenate([np.concatenate([i["L1_ffn_w1"][e], i["L1_ffn_w3"][e], tiles(i["L1_ffn_w2"][e])], 1)
                           for e in range(8)], 1)


def expert_weights2(i):
    pairs = [np.concatenate([np.concatenate([i[f"L2_ffn_{n}_proj"][2 * m], i[f"L2_ffn_{n}_proj"][2 * m + 1]], 1)
                             for m in range(8)], 1) for n in ("up", "gate")]
    down = np.concatenate([np.concatenate([i["L2_ffn_down_proj"][2 * m], i["L2_ffn_down_proj"][2 * m + 1]], 0)
                           for m in range(8)], 1)
    return np.concatenate([*pairs, down, i["L2_ffn_sh_gate"].T, i["L2_ffn_sh_up"].T, i["L2_ffn_sh_down"].T], 1)


def expert_weights3(i):
    return np.stack([np.concatenate([i["L3_ffn_w1"][e], tiles(i["L3_ffn_w2"][e])], 1) for e in range(8)])


def kernel(**inputs):
    import concourse.bacc as bacc
    from concourse.bass_utils import run_bass_kernel_spmd

    i = {name: np.asarray(a) for name, a in inputs.items()}
    feeds = {
        "x_in": np.reshape(i["L0_attn_x"], (TOK, P)).T, "small_in": small_weights(i), "consts_in": constants(),
        "sel_in": selectors(), "experts0_in": expert_weights0(i), "experts1_in": expert_weights1(i),
        "experts2_in": expert_weights2(i), "experts3_in": expert_weights3(i),
    }
    feeds = {name: np.ascontiguousarray(a) for name, a in feeds.items()}
    nc = bacc.Bacc("TRN2", target_bir_lowering=False, num_devices=1)
    args = [nc.dram_tensor(name, a.shape, mybir.dt.from_np(a.dtype), kind="ExternalInput").ap() for name, a in feeds.items()]
    out = nc.dram_tensor("out_0_dram", (P, TOK), F32, kind="ExternalOutput").ap()
    recurrent_layers(nc, *args, out)
    r = run_bass_kernel_spmd(nc, [feeds], core_ids=[0])
    return np.ascontiguousarray(np.reshape(r.results[0]["out_0_dram"].T, (BATCH, SEQ, P)))
```
